# Optimizing a Trainium2 kernel written in Bass

```python
import numpy as np
import jax
import jax.numpy as jnp

def _softmax(x, axis=-1):
    return jax.nn.softmax(x, axis=axis)

def _gelu(x):
    return jax.nn.gelu(x, approximate=True)

def _silu(x):
    return jax.nn.silu(x)

def _sigmoid(x):
    return jax.nn.sigmoid(x)

def _layernorm(x, axis=-1, eps=1e-05):
    m = jnp.mean(x, axis=axis, keepdims=True)
    v = jnp.var(x, axis=axis, keepdims=True)
    return (x - m) / jnp.sqrt(v + eps)

def _scatter_add(tgt, idx, src, axis=0):
    return tgt.at[idx].add(src)

def _segment_sum(src, seg, n):
    return jax.ops.segment_sum(src, seg, n)
kernel_name = 'mk_gps_d1_gnn_r8_83e2a5'

def setup_inputs(seed: int=0):
    np.random.seed(seed)
    _w = jnp.asarray

    def _rec_inputs():
        import jax
        import jax.numpy as jnp
        _gk = jax.random.key(seed)
        x = -0.0002117 + 1 * jax.random.normal(jax.random.fold_in(_gk, 1), (12500, 256), jnp.float32)
        src = jax.random.randint(jax.random.fold_in(_gk, 2), (200000,), 0, 12500, jnp.int32)
        dst = jnp.minimum((12500 * jax.random.uniform(jax.random.fold_in(_gk, 3), (200000,)) ** 2.0).astype(jnp.int32), 99999)
        _o = jnp.argsort(dst, stable=True)
        src = src[_o]
        dst = dst[_o]
        edge_weight = jax.random.uniform(jax.random.fold_in(_gk, 12), (200000,), jnp.float32, 0.0, 0.999999)
        return (x, src, dst, edge_weight)
    x, src, dst, edge_weight = _rec_inputs()

    def _L0_gnn_setup():
        import jax, jax.numpy as jnp
        import numpy as np
        import math
        N_NODES = 12500
        N_EDGES = 200000
        D = 256
        key = jax.random.key(seed)
        k1, k2, k3, k4, k5 = jax.random.split(key, 5)
        stdv = 1.0 / math.sqrt(D)
        inp = {'input': jax.random.normal(k1, (N_NODES, D), dtype=jnp.float32), 'weight': jax.random.uniform(k2, (D, D), dtype=jnp.float32, minval=-stdv, maxval=stdv), 'vals': jax.random.uniform(k3, (N_EDGES,), dtype=jnp.float32), 'row': jax.random.randint(k4, (N_EDGES,), 0, N_NODES, dtype=jnp.int32), 'col': jax.random.randint(k5, (N_EDGES,), 0, N_NODES, dtype=jnp.int32)}
        return inp
    _L0_gnn_all = _L0_gnn_setup()
    _L0_gnn_in = {k: v for k, v in _L0_gnn_all.items() if k in ('weight',)}
    del _L0_gnn_all

    def _L0_mix_setup():
        import jax, jax.numpy as jnp
        import numpy as np
        D_MODEL = 256
        NHEAD = 8
        D_HEAD = D_MODEL // NHEAD
        DIM_FF = 1024
        B, L = (4, 2048)
        LN_EPS = 1e-05

        def _layernorm(x, g, b):
            mu = jnp.mean(x, axis=-1, keepdims=True)
            var = jnp.mean((x - mu) ** 2, axis=-1, keepdims=True)
            return (x - mu) * jax.lax.rsqrt(var + LN_EPS) * g + b

        def _phi(x):
            return jnp.where(x > 0, x + 1.0, jnp.exp(x))
        key = jax.random.key(seed)
        ks = jax.random.split(key, 16)
        s_in = 1.0 / np.sqrt(D_MODEL)
        s_ff = 1.0 / np.sqrt(DIM_FF)
        inp = {'x': jax.random.normal(ks[0], (B, L, D_MODEL), dtype=jnp.float32), 'Wq': jax.random.normal(ks[1], (D_MODEL, D_MODEL), dtype=jnp.float32) * s_in, 'bq': jnp.zeros((D_MODEL,), jnp.float32), 'Wk': jax.random.normal(ks[2], (D_MODEL, D_MODEL), dtype=jnp.float32) * s_in, 'bk': jnp.zeros((D_MODEL,), jnp.float32), 'Wv': jax.random.normal(ks[3], (D_MODEL, D_MODEL), dtype=jnp.float32) * s_in, 'bv': jnp.zeros((D_MODEL,), jnp.float32), 'Wo': jax.random.normal(ks[4], (D_MODEL, D_MODEL), dtype=jnp.float32) * s_in, 'bo': jnp.zeros((D_MODEL,), jnp.float32), 'W1': jax.random.normal(ks[5], (D_MODEL, DIM_FF), dtype=jnp.float32) * s_in, 'b1': jnp.zeros((DIM_FF,), jnp.float32), 'W2': jax.random.normal(ks[6], (DIM_FF, D_MODEL), dtype=jnp.float32) * s_ff, 'b2': jnp.zeros((D_MODEL,), jnp.float32), 'ln1_g': jnp.ones((D_MODEL,), jnp.float32), 'ln1_b': jnp.zeros((D_MODEL,), jnp.float32), 'ln2_g': jnp.ones((D_MODEL,), jnp.float32), 'ln2_b': jnp.zeros((D_MODEL,), jnp.float32)}
        return inp
    _L0_mix_all = _L0_mix_setup()
    _L0_mix_in = {k: v for k, v in _L0_mix_all.items() if k in ('Wq', 'bq', 'Wk', 'bk', 'Wv', 'bv', 'Wo', 'bo', 'W1', 'b1', 'W2', 'b2', 'ln1_g', 'ln1_b', 'ln2_g', 'ln2_b')}
    del _L0_mix_all

    def _L0_ffn_setup():
        import jax, jax.numpy as jnp
        import numpy as np
        B, A = (512, 8)
        IN, OUT = (256, 256)
        SH1, SH2 = (256, 128)
        EH1, EH2 = (128, 64)
        E, TOPK = (4, 2)

        def _shared_mlp(x, W1, b1, W2, b2, W3, b3):
            h = jax.nn.relu(x @ W1 + b1)
            h = jax.nn.relu(h @ W2 + b2)
            return h @ W3 + b3

        def _experts_mlp(x, eW1, eb1, eW2, eb2, eW3, eb3):
            h = jax.nn.relu(jnp.einsum('baf,efh->ebah', x, eW1) + eb1[:, None, None, :])
            h = jax.nn.relu(jnp.einsum('ebah,ehg->ebag', h, eW2) + eb2[:, None, None, :])
            o = jnp.einsum('ebag,ego->ebao', h, eW3) + eb3[:, None, None, :]
            return jnp.moveaxis(o, 0, -1)
        key = jax.random.key(seed)
        ks = jax.random.split(key, 16)
        s = 0.05
        return {'x': jax.random.normal(ks[0], (B, A, IN), jnp.float32), 'sW1': jax.random.normal(ks[1], (IN, SH1), jnp.float32) * s, 'sb1': jnp.zeros((SH1,), jnp.float32), 'sW2': jax.random.normal(ks[2], (SH1, SH2), jnp.float32) * s, 'sb2': jnp.zeros((SH2,), jnp.float32), 'sW3': jax.random.normal(ks[3], (SH2, OUT), jnp.float32) * s, 'sb3': jnp.zeros((OUT,), jnp.float32), 'eW1': jax.random.normal(ks[4], (E, IN, EH1), jnp.float32) * s, 'eb1': jnp.zeros((E, EH1), jnp.float32), 'eW2': jax.random.normal(ks[5], (E, EH1, EH2), jnp.float32) * s, 'eb2': jnp.zeros((E, EH2), jnp.float32), 'eW3': jax.random.normal(ks[6], (E, EH2, OUT), jnp.float32) * s, 'eb3': jnp.zeros((E, OUT), jnp.float32), 'gW': jax.random.normal(ks[7], (IN, E), jnp.float32) * s, 'gb': jnp.zeros((E,), jnp.float32)}
    _L0_ffn_all = _L0_ffn_setup()
    _L0_ffn_in = {k: v for k, v in _L0_ffn_all.items() if k in ('sW1', 'sb1', 'sW2', 'sb2', 'sW3', 'sb3', 'eW1', 'eb1', 'eW2', 'eb2', 'eW3', 'eb3', 'gW', 'gb')}
    del _L0_ffn_all
    return {'x': x, 'src': src, 'dst': dst, 'edge_weight': edge_weight, 'L0_gnn_weight': _L0_gnn_in['weight'], 'L0_mix_Wq': _L0_mix_in['Wq'], 'L0_mix_bq': _L0_mix_in['bq'], 'L0_mix_Wk': _L0_mix_in['Wk'], 'L0_mix_bk': _L0_mix_in['bk'], 'L0_mix_Wv': _L0_mix_in['Wv'], 'L0_mix_bv': _L0_mix_in['bv'], 'L0_mix_Wo': _L0_mix_in['Wo'], 'L0_mix_bo': _L0_mix_in['bo'], 'L0_mix_W1': _L0_mix_in['W1'], 'L0_mix_b1': _L0_mix_in['b1'], 'L0_mix_W2': _L0_mix_in['W2'], 'L0_mix_b2': _L0_mix_in['b2'], 'L0_mix_ln1_g': _L0_mix_in['ln1_g'], 'L0_mix_ln1_b': _L0_mix_in['ln1_b'], 'L0_mix_ln2_g': _L0_mix_in['ln2_g'], 'L0_mix_ln2_b': _L0_mix_in['ln2_b'], 'L0_ffn_sW1': _L0_ffn_in['sW1'], 'L0_ffn_sb1': _L0_ffn_in['sb1'], 'L0_ffn_sW2': _L0_ffn_in['sW2'], 'L0_ffn_sb2': _L0_ffn_in['sb2'], 'L0_ffn_sW3': _L0_ffn_in['sW3'], 'L0_ffn_sb3': _L0_ffn_in['sb3'], 'L0_ffn_eW1': _L0_ffn_in['eW1'], 'L0_ffn_eb1': _L0_ffn_in['eb1'], 'L0_ffn_eW2': _L0_ffn_in['eW2'], 'L0_ffn_eb2': _L0_ffn_in['eb2'], 'L0_ffn_eW3': _L0_ffn_in['eW3'], 'L0_ffn_eb3': _L0_ffn_in['eb3'], 'L0_ffn_gW': _L0_ffn_in['gW'], 'L0_ffn_gb': _L0_ffn_in['gb']}

def reference(x, src, dst, edge_weight, L0_gnn_weight, L0_mix_Wq, L0_mix_bq, L0_mix_Wk, L0_mix_bk, L0_mix_Wv, L0_mix_bv, L0_mix_Wo, L0_mix_bo, L0_mix_W1, L0_mix_b1, L0_mix_W2, L0_mix_b2, L0_mix_ln1_g, L0_mix_ln1_b, L0_mix_ln2_g, L0_mix_ln2_b, L0_ffn_sW1, L0_ffn_sb1, L0_ffn_sW2, L0_ffn_sb2, L0_ffn_sW3, L0_ffn_sb3, L0_ffn_eW1, L0_ffn_eb1, L0_ffn_eW2, L0_ffn_eb2, L0_ffn_eW3, L0_ffn_eb3, L0_ffn_gW, L0_ffn_gb):
    import jax
    import jax.numpy as jnp

    def _L0_gnn_ref(input, weight, vals, row, col):
        import jax, jax.numpy as jnp
        import numpy as np
        import math
        N_NODES = 12500
        N_EDGES = 200000
        D = 256
        support = jnp.matmul(input, weight)
        gathered = support[col] * vals[:, None]
        output = jax.ops.segment_sum(gathered, row, num_segments=N_NODES)
        return output

    def _L0_mix_ref(x, Wq, bq, Wk, bk, Wv, bv, Wo, bo, W1, b1, W2, b2, ln1_g, ln1_b, ln2_g, ln2_b):
        import jax, jax.numpy as jnp
        import numpy as np
        D_MODEL = 256
        NHEAD = 8
        D_HEAD = D_MODEL // NHEAD
        DIM_FF = 1024
        B, L = (4, 2048)
        LN_EPS = 1e-05

        def _layernorm(x, g, b):
            mu = jnp.mean(x, axis=-1, keepdims=True)
            var = jnp.mean((x - mu) ** 2, axis=-1, keepdims=True)
            return (x - mu) * jax.lax.rsqrt(var + LN_EPS) * g + b

        def _phi(x):
            return jnp.where(x > 0, x + 1.0, jnp.exp(x))
        Bq, Lq, _ = x.shape
        q = (x @ Wq + bq).reshape(Bq, Lq, NHEAD, D_HEAD)
        k = (x @ Wk + bk).reshape(Bq, Lq, NHEAD, D_HEAD)
        v = (x @ Wv + bv).reshape(Bq, Lq, NHEAD, D_HEAD)
        q_phi = _phi(q)
        k_phi = _phi(k)
        kv = jnp.einsum('blhd,blhe->bhde', k_phi, v)
        k_sum = k_phi.sum(axis=1)
        z = 1.0 / (jnp.einsum('blhd,bhd->blh', q_phi, k_sum) + 1e-06)
        out = jnp.einsum('blhd,bhde,blh->blhe', q_phi, kv, z)
        out = out.reshape(Bq, Lq, D_MODEL) @ Wo + bo
        x = _layernorm(x + out, ln1_g, ln1_b)
        ff = jax.nn.relu(x @ W1 + b1) @ W2 + b2
        x = _layernorm(x + ff, ln2_g, ln2_b)
        return x

    def _L0_ffn_ref(x, sW1, sb1, sW2, sb2, sW3, sb3, eW1, eb1, eW2, eb2, eW3, eb3, gW, gb):
        import jax, jax.numpy as jnp
        import numpy as np
        B, A = (512, 8)
        IN, OUT = (256, 256)
        SH1, SH2 = (256, 128)
        EH1, EH2 = (128, 64)
        E, TOPK = (4, 2)

        def _shared_mlp(x, W1, b1, W2, b2, W3, b3):
            h = jax.nn.relu(x @ W1 + b1)
            h = jax.nn.relu(h @ W2 + b2)
            return h @ W3 + b3

        def _experts_mlp(x, eW1, eb1, eW2, eb2, eW3, eb3):
            h = jax.nn.relu(jnp.einsum('baf,efh->ebah', x, eW1) + eb1[:, None, None, :])
            h = jax.nn.relu(jnp.einsum('ebah,ehg->ebag', h, eW2) + eb2[:, None, None, :])
            o = jnp.einsum('ebag,ego->ebao', h, eW3) + eb3[:, None, None, :]
            return jnp.moveaxis(o, 0, -1)
        all_out = _experts_mlp(x, eW1, eb1, eW2, eb2, eW3, eb3)
        shared = _shared_mlp(x, sW1, sb1, sW2, sb2, sW3, sb3)
        gates = jax.nn.softmax(x @ gW + gb, axis=-1)
        topv, topi = jax.lax.top_k(gates, TOPK)
        topw = jax.nn.softmax(topv, axis=-1)
        sel = jnp.take_along_axis(all_out, topi[:, :, None, :], axis=-1)
        gated = jnp.sum(sel * topw[:, :, None, :], axis=-1)
        return shared + gated
    xn = _layernorm(x, axis=-1)
    x = x + _L0_gnn_ref(xn, L0_gnn_weight, edge_weight, src, dst) + _L0_mix_ref(xn[None], L0_mix_Wq, L0_mix_bq, L0_mix_Wk, L0_mix_bk, L0_mix_Wv, L0_mix_bv, L0_mix_Wo, L0_mix_bo, L0_mix_W1, L0_mix_b1, L0_mix_W2, L0_mix_b2, L0_mix_ln1_g, L0_mix_ln1_b, L0_mix_ln2_g, L0_mix_ln2_b)[0]
    x = x + _L0_ffn_ref(_layernorm(x, axis=-1)[None], L0_ffn_sW1, L0_ffn_sb1, L0_ffn_sW2, L0_ffn_sb2, L0_ffn_sW3, L0_ffn_sb3, L0_ffn_eW1, L0_ffn_eb1, L0_ffn_eW2, L0_ffn_eb2, L0_ffn_eW3, L0_ffn_eb3, L0_ffn_gW, L0_ffn_gb)[0]
    return x

_drawn_inputs = setup_inputs


def setup_inputs(seed=0):
    import zlib

    import numpy as np

    out = dict(_drawn_inputs(seed))
    spreads = {'L0_mix_bq': (0.0, 2.0),
     'L0_mix_bk': (0.0, 2.0),
     'L0_mix_bv': (0.0, 0.1),
     'L0_mix_bo': (0.0, 0.1),
     'L0_mix_b1': (0.0, 0.312),
     'L0_mix_b2': (0.0, 0.1),
     'L0_mix_ln1_g': (1.0, 0.2),
     'L0_mix_ln1_b': (0.0, 0.1),
     'L0_mix_ln2_g': (1.0, 0.2),
     'L0_mix_ln2_b': (0.0, 0.1),
     'L0_ffn_sb1': (0.0, 0.8),
     'L0_ffn_sb2': (0.0, 0.441),
     'L0_ffn_sb3': (0.0, 0.1),
     'L0_ffn_eb1': (0.0, 2.0),
     'L0_ffn_eb2': (0.0, 0.8),
     'L0_ffn_eb3': (0.0, 0.282),
     'L0_ffn_gb': (0.0, 0.8)}
    factors = {'L0_mix_Wq': 8.0, 'L0_mix_Wk': 8.0, 'L0_mix_Wv': 8.0, 'L0_ffn_eW1': 3.062}
    for name, (base, spread) in spreads.items():
        noise = np.random.default_rng([zlib.crc32(name.encode()), seed]).standard_normal(out[name].shape)
        drawn = base * np.exp(spread * noise) if base else spread * noise
        out[name] = jnp.asarray(drawn.astype(out[name].dtype))
    for name, factor in factors.items():
        out[name] = (out[name] * factor).astype(out[name].dtype)
    return out
```

```python
from contextlib import ExitStack

import concourse.bass as bass
from concourse import mybir

ALU = mybir.AluOpType
ACT = mybir.ActivationFunctionType
AX = mybir.AxisListType
F32, BF16, I32 = mybir.dt.float32, mybir.dt.bfloat16, mybir.dt.int32

N, D, E = 12500, 256, 200000
T = 125
NT = N // T
P = 128
H2 = D // P
HEADS, DH = 8, 32
HPH = P // DH
RW = 3
FF = 1024
FC = FF // P
NE, EH2 = 4, 64
COLS = E // T
STREAMS = 4
SC = COLS // STREAMS
BODY = 4
TURNS = NT // BODY
RANKS = SC // (2 * TURNS)
HALF = RANKS // 2
BATCH = HALF * STREAMS
CH = 16
GROUPS = -(-((E + NT * (P - 1)) // P) // (2 * CH)) * 2
CHUNKS = GROUPS * CH
CPP = 16
CPART = CHUNKS // CPP
GROUP = CH * P
SLOTS = (GROUPS + 2) * GROUP
assert RANKS * 2 * TURNS == SC and SC * STREAMS == COLS and COLS * T == E and CPP * CPART == CHUNKS and CPART <= T
ZEROS = GROUP * RW // 2
LN_EPS = 1e-5
A_STEPS, B_STEPS, B_FRONT, E_STEPS, E_FRONT = 68, 80, 10, 46, 20
KVW = P + HPH


class Steps:

    def __init__(self, engine, sem, base=0):
        self.engine, self.sem, self.base, self.n = engine, sem, base, 0

    def then(self, instruction):
        self.n += 1
        instruction.then_inc(self.sem, 1)
        self.engine.wait_ge(self.sem, self.base + self.n)


def build(nc, x, src, dst, edge_weight, Wg, Wq, bq, Wk, bk, Wv, bv, Wo, bo, W1, b1, W2, b2, g1, be1, g2, be2,
          sW1, sb1, sW2, sb2, sW3, sb3, eW1, eb1, eW2, eb2, eW3, eb3, gW, gb, out):
    ctx = ExitStack()
    with ctx:
        def sb(name, shape, dt=F32):
            return ctx.enter_context(nc.sbuf_tensor(name, shape, dt))

        def sem(name):
            return ctx.enter_context(nc.semaphore(name))

        def sems(name, n):
            return [sem(f"{name}{i}") for i in range(n)]

        banks = [ctx.enter_context(nc.psum_tensor(f"bank{i}", [P, 512], F32)) for i in range(8)]

        support_d = nc.dram_tensor("support_rows", [N, D], F32, kind="Internal").ap()
        xn_d = nc.dram_tensor("xn_rows", [N, D], F32, kind="Internal").ap()
        q_d = nc.dram_tensor("q_phi", [NT, P, H2 * T], F32, kind="Internal").ap()
        table_d = nc.dram_tensor("edge_table", [SLOTS, RW], F32, kind="Internal").ap()
        binof_d = nc.dram_tensor("chunk_offsets", [CHUNKS], I32, kind="Internal").ap()

        wg = sb("wg", [P, H2, D])
        wq, wk, wv, wo = (sb(n, [P, H2, D]) for n in ("wq", "wk", "wv", "wo"))
        w1 = sb("w1", [P, H2, FF])
        w2 = sb("w2", [P, FC, D])
        sw1 = sb("sw1", [P, H2, D])
        sw2 = sb("sw2", [P, H2, P])
        sw3 = sb("sw3", [P, D])
        ew1 = sb("ew1", [P, H2, NE, P])
        ew2 = sb("ew2", [P, NE, EH2])
        ew3 = sb("ew3", [EH2 + 1, NE, D])
        gw = sb("gw", [P, H2, NE])
        bqc, b1c = sb("bqc", [P, H2]), sb("b1c", [P, FC])
        sb1c, sb2c = sb("sb1c", [P, H2]), sb("sb2c", [P, 1])
        eb1c, eb2c = sb("eb1c", [P, NE]), sb("eb2c", [EH2, NE])
        rows = {n: sb(n, [T, D]) for n in ("bkr", "bvr", "bor", "g1r", "be1r", "b2r", "g2r", "be2r", "sb3r")}
        gbr = sb("gbr", [T, NE])
        ident = sb("ident", [P, P])
        iota_n = sb("iota_n", [P, T])
        ones_b = sb("ones_b", [T, P], BF16)
        before = sb("before", [T, T], BF16)
        upto = sb("upto", [T, T], BF16)
        iota_b = sb("iota_b", [T, NT], BF16)
        tiebreak = sb("tiebreak", [T, NE, NE])
        kvb = sb("kvb", [P, H2, KVW])
        base = sb("base", [T, STREAMS, NT])
        ones_f = sb("ones_f", [1, P])
        zero_b = sb("zero_b", [T, P], BF16)
        eps = sb("eps", [T, 2])
        acc = sb("acc", [T, NT, D])

        PAIRS = CH // 2
        AHEAD = 4

        WORK = 54 * 1024 // 4
        work = sb("work", [P, WORK])
        acc_flat = acc[:, :, :].rearrange("p a b -> p (a b)")
        top = [0]

        def carve(shape, dt=F32, memory=work):
            words = 1
            for s in shape[1:]:
                words *= s
            words = words if dt != BF16 else -(-words // 2)
            a = memory[0:shape[0], top[0]:top[0] + words]
            top[0] += words
            assert top[0] <= memory.shape[1], top[0]
            if dt != F32:
                a = a.bitcast(dt)
            if len(shape) > 2:
                names = "abcd"[:len(shape) - 1]
                a = a.rearrange(f"p ({' '.join(names)}) -> p {' '.join(names)}",
                                **{k: s for k, s in zip(names, shape[1:])})
            return a

        src_i, dst_i = (carve([T, COLS], I32, acc_flat) for _ in range(2))
        wgt, grp, srcf = (carve([T, COLS], F32, acc_flat) for _ in range(3))
        iota_i = carve([T, P], I32, acc_flat)
        zeros = carve([GROUPS + 2, ZEROS], F32, acc_flat)
        hist = carve([T, STREAMS, NT], F32, acc_flat)
        total, chunks_f, nothing, first, cum, ended = (carve([T, NT], F32, acc_flat) for _ in range(6))
        chunks_i = carve([T, NT], I32, acc_flat)
        chunk_i, bin_i = (carve([CPART, CPP], I32, acc_flat) for _ in range(2))
        chunk_f, bin_f = (carve([CPART, CPP], F32, acc_flat) for _ in range(2))
        top[0] = 0
        rec = carve([T, COLS, RW])
        grp_b = carve([T, COLS], BF16)
        hot = [carve([T, STREAMS, NT], BF16) for _ in range(2)]
        prod = carve([T, STREAMS, NT])
        slot_f = carve([T, BATCH])
        slot_i, slot_t = carve([T, BATCH], I32), carve([T, BATCH], I32)
        addr = [carve([T, BATCH], I32) for _ in range(2)]
        ring = [carve([T, BATCH, RW]) for _ in range(2)]
        ln, ln2 = carve([T, 16]), carve([T, 16])
        spread_top = top[0]
        qT = [carve([P, H2 * T]) for _ in range(2)]
        xr = [carve([T, D]) for _ in range(2)]
        xo = [carve([T, D]) for _ in range(2)]
        zr = carve([T, H2, HPH])
        at = carve([T, D])
        atT, x1T = carve([P, H2 * T]), carve([P, H2 * T])
        r1 = carve([T, D])
        x1 = [carve([T, D]) for _ in range(2)]
        r2 = carve([T, D])
        hT = carve([P, FC, T])
        top[0] = spread_top
        xnT, qb, qe = (carve([P, H2 * T]) for _ in range(3))
        qphi = [carve([P, H2 * T]) for _ in range(2)]
        top[0] = 0
        xt, xn, sup = ([carve([T, D], F32, acc_flat) for _ in range(2)] for _ in range(3))
        kb, ke, kphi = (carve([T, D], F32, acc_flat) for _ in range(3))
        vt = carve([T, H2, P + 1], F32, acc_flat)
        top[0] = 0
        rowbuf = [[carve([P, D]) for _ in range(CH)] for _ in range(2)]
        onehot = [carve([P, 2, T]) for _ in range(AHEAD)]
        recs = [carve([P, CH, RW]) for _ in range(2)]
        gidx = [carve([P, CH], I32) for _ in range(2)]
        binof = carve([1, CHUNKS], I32)
        top[0] = 0
        yn, res = ([carve([T, D]) for _ in range(2)] for _ in range(2))
        yT = carve([P, H2 * T])
        s1T, e1T = carve([P, H2, T]), carve([P, NE, T])
        s2T, e2T = carve([P, T]), carve([EH2 + 1, NE, T])
        lne = carve([T, 16])
        logit, soft, chosen, rank4 = (carve([T, NE]) for _ in range(4))
        beats, ties = carve([T, NE, NE]), carve([T, NE, NE])
        gstat = carve([T, 4])
        gwt = [carve([T, NE]) for _ in range(2)]


        gate = sem("gate")
        loads, made, pool_step, edges_in = sem("loads"), sem("made"), sem("pool_step"), sem("edges_in")
        dve_step, hist_hot, hist_mm = sem("dve_step"), sem("hist_hot"), sem("hist_mm")
        base_made, bins_out, bins_in = sem("base_made"), sem("bins_out"), sem("bins_in")
        hot_made, rank_ps, rank_read, rank_next = sem("hot_made"), sem("rank_ps"), sem("rank_read"), sem("rank_next")
        rank_step, addr_made, ring_made, pool_go = sem("rank_step"), sem("addr_made"), sem("ring_made"), sem("pool_go")
        scattered = sems("scattered", 2)
        x_in = sems("x_in", BODY)
        x_used, a_step, xn_made, xT_ps, xnT_made = (sem(n) for n in ("x_used", "a_step", "xn_made", "xT_ps", "xnT_made"))
        sup_ps, kv_ps, q_ps, sup_read, kv_read, qb_made = (sem(n) for n in (
            "sup_ps", "kv_ps", "q_ps", "sup_read", "kv_read", "qb_made"))
        km_made, ke_made, qm_made, qe_made, kphi_made, qphi_made, kv_added = (sem(n) for n in (
            "km_made", "ke_made", "qm_made", "qe_made", "kphi_made", "qphi_made", "kv_added"))
        stored = sems("stored", BODY)
        mix_in = sems("mix_in", BODY)
        sums_open, kvb_made, mix_used, b_step = sem("sums_open"), sem("kvb_made"), sem("mix_used"), sem("b_step")
        at_ps, at_made, atT_ps, atT_made, wo_ps, r1_made, x1_made, x1T_ps, x1T_made, h_ps, h_made, ff_ps, ff_read = (
            sem(n) for n in ("at_ps", "at_made", "atT_ps", "atT_made", "wo_ps", "r1_made", "x1_made", "x1T_ps",
                             "x1T_made", "h_ps", "h_made", "ff_ps", "ff_read"))
        var1_made, std1_made, var2_made, std2_made = (sem(n) for n in ("var1_made", "std1_made", "var2_made", "std2_made"))
        recs_in, landed = sems("recs_in", 2), sems("landed", 8)
        recs_used, gidx_made, onehot_made, pair_ps, acc_step = (sem(n) for n in (
            "recs_used", "gidx_made", "onehot_made", "pair_ps", "acc_step"))
        e_step, yn_made, yT_ps, yT_made, l1_ps, l1_made, l2_ps, l2_made, l3_ps, l3_read, gate_read, res_made = (
            sem(n) for n in ("e_step", "yn_made", "yT_ps", "yT_made", "l1_ps", "l1_made", "l2_ps", "l2_made",
                             "l3_ps", "l3_read", "gate_read", "res_made"))
        var_made, rstd_made = sem("var_made"), sem("rstd_made")
        gexp_go, gexp_made = sem("gexp_go"), sem("gexp_made")
        out_stored = sems("out_stored", 2)

        def moments(steps, dve, source, stats):
            steps.then(dve.bn_stats(stats[:, 0:6], source))
            dve.sem_inc(gate, 1)
            steps.then(dve.bn_aggr(stats[:, 6:8], stats[:, 0:6]))

        def rsqrt_newton(steps, dve, stats):
            value, y, t = stats[:, 9:10], stats[:, 8:9], stats[:, 10:11]
            steps.then(dve.tensor_scalar(value, stats[:, 7:8], LN_EPS, None, ALU.add))
            steps.then(dve.tensor_scalar(t.bitcast(I32), value.bitcast(I32), 1, None, ALU.logical_shift_right))
            steps.then(dve.tensor_scalar(y.bitcast(I32), t.bitcast(I32), -1.0, float(0x5F3759DF), ALU.mult, ALU.add))
            for _ in range(3):
                steps.then(dve.scalar_tensor_tensor(t, y, value, y, ALU.mult, ALU.mult))
                steps.then(dve.tensor_scalar(t, t, -0.5, 1.5, ALU.mult, ALU.add))
                steps.then(dve.tensor_tensor(y, y, t, ALU.mult))

        columns = [(bqc[:, :], bq.rearrange("(h p) -> p h", p=P)), (b1c[:, :], b1.rearrange("(h p) -> p h", p=P)),
                   (sb1c[:, :], sb1.rearrange("(h p) -> p h", p=P)), (sb2c[:, :], sb2.rearrange("(h p) -> p h", p=P)),
                   (eb1c[:, :], eb1.rearrange("e p -> p e")), (eb2c[:, :], eb2.rearrange("e p -> p e"))]
        blocks = [(w[:, :, :], d.rearrange("(h p) n -> p h n", p=P)) for w, d in
                  ((wg, Wg), (wq, Wq), (wk, Wk), (wv, Wv), (wo, Wo), (w1, W1), (w2, W2), (sw1, sW1), (sw2, sW2), (gw, gW))]
        blocks += [(sw3[:, :], sW3), (ew2[:, :, :], eW2.rearrange("e p n -> p e n")),
                   (ew3[0:EH2, :, :], eW3.rearrange("e p n -> p e n")),
                   (ew3[EH2:EH2 + 1, :, :], eb3.rearrange("(a e) n -> a e n", a=1))]
        blocks += [(ew1[:, :, e, :], eW1[e].rearrange("(h p) n -> p h n", p=P)) for e in range(NE)]
        broadcasts = [(rows[n][:, :], d.partition_broadcast(T)) for n, d in
                      (("bkr", bk), ("bvr", bv), ("bor", bo), ("g1r", g1), ("be1r", be1), ("b2r", b2), ("g2r", g2),
                       ("be2r", be2), ("sb3r", sb3))] + [(gbr[:, :], gb.partition_broadcast(T))]
        n_loads = len(columns) + len(blocks) + len(broadcasts)

        with nc.Block() as block:
            @block.sync
            def _(sp):
                for a, d in ((src_i, src), (dst_i, dst), (wgt, edge_weight)):
                    sp.dma_start(a, d.rearrange("(p c) -> p c", p=T)).then_inc(edges_in, 16)
                for a, d in blocks + broadcasts:
                    sp.dma_start(a, d).then_inc(loads, 16)
                with nc.allow_non_contiguous_dma(reason="bias columns, once"):
                    for a, d in columns:
                        sp.dma_start(a, d).then_inc(loads, 16)
                for s, n in ((rank_next, 2), (x_used, 2), (sup_read, 1), (kv_read, 1), (kv_added, 1),
                             (stored[2], 48), (stored[3], 48), (mix_used, 2), (ff_read, 1),
                             (pair_ps, 2 * PAIRS), (acc_step, 2 * AHEAD), (l3_read, 1), (gate_read, 1),
                             (out_stored[0], 16), (out_stored[1], 16)):
                    sp.sem_inc(s, n)
                sp.wait_ge(loads, 16 * n_loads)
                sp.wait_ge(base_made, 1)
                sp.dma_start(binof_d.rearrange("(p c) -> p c", p=CPART), bin_i).then_inc(bins_out, 16)
                sp.wait_ge(bins_out, 16)

            @block.gpsimd
            def _(pool):
                pool.iota(iota_i, pattern=[[1, P]], base=0, channel_multiplier=0).then_inc(made, 1)
                pool.iota(chunk_i, pattern=[[1, CPP]], base=0, channel_multiplier=CPP).then_inc(made, 1)
                pool.iota(iota_n[:, :], pattern=[[1, T]], base=0, channel_multiplier=0,
                          allow_small_or_imprecise_dtypes=True).then_inc(pool_step, 1)
                pool.memset(zeros, 0.0).then_inc(made, 1)
                pool.memset(kvb[:, :, :], 0.0).then_inc(made, 1)
                pool.memset(ident[:, :], 0.0).then_inc(pool_step, 1)
                pool.memset(ones_b[:, :], 1.0).then_inc(pool_step, 1)
                pool.memset(ones_f[:, :], 1.0).then_inc(pool_step, 1)
                pool.memset(zero_b[:, :], 0.0).then_inc(pool_step, 1)
                pool.memset(tiebreak[:, :, :], 1.0).then_inc(pool_step, 1)
                pool.memset(eps[:, 0:1], LN_EPS).then_inc(pool_step, 1)
                pool.memset(eps[:, 1:2], -0.5).then_inc(pool_step, 1)
                pool.wait_ge(pool_step, 8)
                pool.affine_select(out=ident[:, :], in_=ident[:, :], compare_op=ALU.not_equal, fill=1.0, base=0,
                                   pattern=[[-1, P]], channel_multiplier=1).then_inc(pool_step, 1)
                pool.affine_select(out=before[:, :], in_=ones_b[:, 0:T], compare_op=ALU.is_gt, fill=0.0, base=0,
                                   pattern=[[1, T]], channel_multiplier=-1).then_inc(pool_step, 1)
                pool.affine_select(out=upto[:, :], in_=ones_b[:, 0:T], compare_op=ALU.is_ge, fill=0.0, base=0,
                                   pattern=[[-1, T]], channel_multiplier=1).then_inc(pool_step, 1)
                pool.affine_select(out=tiebreak[:, :, :], in_=tiebreak[:, :, :], compare_op=ALU.is_gt, fill=0.0,
                                   base=0, pattern=[[1, NE], [-1, NE]], channel_multiplier=0).then_inc(pool_step, 1)
                pool.wait_ge(made, 4)
                table_rows = table_d.rearrange("(p c) w -> p (c w)", p=GROUPS + 2)
                for k in range(2):
                    pool.dma_start(table_rows[:, k * ZEROS:(k + 1) * ZEROS], zeros).then_inc(scattered[k], 16)
                pool.wait_ge(pool_step, 12)
                for k in range(2):
                    pool.wait_ge(scattered[k], 16)

            MAGIC = 12582912.0

            @block.vector
            def _(dve):
                s = Steps(dve, dve_step)
                dve.wait_ge(edges_in, 48)
                dve.wait_ge(made, 2)
                s.then(dve.tensor_copy(srcf, src_i))
                s.then(dve.tensor_scalar(grp, srcf, -float(T // 2), 1.0 / T, ALU.add, ALU.mult))
                s.then(dve.tensor_scalar(grp, grp, MAGIC, None, ALU.add))
                s.then(dve.tensor_scalar(grp, grp, -MAGIC, None, ALU.add))
                s.then(dve.tensor_copy(grp_b, grp))
                s.then(dve.tensor_copy(iota_b[:, :], iota_i[:, 0:NT]))
                groups = grp_b.rearrange("p (k r) -> p k r", k=STREAMS)
                numbers = iota_b[:, :].unsqueeze(1).to_broadcast([T, STREAMS, NT])
                with dve.Fori(0, SC // 2) as i:
                    for h in range(2):
                        dve.wait_ge(hist_mm, 2 * i + h + 1)
                        dve.tensor_tensor(hot[h], groups[:, :, bass.ds(2 * i + h, 1)].to_broadcast([T, STREAMS, NT]),
                                          numbers, ALU.is_equal).then_inc(hist_hot, 1)
                dve.wait_ge(hist_mm, SC + 2)
                counts = banks[7][0:T, 0:STREAMS * NT].rearrange("p (k b) -> p k b", k=STREAMS)
                s.then(dve.tensor_copy(hist, counts))
                s.then(dve.tensor_reduce(total, hist.rearrange("p k b -> p b k"), AX.X, ALU.add))
                s.then(dve.tensor_scalar(chunks_i, total, float(P - 1), None, ALU.add))
                s.then(dve.tensor_scalar(chunks_i, chunks_i, 7, None, ALU.logical_shift_right))
                s.then(dve.tensor_copy(chunks_f, chunks_i))
                s.then(dve.memset(nothing, 0.0))
                s.then(dve.tensor_tensor_scan(cum, chunks_f, nothing, 0.0, ALU.add, ALU.add))
                s.then(dve.tensor_tensor(first, cum, chunks_f, ALU.subtract))
                s.then(dve.tensor_scalar(base[:, 0, :], first, float(P), None, ALU.mult))
                for k in range(1, STREAMS):
                    s.then(dve.tensor_tensor(base[:, k, :], base[:, k - 1, :], hist[:, k - 1, :], ALU.add))
                s.then(dve.tensor_copy(chunk_f, chunk_i))
                for q in range(CPP):
                    s.then(dve.tensor_scalar(ended[0:CPART], cum[0:CPART], chunk_f[:, q:q + 1], None, ALU.is_le))
                    s.then(dve.tensor_reduce(bin_f[:, q:q + 1], ended[0:CPART], AX.X, ALU.add))
                s.then(dve.tensor_scalar(bin_f, bin_f, float(NT - 1), float(D), ALU.min, ALU.mult))
                dve.tensor_copy(bin_i, bin_f).then_inc(base_made, 1)
                s.then(dve.tensor_scalar(grp, grp, -float(T), None, ALU.mult))
                s.then(dve.tensor_tensor(rec[:, :, 1], srcf, grp, ALU.add))
                s.then(dve.tensor_copy(rec[:, :, 0], dst_i))
                s.then(dve.tensor_copy(rec[:, :, 2], wgt))

            @block.tensor
            def _(pe):
                counts = banks[7][:, 0:STREAMS * NT]
                pe.sem_inc(hist_mm, 2)
                pe.wait_ge(pool_step, 12)
                pe.wait_ge(hist_hot, 1)
                pe.matmul(counts, zero_b[:, :], hot[0].rearrange("p k b -> p (k b)"), start=True, stop=False,
                          skip_group_check=True)
                with pe.Fori(0, SC // 2) as i:
                    for h in range(2):
                        pe.wait_ge(hist_hot, 2 * i + h + 1)
                        pe.matmul(counts, ones_b[:, :], hot[h].rearrange("p k b -> p (k b)"), start=False, stop=False,
                                  skip_group_check=True).then_inc(hist_mm, 1)

        ranks = banks[0][0:T, 0:STREAMS * NT]
        groups = grp_b.rearrange("p (k r) -> p k r", k=STREAMS)
        records = rec.rearrange("p (k r) w -> p k r w", k=STREAMS)

        def rank_hot(dve, r, h):
            dve.wait_ge(rank_next, r + 1)
            dve.tensor_tensor(hot[h], groups[:, :, bass.ds(r, 1)].to_broadcast([T, STREAMS, NT]),
                              iota_b[:, :].unsqueeze(1).to_broadcast([T, STREAMS, NT]), ALU.is_equal).then_inc(hot_made, 1)

        def rank_sum(dve, r, u):
            dve.wait_ge(rank_ps, r + 1)
            dve.tensor_tensor(prod, ranks.rearrange("p (k b) -> p k b", k=STREAMS), hot[u % 2],
                              ALU.mult).then_inc(rank_read, 1)
            dve.wait_ge(rank_read, r + 1)
            dve.tensor_reduce(slot_f[:, u * STREAMS:(u + 1) * STREAMS], prod, AX.X, ALU.add).then_inc(rank_step, 1)

        def rank_before(pe, r, h):
            pe.wait_ge(hot_made, r + 1)
            pe.matmul(ranks, before[:, :], hot[h].rearrange("p k b -> p (k b)"), start=False, stop=False,
                      skip_group_check=True).then_inc(rank_ps, 1)

        def rank_advance(pe, r, h):
            pe.wait_ge(rank_read, r + 1)
            pe.matmul(ranks, upto[:, :], hot[h].rearrange("p k b -> p (k b)"), start=False, stop=False,
                      skip_group_check=True).then_inc(rank_next, 1)

        def addresses(dve, turn, b, s):
            dve.wait_ge(rank_step, RANKS * turn + HALF * (b + 1))
            s.then(dve.tensor_copy(slot_i, slot_f))
            s.then(dve.tensor_scalar(slot_t, slot_i, P - 1, 4, ALU.bitwise_and, ALU.logical_shift_left))
            s.then(dve.scalar_tensor_tensor(slot_t, slot_i, -GROUP, slot_t, ALU.bitwise_and, ALU.bitwise_or))
            s.then(dve.tensor_scalar(slot_i, slot_i, 7, CH - 1, ALU.logical_shift_right, ALU.bitwise_and))
            dve.wait_ge(scattered[b], 16 * BATCH * turn + 16)
            dve.tensor_tensor(addr[b], slot_i, slot_t, ALU.bitwise_or).then_inc(addr_made, 1)

        def ring_records(act, turn, b):
            act.wait_ge(scattered[b], 16 * BATCH * turn + 16)
            act.sem_inc(gate, 1)
            act.copy(ring[b].rearrange("p (u k) w -> p k u w", u=HALF),
                     records[:, :, bass.ds(RANKS * turn + HALF * b, HALF), :]).then_inc(ring_made, 1)

        def scatter(pool, turn, b):
            pool.wait_ge(addr_made, 2 * turn + b + 1)
            pool.wait_ge(ring_made, 2 * turn + b + 1)
            pool.sem_inc(pool_go, 1)
            for c in range(BATCH):
                pool.indirect_dma_start(table_d, bass.IndirectOffsetOnAxis(addr[b][:, c:c + 1], 0), ring[b][:, c, :],
                                        None).then_inc(scattered[b], 16)

        kv_sum = [banks[1][:, 0:P + 1], banks[2][:, 0:P + 1]]

        with nc.Block() as block:
            @block.sync
            def _(sp):
                with sp.Fori(0, TURNS) as i:
                    for j in range(BODY):
                        sp.wait_ge(x_used, BODY * i + j + 1)
                        sp.dma_start(xt[j % 2], x[bass.ds((BODY * i + j) * T, T), :]).then_inc(x_in[j], 16)

            @block.gpsimd
            def _(pool):
                with pool.Fori(0, TURNS) as i:
                    for b in range(2):
                        scatter(pool, i, b)

            @block.tensor
            def _(pe):
                pe.matmul(ranks, ones_f[0:1, 0:T], base[0:1, :, :].rearrange("p k b -> p (k b)"), start=True,
                          stop=False, skip_group_check=True)
                for f in range(H2):
                    mm = pe.matmul(kv_sum[f], zero_b[:, :], hot[0].rearrange("p k b -> p (k b)")[:, 0:P + 1],
                                   start=True, stop=False, skip_group_check=True)
                mm.then_inc(sums_open, 1)
                with pe.Fori(0, TURNS) as i:
                    for j in range(BODY):
                        t, r = BODY * i + j, RANKS * i + 2 * j
                        rank_before(pe, r, 0)
                        pe.wait_ge(xn_made, t + 1)
                        for f in range(H2):
                            mm = pe.transpose(banks[3][:, f * T:(f + 1) * T], xn[j % 2][:, f * P:(f + 1) * P],
                                              ident[0:T, 0:T])
                        mm.then_inc(xT_ps, 1)
                        rank_advance(pe, r, 0)
                        pe.wait_ge(xnT_made, t + 1)
                        pe.wait_ge(kv_read, t + 1)
                        pe.wait_ge(sup_read, t + 1)
                        for n, w in enumerate((wk, wv)):
                            for f in range(H2):
                                mm = pe.matmul(banks[5][0:T, n * D:(n + 1) * D], xnT[:, f * T:(f + 1) * T], w[:, f, :],
                                               start=f == 0, stop=f == H2 - 1)
                        mm.then_inc(kv_ps, 1)
                        for m in range(H2):
                            for f in range(H2):
                                mm = pe.matmul(banks[6][:, m * T:(m + 1) * T], wq[:, f, m * P:(m + 1) * P],
                                               xnT[:, f * T:(f + 1) * T], start=f == 0, stop=f == H2 - 1)
                        mm.then_inc(q_ps, 1)
                        for f in range(H2):
                            mm = pe.matmul(banks[4][0:T, 0:D], xnT[:, f * T:(f + 1) * T], wg[:, f, :], start=f == 0,
                                           stop=f == H2 - 1)
                        mm.then_inc(sup_ps, 1)
                        rank_before(pe, r + 1, 1)
                        pe.wait_ge(kphi_made, t + 1)
                        for f in range(H2):
                            mm = pe.matmul(kv_sum[f], kphi[:, f * P:(f + 1) * P], vt[:, f, :], start=False, stop=False,
                                           skip_group_check=True)
                        mm.then_inc(kv_added, 1)
                        rank_advance(pe, r + 1, 1)

            @block.scalar
            def _(act):
                with act.Fori(0, TURNS) as i:
                    for j in range(BODY):
                        t = BODY * i + j
                        if j % 2 == 0:
                            ring_records(act, i, j // 2)
                        act.wait_ge(xT_ps, t + 1)
                        act.copy(xnT, banks[3][:, 0:H2 * T]).then_inc(xnT_made, 1)
                        act.wait_ge(km_made, t + 1)
                        act.activation(ke, ke, ACT.Exp).then_inc(ke_made, 1)
                        act.wait_ge(q_ps, t + 1)
                        for m in range(H2):
                            mm = act.activation(qb[:, m * T:(m + 1) * T], banks[6][:, m * T:(m + 1) * T], ACT.Identity,
                                                bias=bqc[:, m:m + 1])
                        mm.then_inc(qb_made, 1)
                        act.wait_ge(stored[(j + 2) % BODY], 48 * i + 48)
                        act.wait_ge(sup_ps, t + 1)
                        act.copy(sup[j % 2], banks[4][0:T, 0:D]).then_inc(sup_read, 1)
                        act.wait_ge(qm_made, t + 1)
                        act.activation(qe, qe, ACT.Exp).then_inc(qe_made, 1)
                        act.wait_ge(sup_read, t + 2)
                        act.dma_start(support_d[bass.ds(t * T, T), :], sup[j % 2]).then_inc(stored[j], 16)
                        act.dma_start(xn_d[bass.ds(t * T, T), :], xn[j % 2]).then_inc(stored[j], 16)
                        act.wait_ge(qphi_made, t + 1)
                        act.dma_start(q_d[bass.ds(t, 1)].rearrange("t p c -> (t p) c"), qphi[j % 2]).then_inc(stored[j], 16)
                for j in range(BODY):
                    act.wait_ge(stored[j], 48 * (TURNS + (j >= 2)))

            @block.vector
            def _(dve):
                dve.memset(vt[:, :, P:P + 1], 1.0)
                dve.wait_ge(sums_open, 1)
                with dve.Fori(0, TURNS) as i:
                    a = Steps(dve, a_step, A_STEPS * i)
                    for j in range(BODY):
                        t, r = BODY * i + j, RANKS * i + 2 * j
                        rank_hot(dve, r, 0)
                        dve.wait_ge(x_in[j], 16 * i + 16)
                        moments(a, dve, xt[j % 2], ln)
                        rsqrt_newton(a, dve, ln)
                        dve.wait_ge(stored[(j + 2) % BODY], 48 * i + 48)
                        dve.tensor_scalar(xn[j % 2], xt[j % 2], ln[:, 6:7], ln[:, 8:9], ALU.subtract,
                                          ALU.mult).then_inc(xn_made, 1)
                        dve.wait_ge(xn_made, t + 1)
                        dve.sem_inc(x_used, 1)
                        rank_sum(dve, r, 2 * j % HALF)
                        rank_hot(dve, r + 1, 1)
                        dve.wait_ge(kv_ps, t + 1)
                        dve.wait_ge(kv_added, t + 1)
                        a.then(dve.tensor_tensor(kb, banks[5][0:T, 0:D], rows["bkr"][:, :], ALU.add))
                        dve.tensor_scalar(ke, kb, 0.0, None, ALU.min).then_inc(km_made, 1)
                        dve.tensor_tensor(vt[:, :, 0:P], banks[5][0:T, D:2 * D].rearrange("p (f c) -> p f c", f=H2),
                                          rows["bvr"][:, :].rearrange("p (f c) -> p f c", f=H2), ALU.add).then_inc(kv_read, 1)
                        dve.wait_ge(ke_made, t + 1)
                        dve.wait_ge(kv_read, t + 2)
                        dve.scalar_tensor_tensor(kphi, kb, 0.0, ke, ALU.max, ALU.add).then_inc(kphi_made, 1)
                        dve.wait_ge(qb_made, t + 1)
                        dve.tensor_scalar(qe, qb, 0.0, None, ALU.min).then_inc(qm_made, 1)
                        rank_sum(dve, r + 1, 2 * j % HALF + 1)
                        dve.wait_ge(qe_made, t + 1)
                        dve.scalar_tensor_tensor(qphi[j % 2], qb, 0.0, qe, ALU.max, ALU.add).then_inc(qphi_made, 1)
                        if j % 2:
                            addresses(dve, i, j // 2, a)
                    assert a.n == A_STEPS, a.n
                dve.wait_ge(kv_added, NT + 1)
                for f in range(H2):
                    for h in range(HPH):
                        q = slice(h * DH, (h + 1) * DH)
                        dve.tensor_copy(kvb[q, f, q], kv_sum[f][q, q]).then_inc(kvb_made, 1)
                        dve.tensor_copy(kvb[q, f, P + h:P + h + 1], kv_sum[f][q, P:P + 1]).then_inc(kvb_made, 1)

        with nc.Block() as block:
            @block.sync
            def _(sp):
                def load(i, j):
                    t = BODY * i + j
                    sp.wait_ge(mix_used, t + 1)
                    sp.dma_start(qT[j % 2], q_d[bass.ds(t, 1)].rearrange("t p c -> (t p) c")).then_inc(mix_in[j], 16)
                    sp.dma_start(xr[j % 2], xn_d[bass.ds(t * T, T), :]).then_inc(mix_in[j], 16)
                    sp.dma_start(xo[j % 2], x[bass.ds(t * T, T), :]).then_inc(mix_in[j], 16)

                with sp.Fori(0, TURNS) as i:
                    for j in range(BODY):
                        load(i, j)

            @block.gpsimd
            def _(pool):
                with pool.Fori(TURNS, 2 * TURNS) as i:
                    for b in range(2):
                        scatter(pool, i, b)
                for b in range(2):
                    pool.wait_ge(scattered[b], 16 * BATCH * 2 * TURNS + 16)

            attn = banks[1][0:T, 0:H2 * KVW]

            @block.tensor
            def _(pe):
                def attend(i, j):
                    pe.wait_ge(mix_in[j], 48 * i + 48)
                    for f in range(H2):
                        mm = pe.matmul(attn[:, f * KVW:(f + 1) * KVW], qT[j % 2][:, f * T:(f + 1) * T], kvb[:, f, :],
                                       start=True, stop=True)
                    mm.then_inc(at_ps, 1)

                def turn_attention(t):
                    pe.wait_ge(at_made, t + 1)
                    for f in range(H2):
                        mm = pe.transpose(banks[2][:, f * T:(f + 1) * T], at[:, f * P:(f + 1) * P], ident[0:T, 0:T])
                    mm.then_inc(atT_ps, 1)

                def project(t):
                    pe.wait_ge(atT_made, t + 1)
                    for f in range(H2):
                        mm = pe.matmul(banks[3][0:T, 0:D], atT[:, f * T:(f + 1) * T], wo[:, f, :], start=f == 0,
                                       stop=f == H2 - 1)
                    mm.then_inc(wo_ps, 1)

                def turn_x1(t, j):
                    pe.wait_ge(x1_made, t + 1)
                    for f in range(H2):
                        mm = pe.transpose(banks[4][:, f * T:(f + 1) * T], x1[j % 2][:, f * P:(f + 1) * P],
                                          ident[0:T, 0:T])
                    mm.then_inc(x1T_ps, 1)

                def widen(t, c):
                    if c == 0:
                        pe.wait_ge(x1T_made, t + 1)
                        pe.wait_ge(ff_read, t + 1)
                    for m in range(c * FC // 2, (c + 1) * FC // 2):
                        for f in range(H2):
                            mm = pe.matmul(banks[5 + c][:, m % 4 * T:(m % 4 + 1) * T], w1[:, f, m * P:(m + 1) * P],
                                           x1T[:, f * T:(f + 1) * T], start=f == 0, stop=f == H2 - 1)
                    mm.then_inc(h_ps, 1)

                def narrow(t):
                    pe.wait_ge(h_made, t + 1)
                    for m in range(FC):
                        mm = pe.matmul(banks[7][0:T, 0:D], hT[:, m, :], w2[:, m, :], start=m == 0, stop=m == FC - 1)
                    mm.then_inc(ff_ps, 1)

                def turn(i, last=False):
                    for j in range(BODY):
                        t, r = BODY * i + j, RANKS * (i + TURNS) + 2 * j
                        front = not (last and j == BODY - 1)
                        n = (i, j + 1) if j < BODY - 1 else (i + 1, 0)
                        rank_before(pe, r, 0)
                        if front:
                            attend(*n)
                        widen(t, 0)
                        rank_advance(pe, r, 0)
                        if front:
                            turn_attention(t + 1)
                        widen(t, 1)
                        rank_before(pe, r + 1, 1)
                        if front:
                            project(t + 1)
                        narrow(t)
                        rank_advance(pe, r + 1, 1)
                        if front:
                            turn_x1(t + 1, j + 1)

                pe.wait_ge(kvb_made, 4 * HPH)
                attend(0, 0)
                turn_attention(0)
                project(0)
                turn_x1(0, 0)
                with pe.Fori(0, TURNS - 1) as i:
                    turn(i)
                turn(TURNS - 1, last=True)

            @block.scalar
            def _(act):
                def copies(t):
                    act.wait_ge(atT_ps, t + 1)
                    act.copy(atT, banks[2][:, 0:H2 * T]).then_inc(atT_made, 1)

                def hidden(t, c):
                    act.wait_ge(h_ps, 2 * t + c + 1)
                    for m in range(c * FC // 2, (c + 1) * FC // 2):
                        mm = act.activation(hT[:, m, :], banks[5 + c][:, m % 4 * T:(m % 4 + 1) * T], ACT.Relu,
                                            bias=b1c[:, m:m + 1])
                    if c:
                        mm.then_inc(h_made, 1)

                def x1_copy(t):
                    act.wait_ge(x1T_ps, t + 1)
                    act.copy(x1T, banks[4][:, 0:H2 * T]).then_inc(x1T_made, 1)

                def turn(i, last=False):
                    for j in range(BODY):
                        t = BODY * i + j
                        front = not (last and j == BODY - 1)
                        if j % 2 == 0:
                            ring_records(act, i + TURNS, j // 2)
                        hidden(t, 0)
                        if front:
                            copies(t + 1)
                        hidden(t, 1)
                        if front:
                            deviation(t + 1, var1_made, std1_made, ln)
                            x1_copy(t + 1)
                        deviation(t, var2_made, std2_made, ln2)

                def deviation(t, variance, made, stats):
                    act.wait_ge(variance, t + 1)
                    act.activation(stats[:, 9:10], stats[:, 7:8], ACT.Sqrt, bias=eps[:, 0:1]).then_inc(made, 1)

                copies(0)
                deviation(0, var1_made, std1_made, ln)
                x1_copy(0)
                with act.Fori(0, TURNS - 1) as i:
                    turn(i)
                turn(TURNS - 1, last=True)

            @block.vector
            def _(dve):
                def normalise(b, i, j):
                    t = BODY * i + j
                    dve.wait_ge(at_ps, t + 1)
                    halves = attn.rearrange("p (f c) -> p f c", f=H2)
                    b.then(dve.tensor_scalar(zr, halves[:, :, P:KVW], 1e-6, None, ALU.add))
                    b.then(dve.reciprocal(zr, zr))
                    for f in range(H2):
                        mm = dve.tensor_tensor(at[:, f * P:(f + 1) * P].rearrange("p (h e) -> p h e", h=HPH),
                                               halves[:, f, 0:P].rearrange("p (h e) -> p h e", h=HPH),
                                               zr[:, f, :].unsqueeze(2).to_broadcast([T, HPH, DH]), ALU.mult)
                    mm.then_inc(at_made, 1)

                def first_norm(b, i, j):
                    t = BODY * i + j
                    b.then(dve.tensor_tensor(xr[j % 2], xr[j % 2], rows["bor"][:, :], ALU.add))
                    dve.wait_ge(wo_ps, t + 1)
                    b.then(dve.tensor_tensor(r1, banks[3][0:T, 0:D], xr[j % 2], ALU.add))
                    moments(b, dve, r1, ln)
                    dve.sem_inc(var1_made, 1)
                    dve.wait_ge(std1_made, t + 1)
                    b.then(dve.reciprocal(ln[:, 8:9], ln[:, 9:10]))
                    b.then(dve.tensor_scalar(r1, r1, ln[:, 6:7], ln[:, 8:9], ALU.subtract, ALU.mult))
                    b.then(dve.tensor_tensor(r1, r1, rows["g1r"][:, :], ALU.mult))
                    b.then(dve.tensor_tensor(x1[j % 2], r1, rows["be1r"][:, :], ALU.add))
                    dve.sem_inc(x1_made, 1)

                def second_norm(b, i, j):
                    t = BODY * i + j
                    dve.wait_ge(x1T_ps, t + 1)
                    b.then(dve.tensor_tensor(x1[j % 2], x1[j % 2], rows["b2r"][:, :], ALU.add))
                    b.then(dve.tensor_tensor(xo[j % 2], xo[j % 2], rows["be2r"][:, :], ALU.add))
                    dve.wait_ge(ff_ps, t + 1)
                    dve.tensor_tensor(r2, banks[7][0:T, 0:D], x1[j % 2], ALU.add).then_inc(ff_read, 1)
                    dve.wait_ge(ff_read, t + 2)
                    moments(b, dve, r2, ln2)
                    dve.sem_inc(var2_made, 1)
                    dve.wait_ge(std2_made, t + 1)
                    b.then(dve.reciprocal(ln2[:, 8:9], ln2[:, 9:10]))
                    b.then(dve.tensor_scalar(r2, r2, ln2[:, 6:7], ln2[:, 8:9], ALU.subtract, ALU.mult))
                    b.then(dve.tensor_tensor(r2, r2, rows["g2r"][:, :], ALU.mult))
                    b.then(dve.tensor_tensor(acc_flat[:, bass.ds(t * D, D)], r2, xo[j % 2], ALU.add))
                    dve.sem_inc(mix_used, 1)

                def turn(i, last=False):
                    b = Steps(dve, b_step, B_FRONT + B_STEPS * i)
                    for j in range(BODY):
                        t, r = BODY * i + j, RANKS * (i + TURNS) + 2 * j
                        front = not (last and j == BODY - 1)
                        n = (i, j + 1) if j < BODY - 1 else (i + 1, 0)
                        rank_hot(dve, r, 0)
                        if front:
                            normalise(b, *n)
                        rank_sum(dve, r, 2 * j % HALF)
                        rank_hot(dve, r + 1, 1)
                        if front:
                            first_norm(b, *n)
                        rank_sum(dve, r + 1, 2 * j % HALF + 1)
                        second_norm(b, i, j)
                        if j % 2:
                            addresses(dve, i + TURNS, j // 2, b)
                    assert last or b.n == B_STEPS, b.n

                b = Steps(dve, b_step)
                normalise(b, 0, 0)
                first_norm(b, 0, 0)
                assert b.n == B_FRONT, b.n
                with dve.Fori(0, TURNS - 1) as i:
                    turn(i)
                turn(TURNS - 1, last=True)

        products = [banks[b][0:T, :] for b in range(AHEAD)]
        with nc.Block() as block:
            @block.sync
            def _(sp):
                sp.dma_start(binof, binof_d.rearrange("(a c) -> a c", a=1)).then_inc(bins_in, 16)
                table_groups = table_d.rearrange("(g p c) w -> g p (c w)", p=P, c=CH)

                def load(g, h):
                    sp.dma_start(recs[h].rearrange("p c w -> p (c w)"),
                                 table_groups[bass.ds(g, 1)].rearrange("g p c -> (g p) c")).then_inc(recs_in[h], 16)

                load(0, 0)
                load(1, 1)
                with sp.Fori(0, GROUPS // 2) as i:
                    for h in range(2):
                        sp.wait_ge(recs_used, 2 * i + h + 1)
                        load(2 * i + h + 2, h)
                for h in range(2):
                    sp.wait_ge(recs_in[h], 16 * (GROUPS // 2 + 1))

            @block.gpsimd
            def _(pool):
                with pool.Fori(0, GROUPS // 2) as i:
                    for h in range(2):
                        for q in range(4):
                            if q == 0:
                                pool.wait_ge(gidx_made, 2 * i + h + 1)
                            pool.wait_ge(pair_ps, PAIRS * (2 * i + h) + 2 * q + 2)
                            pool.sem_inc(pool_go, 1)
                            for c in range(4 * q, 4 * q + 4):
                                pool.indirect_dma_start(rowbuf[h][c], None, support_d,
                                                        bass.IndirectOffsetOnAxis(gidx[h][:, c:c + 1], 0)
                                                        ).then_inc(landed[4 * h + q], 16)

            @block.tensor
            def _(pe):
                with pe.Fori(0, GROUPS // 2) as i:
                    for h in range(2):
                        g = 2 * i + h
                        for p in range(PAIRS):
                            if p % 2 == 0:
                                pe.wait_ge(landed[4 * h + p // 2], 64 * i + 64)
                            pe.wait_ge(onehot_made, PAIRS * g + p + 1)
                            pe.wait_ge(acc_step, CH * g + 2 * p + 2)
                            for c in range(2):
                                mm = pe.matmul(products[p % AHEAD][:, c * D:(c + 1) * D], onehot[p % AHEAD][:, c, :],
                                               rowbuf[h][2 * p + c], start=True, stop=True)
                            mm.then_inc(pair_ps, 1)

            @block.vector
            def _(dve):
                def select(h, p, c):
                    mm = dve.tensor_scalar(onehot[p % AHEAD][:, c, :], iota_n[:, :], recs[h][:, 2 * p + c, 1:2],
                                           recs[h][:, 2 * p + c, 2:3], ALU.is_equal, ALU.mult)
                    if c:
                        mm.then_inc(onehot_made, 1)

                column_regs = [dve.alloc_register(f"column{c}") for c in range(CH)]
                dve.wait_ge(bins_in, 16)
                dve.wait_ge(recs_in[0], 16)
                dve.tensor_copy(gidx[0], recs[0][:, :, 0]).then_inc(gidx_made, 1)
                for p in range(2):
                    for c in range(2):
                        select(0, p, c)
                with dve.Fori(0, GROUPS // 2) as i:
                    for h in range(2):
                        g = 2 * i + h
                        dve.load(column_regs, binof[0:1, bass.ds(CH * g, CH)])
                        columns = [dve.snap(c, min_val=0, max_val=(NT - 1) * D) for c in column_regs]
                        dve.wait_ge(recs_in[1 - h], 16 * i + 16 + 16 * h)
                        dve.tensor_copy(gidx[1 - h], recs[1 - h][:, :, 0]).then_inc(gidx_made, 1)
                        for p in range(PAIRS):
                            if p == PAIRS - 2:
                                dve.wait_ge(onehot_made, PAIRS * (g + 1))
                                dve.sem_inc(recs_used, 1)
                            dve.wait_ge(pair_ps, PAIRS * (g + 2) + p + 1)
                            for c in range(2):
                                a = acc_flat[:, bass.ds(columns[2 * p + c], D)]
                                dve.wait_ge(acc_step, CH * g + 2 * p + c + 8)
                                dve.tensor_tensor(a, products[p % AHEAD][:, c * D:(c + 1) * D], a, ALU.add).then_inc(acc_step, 1)
                                if p < PAIRS - 2:
                                    select(h, p + 2, c)
                                else:
                                    select(1 - h, p + 2 - PAIRS, c)

        with nc.Block() as block:
            @block.sync
            def _(sp):
                with sp.Fori(0, NT // 2) as i:
                    for h in range(2):
                        sp.wait_ge(res_made, 2 * i + h + 1)
                        sp.dma_start(out[bass.ds((2 * i + h) * T, T), :], res[h]).then_inc(out_stored[h], 16)
                for h in range(2):
                    sp.wait_ge(out_stored[h], 16 * (NT // 2) + 16)

            @block.gpsimd
            def _(pool):
                with pool.Fori(0, NT) as t:
                    pool.wait_ge(var_made, t + 1)
                    pool.tensor_tensor(lne[:, 8:9], lne[:, 9:10], eps[:, 1:2], ALU.pow).then_inc(rstd_made, 1)

            @block.tensor
            def _(pe):
                def turn_y(t, h):
                    pe.wait_ge(yn_made, t + 1)
                    for f in range(H2):
                        mm = pe.transpose(banks[0][:, f * T:(f + 1) * T], yn[h][:, f * P:(f + 1) * P], ident[0:T, 0:T])
                    mm.then_inc(yT_ps, 1)

                def first(t):
                    pe.wait_ge(yT_made, t + 1)
                    pe.wait_ge(gate_read, t + 1)
                    for f in range(H2):
                        pe.matmul(banks[1][0:T, 0:NE], yT[:, f * T:(f + 1) * T], gw[:, f, :], start=f == 0,
                                  stop=f == H2 - 1)
                    for m in range(H2):
                        for f in range(H2):
                            pe.matmul(banks[2][:, m * T:(m + 1) * T], sw1[:, f, m * P:(m + 1) * P],
                                      yT[:, f * T:(f + 1) * T], start=f == 0, stop=f == H2 - 1)
                    for e in range(NE):
                        for f in range(H2):
                            mm = pe.matmul(banks[3][:, e * T:(e + 1) * T], ew1[:, f, e, :], yT[:, f * T:(f + 1) * T],
                                           start=f == 0, stop=f == H2 - 1)
                    mm.then_inc(l1_ps, 1)

                def second(t):
                    pe.wait_ge(l1_made, t + 1)
                    for m in range(H2):
                        pe.matmul(banks[2][:, H2 * T:(H2 + 1) * T], sw2[:, m, :], s1T[:, m, :], start=m == 0,
                                  stop=m == H2 - 1)
                    for e in range(NE):
                        mm = pe.matmul(banks[4][0:EH2, e * T:(e + 1) * T], ew2[:, e, :], e1T[:, e, :], start=True,
                                       stop=True)
                    mm.then_inc(l2_ps, 1)

                def third(t):
                    pe.wait_ge(l2_made, t + 1)
                    pe.wait_ge(l3_read, t + 1)
                    pe.matmul(banks[5][0:T, 0:D], s2T, sw3[:, :], start=True, stop=True)
                    for e in range(NE):
                        mm = pe.matmul(banks[6 + e // 2][0:T, e % 2 * D:(e % 2 + 1) * D], e2T[:, e, :], ew3[:, e, :],
                                       start=True, stop=True)
                    mm.then_inc(l3_ps, 1)

                turn_y(0, 0)
                first(0)
                second(0)
                turn_y(1, 1)
                with pe.Fori(0, NT // 2 - 1) as i:
                    for h in range(2):
                        t = 2 * i + h + 1
                        first(t)
                        third(t - 1)
                        second(t)
                        turn_y(t + 1, h)
                first(NT - 1)
                third(NT - 2)
                second(NT - 1)
                third(NT - 1)

            @block.scalar
            def _(act):
                def copy_y(t):
                    act.wait_ge(yT_ps, t + 1)
                    act.copy(yT, banks[0][:, 0:H2 * T]).then_inc(yT_made, 1)

                def hidden(t):
                    act.wait_ge(l1_ps, t + 1)
                    for m in range(H2):
                        act.activation(s1T[:, m, :], banks[2][:, m * T:(m + 1) * T], ACT.Relu, bias=sb1c[:, m:m + 1])
                    for e in range(NE):
                        mm = act.activation(e1T[:, e, :], banks[3][:, e * T:(e + 1) * T], ACT.Relu, bias=eb1c[:, e:e + 1])
                    mm.then_inc(l1_made, 1)
                    act.wait_ge(gexp_go, 2 * t + 1)
                    act.activation(soft, soft, ACT.Exp).then_inc(gexp_made, 1)
                    act.wait_ge(l2_ps, t + 1)
                    act.activation(s2T, banks[2][:, H2 * T:(H2 + 1) * T], ACT.Relu, bias=sb2c[:, 0:1])
                    for e in range(NE):
                        mm = act.activation(e2T[0:EH2, e, :], banks[4][0:EH2, e * T:(e + 1) * T], ACT.Relu,
                                            bias=eb2c[:, e:e + 1])
                    mm.then_inc(l2_made, 1)
                    act.wait_ge(gexp_go, 2 * t + 2)
                    act.activation(soft, soft, ACT.Exp).then_inc(gexp_made, 1)

                copy_y(0)
                hidden(0)
                with act.Fori(0, NT // 2 - 1) as i:
                    for h in range(2):
                        copy_y(2 * i + h + 1)
                        hidden(2 * i + h + 1)
                copy_y(NT - 1)
                hidden(NT - 1)

            @block.vector
            def _(dve):
                def norm(e, t, h):
                    row = acc_flat[:, bass.ds(t * D, D)]
                    moments(e, dve, row, lne)
                    dve.tensor_scalar(lne[:, 9:10], lne[:, 7:8], LN_EPS, None, ALU.add).then_inc(var_made, 1)
                    dve.wait_ge(rstd_made, t + 1)
                    dve.tensor_scalar(yn[h], row, lne[:, 6:7], lne[:, 8:9], ALU.subtract, ALU.mult).then_inc(yn_made, 1)
                    dve.wait_ge(yn_made, t + 1)

                def route(e, t, h):
                    dve.wait_ge(l1_ps, t + 1)
                    dve.tensor_tensor(logit, banks[1][0:T, 0:NE], gbr[:, :], ALU.add).then_inc(gate_read, 1)
                    dve.wait_ge(gate_read, t + 2)
                    e.then(dve.tensor_reduce(gstat[:, 0:1], logit, AX.X, ALU.max))
                    dve.tensor_scalar(soft, logit, gstat[:, 0:1], None, ALU.subtract).then_inc(gexp_go, 1)
                    dve.wait_ge(gexp_made, 2 * t + 1)
                    e.then(dve.tensor_reduce(gstat[:, 1:2], soft, AX.X, ALU.add))
                    e.then(dve.reciprocal(gstat[:, 2:3], gstat[:, 1:2]))
                    e.then(dve.tensor_scalar(logit, soft, gstat[:, 2:3], None, ALU.mult))
                    mine = logit.unsqueeze(2).to_broadcast([T, NE, NE])
                    others = logit.unsqueeze(1).to_broadcast([T, NE, NE])
                    e.then(dve.tensor_tensor(beats, others, mine, ALU.is_gt))
                    e.then(dve.tensor_tensor(ties, others, mine, ALU.is_equal))
                    e.then(dve.tensor_tensor(ties, ties, tiebreak[:, :, :], ALU.mult))
                    e.then(dve.tensor_tensor(beats, beats, ties, ALU.add))
                    e.then(dve.tensor_reduce(rank4, beats, AX.X, ALU.add))
                    e.then(dve.tensor_scalar(chosen, rank4, 1.5, None, ALU.is_lt))
                    e.then(dve.tensor_reduce(gstat[:, 0:1], logit, AX.X, ALU.max))
                    dve.tensor_scalar(soft, logit, gstat[:, 0:1], None, ALU.subtract).then_inc(gexp_go, 1)
                    dve.wait_ge(gexp_made, 2 * t + 2)
                    e.then(dve.tensor_tensor(soft, soft, chosen, ALU.mult))
                    e.then(dve.tensor_reduce(gstat[:, 1:2], soft, AX.X, ALU.add))
                    e.then(dve.reciprocal(gstat[:, 2:3], gstat[:, 1:2]))
                    e.then(dve.tensor_scalar(gwt[h], soft, gstat[:, 2:3], None, ALU.mult))

                def combine(e, t, h, use):
                    dve.wait_ge(l3_ps, t + 1)
                    dve.wait_ge(out_stored[h], use)
                    e.then(dve.tensor_tensor(res[h], banks[5][0:T, 0:D], acc_flat[:, bass.ds(t * D, D)], ALU.add))
                    e.then(dve.tensor_tensor(res[h], res[h], rows["sb3r"][:, :], ALU.add))
                    for n in range(NE):
                        e.then(dve.scalar_tensor_tensor(res[h], banks[6 + n // 2][0:T, n % 2 * D:(n % 2 + 1) * D],
                                                        gwt[h][:, n:n + 1], res[h], ALU.mult, ALU.add))
                    dve.sem_inc(l3_read, 1)
                    dve.sem_inc(res_made, 1)

                e = Steps(dve, e_step)
                e.then(dve.memset(e2T[EH2:EH2 + 1, :, :], 1.0))
                norm(e, 0, 0)
                norm(e, 1, 1)
                route(e, 0, 0)
                assert e.n == E_FRONT, e.n
                with dve.Fori(0, NT // 2 - 1) as i:
                    e = Steps(dve, e_step, E_FRONT + E_STEPS * i)
                    for h in range(2):
                        t = 2 * i + h + 1
                        norm(e, t + 1, h)
                        route(e, t, 1 - h)
                        combine(e, t - 1, h, 16 * i + 16)
                    assert e.n == E_STEPS, e.n
                e = Steps(dve, e_step, E_FRONT + E_STEPS * (NT // 2 - 1))
                route(e, NT - 1, 1)
                combine(e, NT - 2, 0, 16 * (NT // 2))
                combine(e, NT - 1, 1, 16 * (NT // 2))


_INS = ["x", "src", "dst", "edge_weight", "L0_gnn_weight", "L0_mix_Wq", "L0_mix_bq", "L0_mix_Wk", "L0_mix_bk",
        "L0_mix_Wv", "L0_mix_bv", "L0_mix_Wo", "L0_mix_bo", "L0_mix_W1", "L0_mix_b1", "L0_mix_W2", "L0_mix_b2",
        "L0_mix_ln1_g", "L0_mix_ln1_b", "L0_mix_ln2_g", "L0_mix_ln2_b", "L0_ffn_sW1", "L0_ffn_sb1", "L0_ffn_sW2",
        "L0_ffn_sb2", "L0_ffn_sW3", "L0_ffn_sb3", "L0_ffn_eW1", "L0_ffn_eb1", "L0_ffn_eW2", "L0_ffn_eb2",
        "L0_ffn_eW3", "L0_ffn_eb3", "L0_ffn_gW", "L0_ffn_gb"]
_OUTS = [((N, D), "float32")]


def kernel(**inputs):
    import numpy as _np
    import concourse.bacc as _bacc
    from concourse import mybir as _mybir
    from concourse.bass_utils import run_bass_kernel_spmd as _run

    nc = _bacc.Bacc("TRN2", target_bir_lowering=False, num_devices=1)
    arrays, args = {}, []
    for name in _INS:
        a = _np.ascontiguousarray(inputs[name])
        arrays[f"in_{name}_dram"] = a
        args.append(nc.dram_tensor(f"in_{name}_dram", a.shape, _mybir.dt.from_np(a.dtype), kind="ExternalInput").ap())
    for i, (shape, dtype) in enumerate(_OUTS):
        dt = _mybir.dt.from_np(_np.dtype(dtype))
        args.append(nc.dram_tensor(f"out_{i}_dram", shape, dt, kind="ExternalOutput").ap())
    build(nc, *args)
    r = _run(nc, [arrays], core_ids=[0])
    return r.results[0]["out_0_dram"]
```

```python
from contextlib import ExitStack

import concourse.bass as bass
from concourse import mybir

ALU = mybir.AluOpType
ACT = mybir.ActivationFunctionType
AX = mybir.AxisListType
F32, BF16, I32 = mybir.dt.float32, mybir.dt.bfloat16, mybir.dt.int32

N, D, E = 12500, 256, 200000
T = 125
NT = N // T
P = 128
H2 = D // P
HEADS, DH = 8, 32
HPH = P // DH
RW = 3
FF = 1024
FC = FF // P
NE, EH2 = 4, 64
COLS = E // T
STREAMS = 4
SC = COLS // STREAMS
BODY = 4
TURNS = NT // BODY
RANKS = SC // (2 * TURNS)
HALF = RANKS // 2
BATCH = HALF * STREAMS
CH = 16
GROUPS = -(-((E + NT * (P - 1)) // P) // (2 * CH)) * 2
CHUNKS = GROUPS * CH
CPP = 16
CPART = CHUNKS // CPP
GROUP = CH * P
SLOTS = (GROUPS + 2) * GROUP
assert RANKS * 2 * TURNS == SC and SC * STREAMS == COLS and COLS * T == E and CPP * CPART == CHUNKS and CPART <= T
ZEROS = GROUP * RW // 2
LN_EPS = 1e-5
A_STEPS, A_FRONT, B_STEPS, B_FRONT, B_BACK, E_STEPS, E_FRONT = 31, 23, 80, 10, 8, 46, 20
KVW = P + HPH


class Steps:

    def __init__(self, engine, sem, base=0):
        self.engine, self.sem, self.base, self.n = engine, sem, base, 0

    def issue(self, instruction):
        self.n += 1
        instruction.then_inc(self.sem, 1)

    def settle(self):
        self.engine.wait_ge(self.sem, self.base + self.n)

    def then(self, instruction):
        self.issue(instruction)
        self.settle()


def build(nc, x, src, dst, edge_weight, Wg, Wq, bq, Wk, bk, Wv, bv, Wo, bo, W1, b1, W2, b2, g1, be1, g2, be2,
          sW1, sb1, sW2, sb2, sW3, sb3, eW1, eb1, eW2, eb2, eW3, eb3, gW, gb, out):
    ctx = ExitStack()
    with ctx:
        def sb(name, shape, dt=F32):
            return ctx.enter_context(nc.sbuf_tensor(name, shape, dt))

        def sem(name):
            return ctx.enter_context(nc.semaphore(name))

        def sems(name, n):
            return [sem(f"{name}{i}") for i in range(n)]

        banks = [ctx.enter_context(nc.psum_tensor(f"bank{i}", [P, 512], F32)) for i in range(8)]

        support_d = nc.dram_tensor("support_rows", [N, D], F32, kind="Internal").ap()
        xn_d = nc.dram_tensor("xn_rows", [N, D], F32, kind="Internal").ap()
        q_d = nc.dram_tensor("q_phi", [NT, P, H2 * T], F32, kind="Internal").ap()
        table_d = nc.dram_tensor("edge_table", [SLOTS, RW], F32, kind="Internal").ap()
        binof_d = nc.dram_tensor("chunk_offsets", [CHUNKS], I32, kind="Internal").ap()

        wg = sb("wg", [P, H2, D])
        wq, wk, wv, wo = (sb(n, [P, H2, D]) for n in ("wq", "wk", "wv", "wo"))
        w1 = sb("w1", [P, H2, FF])
        w2 = sb("w2", [P, FC, D])
        sw1 = sb("sw1", [P, H2, D])
        sw2 = sb("sw2", [P, H2, P])
        sw3 = sb("sw3", [P, D])
        ew1 = sb("ew1", [P, H2, NE, P])
        ew2 = sb("ew2", [P, NE, EH2])
        ew3 = sb("ew3", [EH2 + 1, NE, D])
        gw = sb("gw", [P, H2, NE])
        bqc, b1c = sb("bqc", [P, H2]), sb("b1c", [P, FC])
        sb1c, sb2c = sb("sb1c", [P, H2]), sb("sb2c", [P, 1])
        eb1c, eb2c = sb("eb1c", [P, NE]), sb("eb2c", [EH2, NE])
        rows = {n: sb(n, [T, D]) for n in ("bkr", "bvr", "bor", "g1r", "be1r", "b2r", "g2r", "be2r", "sb3r")}
        gbr = sb("gbr", [T, NE])
        ident = sb("ident", [P, P])
        iota_n = sb("iota_n", [P, T])
        ones_b = sb("ones_b", [T, P], BF16)
        before = sb("before", [T, T], BF16)
        upto = sb("upto", [T, T], BF16)
        iota_b = sb("iota_b", [T, NT], BF16)
        tiebreak = sb("tiebreak", [T, NE, NE])
        kvb = sb("kvb", [P, H2, KVW])
        base = sb("base", [T, STREAMS, NT])
        ones_f = sb("ones_f", [1, P])
        zero_b = sb("zero_b", [T, P], BF16)
        eps = sb("eps", [T, 2])
        acc = sb("acc", [T, NT, D])

        PAIRS = CH // 2
        AHEAD = 4

        WORK = 54 * 1024 // 4
        work = sb("work", [P, WORK])
        acc_flat = acc[:, :, :].rearrange("p a b -> p (a b)")
        top = [0]

        def carve(shape, dt=F32, memory=work):
            words = 1
            for s in shape[1:]:
                words *= s
            words = words if dt != BF16 else -(-words // 2)
            a = memory[0:shape[0], top[0]:top[0] + words]
            top[0] += words
            assert top[0] <= memory.shape[1], top[0]
            if dt != F32:
                a = a.bitcast(dt)
            if len(shape) > 2:
                names = "abcd"[:len(shape) - 1]
                a = a.rearrange(f"p ({' '.join(names)}) -> p {' '.join(names)}",
                                **{k: s for k, s in zip(names, shape[1:])})
            return a

        src_i, dst_i = (carve([T, COLS], I32, acc_flat) for _ in range(2))
        wgt, grp, srcf = (carve([T, COLS], F32, acc_flat) for _ in range(3))
        iota_i = carve([T, P], I32, acc_flat)
        zeros = carve([GROUPS + 2, ZEROS], F32, acc_flat)
        hist = carve([T, STREAMS, NT], F32, acc_flat)
        total, chunks_f, nothing, first, cum, ended = (carve([T, NT], F32, acc_flat) for _ in range(6))
        chunks_i = carve([T, NT], I32, acc_flat)
        chunk_i, bin_i = (carve([CPART, CPP], I32, acc_flat) for _ in range(2))
        chunk_f, bin_f = (carve([CPART, CPP], F32, acc_flat) for _ in range(2))
        top[0] = 0
        rec = carve([T, COLS, RW])
        grp_b = carve([T, COLS], BF16)
        hot = [carve([T, STREAMS, NT], BF16) for _ in range(2)]
        prod = carve([T, STREAMS, NT])
        slot_f = carve([T, BATCH])
        slot_i, slot_t = carve([T, BATCH], I32), carve([T, BATCH], I32)
        addr = [carve([T, BATCH], I32) for _ in range(2)]
        ring = [carve([T, BATCH, RW]) for _ in range(2)]
        ln, ln2 = carve([T, 16]), carve([T, 16])
        spread_top = top[0]
        qT = [carve([P, H2 * T]) for _ in range(BODY)]
        xr = [carve([T, D]) for _ in range(BODY)]
        xo = [carve([T, D]) for _ in range(BODY)]
        zr = carve([T, H2, HPH])
        at = carve([T, D])
        atT, x1T = carve([P, H2 * T]), carve([P, H2 * T])
        r1 = carve([T, D])
        x1 = [carve([T, D]) for _ in range(2)]
        r2 = carve([T, D])
        hT = carve([P, FC, T])
        top[0] = spread_top
        qe, qr = (carve([P, H2 * T]) for _ in range(2))
        xnT = [carve([P, H2 * T]) for _ in range(2)]
        qphi = [carve([P, H2 * T]) for _ in range(2)]
        top[0] = 0
        xt, xn = ([carve([T, D], F32, acc_flat) for _ in range(BODY)] for _ in range(2))
        sup = [carve([T, D], F32, acc_flat) for _ in range(2)]
        stats6, mean_var = carve([T, BODY, 6], F32, acc_flat), carve([T, BODY, 2], F32, acc_flat)
        var4, rstd4, t4 = (carve([T, BODY], F32, acc_flat) for _ in range(3))
        kb, ke, kr, kphi = (carve([T, D], F32, acc_flat) for _ in range(4))
        vt = carve([T, H2, P + 1], F32, acc_flat)
        top[0] = 0
        rowbuf = [[carve([P, D]) for _ in range(CH)] for _ in range(2)]
        onehot = [carve([P, 2, T]) for _ in range(AHEAD)]
        recs = [carve([P, CH, RW]) for _ in range(2)]
        gidx = [carve([P, CH], I32) for _ in range(2)]
        binof = carve([1, CHUNKS], I32)
        top[0] = 0
        yn, res = ([carve([T, D]) for _ in range(2)] for _ in range(2))
        yT = carve([P, H2 * T])
        s1T, e1T = carve([P, H2, T]), carve([P, NE, T])
        s2T, e2T = carve([P, T]), carve([EH2 + 1, NE, T])
        lne = carve([T, 16])
        logit, soft, chosen, rank4 = (carve([T, NE]) for _ in range(4))
        beats, ties = carve([T, NE, NE]), carve([T, NE, NE])
        gstat = carve([T, 4])
        gwt = [carve([T, NE]) for _ in range(2)]


        gate = sem("gate")
        loads, made, pool_step, edges_in = sem("loads"), sem("made"), sem("pool_step"), sem("edges_in")
        dve_step, hist_hot, hist_mm = sem("dve_step"), sem("hist_hot"), sem("hist_mm")
        base_made, bins_out, bins_in = sem("base_made"), sem("bins_out"), sem("bins_in")
        hot_made, rank_ps, rank_read, rank_next = sem("hot_made"), sem("rank_ps"), sem("rank_read"), sem("rank_next")
        rank_step, addr_made, ring_made, pool_go = sem("rank_step"), sem("addr_made"), sem("ring_made"), sem("pool_go")
        scattered = sems("scattered", 2)
        x_in = sems("x_in", BODY)
        a_step, xn_made, xT_ps, xnT_made = (sem(n) for n in ("a_step", "xn_made", "xT_ps", "xnT_made"))
        sup_ps, kv_ps, q_ps, sup_read, kv_read = (sem(n) for n in (
            "sup_ps", "kv_ps", "q_ps", "sup_read", "kv_read"))
        kb_made, ke_made, qe_made, kphi_made, qphi_made, kv_added = (sem(n) for n in (
            "kb_made", "ke_made", "qe_made", "kphi_made", "qphi_made", "kv_added"))
        xn_stored = sems("xn_stored", BODY)
        stored = sems("stored", BODY)
        mix_in = sems("mix_in", BODY)
        sums_open, kvb_made, mix_used, b_step = sem("sums_open"), sem("kvb_made"), sem("mix_used"), sem("b_step")
        at_ps, at_made, atT_ps, atT_made, wo_ps, r1_made, x1_made, x1T_ps, x1T_made, h_ps, h_made, ff_ps, ff_read = (
            sem(n) for n in ("at_ps", "at_made", "atT_ps", "atT_made", "wo_ps", "r1_made", "x1_made", "x1T_ps",
                             "x1T_made", "h_ps", "h_made", "ff_ps", "ff_read"))
        var1_made, std1_made, var2_made, std2_made = (sem(n) for n in ("var1_made", "std1_made", "var2_made", "std2_made"))
        recs_in, landed = sems("recs_in", 2), sems("landed", 8)
        recs_used, gidx_made, onehot_made, pair_ps, acc_step = (sem(n) for n in (
            "recs_used", "gidx_made", "onehot_made", "pair_ps", "acc_step"))
        e_step, yn_made, yT_ps, yT_made, l1_ps, l1_made, l2_ps, l2_made, l3_ps, l3_read, gate_read, res_made = (
            sem(n) for n in ("e_step", "yn_made", "yT_ps", "yT_made", "l1_ps", "l1_made", "l2_ps", "l2_made",
                             "l3_ps", "l3_read", "gate_read", "res_made"))
        var_made, rstd_made = sem("var_made"), sem("rstd_made")
        gexp_go, gexp_made = sem("gexp_go"), sem("gexp_made")
        out_stored = sems("out_stored", 2)

        def moments(steps, dve, source, stats):
            steps.then(dve.bn_stats(stats[:, 0:6], source))
            dve.sem_inc(gate, 1)
            steps.then(dve.bn_aggr(stats[:, 6:8], stats[:, 0:6]))

        columns = [(bqc[:, :], bq.rearrange("(h p) -> p h", p=P)), (b1c[:, :], b1.rearrange("(h p) -> p h", p=P)),
                   (sb1c[:, :], sb1.rearrange("(h p) -> p h", p=P)), (sb2c[:, :], sb2.rearrange("(h p) -> p h", p=P)),
                   (eb1c[:, :], eb1.rearrange("e p -> p e")), (eb2c[:, :], eb2.rearrange("e p -> p e"))]
        blocks = [(w[:, :, :], d.rearrange("(h p) n -> p h n", p=P)) for w, d in
                  ((wg, Wg), (wq, Wq), (wk, Wk), (wv, Wv), (wo, Wo), (w1, W1), (w2, W2), (sw1, sW1), (sw2, sW2), (gw, gW))]
        blocks += [(sw3[:, :], sW3), (ew2[:, :, :], eW2.rearrange("e p n -> p e n")),
                   (ew3[0:EH2, :, :], eW3.rearrange("e p n -> p e n")),
                   (ew3[EH2:EH2 + 1, :, :], eb3.rearrange("(a e) n -> a e n", a=1))]
        blocks += [(ew1[:, :, e, :], eW1[e].rearrange("(h p) n -> p h n", p=P)) for e in range(NE)]
        broadcasts = [(rows[n][:, :], d.partition_broadcast(T)) for n, d in
                      (("bkr", bk), ("bvr", bv), ("bor", bo), ("g1r", g1), ("be1r", be1), ("b2r", b2), ("g2r", g2),
                       ("be2r", be2), ("sb3r", sb3))] + [(gbr[:, :], gb.partition_broadcast(T))]
        n_loads = len(columns) + len(blocks) + len(broadcasts)

        with nc.Block() as block:
            @block.sync
            def _(sp):
                for a, d in ((src_i, src), (dst_i, dst), (wgt, edge_weight)):
                    sp.dma_start(a, d.rearrange("(p c) -> p c", p=T)).then_inc(edges_in, 16)
                for a, d in blocks + broadcasts:
                    sp.dma_start(a, d).then_inc(loads, 16)
                with nc.allow_non_contiguous_dma(reason="bias columns, once"):
                    for a, d in columns:
                        sp.dma_start(a, d).then_inc(loads, 16)
                for s, n in ((rank_next, 2), (kphi_made, 1), (qphi_made, 1), (sup_read, 1), (kv_read, 1), (kv_added, 1),
                             (stored[2], 32), (stored[3], 32), (mix_used, BODY), (ff_read, 1),
                             (pair_ps, 2 * PAIRS), (acc_step, 2 * AHEAD), (l3_read, 1), (gate_read, 1),
                             (out_stored[0], 16), (out_stored[1], 16)):
                    sp.sem_inc(s, n)
                for j in range(BODY):
                    sp.sem_inc(xn_stored[j], 16)
                sp.wait_ge(loads, 16 * n_loads)
                sp.wait_ge(base_made, 1)
                sp.dma_start(binof_d.rearrange("(p c) -> p c", p=CPART), bin_i).then_inc(bins_out, 16)
                sp.wait_ge(bins_out, 16)

            @block.gpsimd
            def _(pool):
                pool.iota(iota_i, pattern=[[1, P]], base=0, channel_multiplier=0).then_inc(made, 1)
                pool.iota(chunk_i, pattern=[[1, CPP]], base=0, channel_multiplier=CPP).then_inc(made, 1)
                pool.iota(iota_n[:, :], pattern=[[1, T]], base=0, channel_multiplier=0,
                          allow_small_or_imprecise_dtypes=True).then_inc(pool_step, 1)
                pool.memset(zeros, 0.0).then_inc(made, 1)
                pool.memset(kvb[:, :, :], 0.0).then_inc(made, 1)
                pool.memset(ident[:, :], 0.0).then_inc(pool_step, 1)
                pool.memset(ones_b[:, :], 1.0).then_inc(pool_step, 1)
                pool.memset(ones_f[:, :], 1.0).then_inc(pool_step, 1)
                pool.memset(zero_b[:, :], 0.0).then_inc(pool_step, 1)
                pool.memset(tiebreak[:, :, :], 1.0).then_inc(pool_step, 1)
                pool.memset(eps[:, 0:1], LN_EPS).then_inc(pool_step, 1)
                pool.memset(eps[:, 1:2], -0.5).then_inc(pool_step, 1)
                pool.wait_ge(pool_step, 8)
                pool.affine_select(out=ident[:, :], in_=ident[:, :], compare_op=ALU.not_equal, fill=1.0, base=0,
                                   pattern=[[-1, P]], channel_multiplier=1).then_inc(pool_step, 1)
                pool.affine_select(out=before[:, :], in_=ones_b[:, 0:T], compare_op=ALU.is_gt, fill=0.0, base=0,
                                   pattern=[[1, T]], channel_multiplier=-1).then_inc(pool_step, 1)
                pool.affine_select(out=upto[:, :], in_=ones_b[:, 0:T], compare_op=ALU.is_ge, fill=0.0, base=0,
                                   pattern=[[-1, T]], channel_multiplier=1).then_inc(pool_step, 1)
                pool.affine_select(out=tiebreak[:, :, :], in_=tiebreak[:, :, :], compare_op=ALU.is_gt, fill=0.0,
                                   base=0, pattern=[[1, NE], [-1, NE]], channel_multiplier=0).then_inc(pool_step, 1)
                pool.wait_ge(made, 4)
                table_rows = table_d.rearrange("(p c) w -> p (c w)", p=GROUPS + 2)
                for k in range(2):
                    pool.dma_start(table_rows[:, k * ZEROS:(k + 1) * ZEROS], zeros).then_inc(scattered[k], 16)
                pool.wait_ge(pool_step, 12)
                for k in range(2):
                    pool.wait_ge(scattered[k], 16)

            MAGIC = 12582912.0

            @block.vector
            def _(dve):
                s = Steps(dve, dve_step)
                dve.wait_ge(edges_in, 48)
                dve.wait_ge(made, 2)
                s.then(dve.tensor_copy(srcf, src_i))
                s.then(dve.tensor_scalar(grp, srcf, -float(T // 2), 1.0 / T, ALU.add, ALU.mult))
                s.then(dve.tensor_scalar(grp, grp, MAGIC, None, ALU.add))
                s.then(dve.tensor_scalar(grp, grp, -MAGIC, None, ALU.add))
                s.then(dve.tensor_copy(grp_b, grp))
                s.then(dve.tensor_copy(iota_b[:, :], iota_i[:, 0:NT]))
                groups = grp_b.rearrange("p (k r) -> p k r", k=STREAMS)
                numbers = iota_b[:, :].unsqueeze(1).to_broadcast([T, STREAMS, NT])
                with dve.Fori(0, SC // 2) as i:
                    for h in range(2):
                        dve.wait_ge(hist_mm, 2 * i + h + 1)
                        dve.tensor_tensor(hot[h], groups[:, :, bass.ds(2 * i + h, 1)].to_broadcast([T, STREAMS, NT]),
                                          numbers, ALU.is_equal).then_inc(hist_hot, 1)
                dve.wait_ge(hist_mm, SC + 2)
                counts = banks[7][0:T, 0:STREAMS * NT].rearrange("p (k b) -> p k b", k=STREAMS)
                s.then(dve.tensor_copy(hist, counts))
                s.then(dve.tensor_reduce(total, hist.rearrange("p k b -> p b k"), AX.X, ALU.add))
                s.then(dve.tensor_scalar(chunks_i, total, float(P - 1), None, ALU.add))
                s.then(dve.tensor_scalar(chunks_i, chunks_i, 7, None, ALU.logical_shift_right))
                s.then(dve.tensor_copy(chunks_f, chunks_i))
                s.then(dve.memset(nothing, 0.0))
                s.then(dve.tensor_tensor_scan(cum, chunks_f, nothing, 0.0, ALU.add, ALU.add))
                s.then(dve.tensor_tensor(first, cum, chunks_f, ALU.subtract))
                s.then(dve.tensor_scalar(base[:, 0, :], first, float(P), None, ALU.mult))
                for k in range(1, STREAMS):
                    s.then(dve.tensor_tensor(base[:, k, :], base[:, k - 1, :], hist[:, k - 1, :], ALU.add))
                s.then(dve.tensor_copy(chunk_f, chunk_i))
                for q in range(CPP):
                    s.then(dve.tensor_scalar(ended[0:CPART], cum[0:CPART], chunk_f[:, q:q + 1], None, ALU.is_le))
                    s.then(dve.tensor_reduce(bin_f[:, q:q + 1], ended[0:CPART], AX.X, ALU.add))
                s.then(dve.tensor_scalar(bin_f, bin_f, float(NT - 1), float(D), ALU.min, ALU.mult))
                dve.tensor_copy(bin_i, bin_f).then_inc(base_made, 1)
                s.then(dve.tensor_scalar(grp, grp, -float(T), None, ALU.mult))
                s.then(dve.tensor_tensor(rec[:, :, 1], srcf, grp, ALU.add))
                s.then(dve.tensor_copy(rec[:, :, 0], dst_i))
                s.then(dve.tensor_copy(rec[:, :, 2], wgt))

            @block.tensor
            def _(pe):
                counts = banks[7][:, 0:STREAMS * NT]
                pe.sem_inc(hist_mm, 2)
                pe.wait_ge(pool_step, 12)
                pe.wait_ge(hist_hot, 1)
                pe.matmul(counts, zero_b[:, :], hot[0].rearrange("p k b -> p (k b)"), start=True, stop=False,
                          skip_group_check=True)
                with pe.Fori(0, SC // 2) as i:
                    for h in range(2):
                        pe.wait_ge(hist_hot, 2 * i + h + 1)
                        pe.matmul(counts, ones_b[:, :], hot[h].rearrange("p k b -> p (k b)"), start=False, stop=False,
                                  skip_group_check=True).then_inc(hist_mm, 1)

        ranks = banks[0][0:T, 0:STREAMS * NT]
        groups = grp_b.rearrange("p (k r) -> p k r", k=STREAMS)
        records = rec.rearrange("p (k r) w -> p k r w", k=STREAMS)

        def rank_hot(dve, r, h):
            dve.wait_ge(rank_next, r + 1)
            dve.tensor_tensor(hot[h], groups[:, :, bass.ds(r, 1)].to_broadcast([T, STREAMS, NT]),
                              iota_b[:, :].unsqueeze(1).to_broadcast([T, STREAMS, NT]), ALU.is_equal).then_inc(hot_made, 1)

        def rank_product(dve, r, u):
            dve.wait_ge(rank_ps, r + 1)
            dve.tensor_tensor(prod, ranks.rearrange("p (k b) -> p k b", k=STREAMS), hot[u % 2],
                              ALU.mult).then_inc(rank_read, 1)

        def rank_reduce(dve, r, u):
            dve.wait_ge(rank_read, r + 1)
            dve.tensor_reduce(slot_f[:, u * STREAMS:(u + 1) * STREAMS], prod, AX.X, ALU.add).then_inc(rank_step, 1)

        def rank_before(pe, r, h):
            pe.wait_ge(hot_made, r + 1)
            pe.matmul(ranks, before[:, :], hot[h].rearrange("p k b -> p (k b)"), start=False, stop=False,
                      skip_group_check=True).then_inc(rank_ps, 1)

        def rank_advance(pe, r, h):
            pe.wait_ge(rank_read, r + 1)
            pe.matmul(ranks, upto[:, :], hot[h].rearrange("p k b -> p (k b)"), start=False, stop=False,
                      skip_group_check=True).then_inc(rank_next, 1)

        def addresses(dve, turn, b, s):
            dve.wait_ge(rank_step, RANKS * turn + HALF * (b + 1))
            s.then(dve.tensor_copy(slot_i, slot_f))
            s.then(dve.tensor_scalar(slot_t, slot_i, P - 1, 4, ALU.bitwise_and, ALU.logical_shift_left))
            s.then(dve.scalar_tensor_tensor(slot_t, slot_i, -GROUP, slot_t, ALU.bitwise_and, ALU.bitwise_or))
            s.then(dve.tensor_scalar(slot_i, slot_i, 7, CH - 1, ALU.logical_shift_right, ALU.bitwise_and))
            dve.wait_ge(scattered[b], 16 * BATCH * turn + 16)
            dve.tensor_tensor(addr[b], slot_i, slot_t, ALU.bitwise_or).then_inc(addr_made, 1)

        def ring_records(act, turn, b):
            act.wait_ge(scattered[b], 16 * BATCH * turn + 16)
            act.sem_inc(gate, 1)
            act.copy(ring[b].rearrange("p (u k) w -> p k u w", u=HALF),
                     records[:, :, bass.ds(RANKS * turn + HALF * b, HALF), :]).then_inc(ring_made, 1)

        def scatter(pool, turn, b):
            pool.wait_ge(addr_made, 2 * turn + b + 1)
            pool.wait_ge(ring_made, 2 * turn + b + 1)
            pool.sem_inc(pool_go, 1)
            for c in range(BATCH):
                pool.indirect_dma_start(table_d, bass.IndirectOffsetOnAxis(addr[b][:, c:c + 1], 0), ring[b][:, c, :],
                                        None).then_inc(scattered[b], 16)

        kv_sum = [banks[1][:, 0:P + 1], banks[2][:, 0:P + 1]]

        with nc.Block() as block:
            @block.sync
            def _(sp):
                def turn(i, last=False):
                    for j in range(BODY):
                        sp.wait_ge(xn_made, BODY * i + j + 1)
                        sp.dma_start(xn_d[bass.ds((BODY * i + j) * T, T), :], xn[j]).then_inc(xn_stored[j], 16)
                        if not last:
                            sp.dma_start(xt[j], x[bass.ds((BODY * i + BODY + j) * T, T), :]).then_inc(x_in[j], 16)
                    for j in range(BODY):
                        t = BODY * i + j
                        sp.wait_ge(sup_read, t + 2)
                        sp.dma_start(support_d[bass.ds(t * T, T), :], sup[j % 2]).then_inc(stored[j], 16)
                        sp.wait_ge(qphi_made, t + 2)
                        sp.dma_start(q_d[bass.ds(t, 1)].rearrange("t p c -> (t p) c"), qphi[j % 2]).then_inc(stored[j], 16)

                for j in range(BODY):
                    sp.dma_start(xt[j], x[j * T:(j + 1) * T, :]).then_inc(x_in[j], 16)
                with sp.Fori(0, TURNS - 1) as i:
                    turn(i)
                turn(TURNS - 1, last=True)
                for j in range(BODY):
                    sp.wait_ge(stored[j], 32 * (TURNS + (j >= 2)))
                    sp.wait_ge(xn_stored[j], 16 * TURNS + 16)

            @block.gpsimd
            def _(pool):
                with pool.Fori(0, TURNS) as i:
                    for b in range(2):
                        scatter(pool, i, b)

            @block.tensor
            def _(pe):
                def turn_x(t, j):
                    pe.wait_ge(xn_made, t + 1)
                    for f in range(H2):
                        mm = pe.transpose(banks[3][:, f * T:(f + 1) * T], xn[j][:, f * P:(f + 1) * P], ident[0:T, 0:T])
                    mm.then_inc(xT_ps, 1)

                def turn(i, last=False):
                    for j in range(BODY):
                        t, r = BODY * i + j, RANKS * i + 2 * j
                        rows_T = [xnT[j % 2][:, f * T:(f + 1) * T] for f in range(H2)]
                        rank_before(pe, r, 0)
                        pe.wait_ge(xnT_made, t + 1)
                        pe.wait_ge(kv_read, t + 1)
                        for n, w in enumerate((wk, wv)):
                            for f in range(H2):
                                mm = pe.matmul(banks[5][0:T, n * D:(n + 1) * D], rows_T[f], w[:, f, :], start=f == 0,
                                               stop=f == H2 - 1)
                        mm.then_inc(kv_ps, 1)
                        for m in range(H2):
                            for f in range(H2):
                                mm = pe.matmul(banks[6][:, m * T:(m + 1) * T], wq[:, f, m * P:(m + 1) * P], rows_T[f],
                                               start=f == 0, stop=f == H2 - 1)
                        mm.then_inc(q_ps, 1)
                        if j < BODY - 1:
                            turn_x(t + 1, j + 1)
                        pe.wait_ge(sup_read, t + 1)
                        for f in range(H2):
                            mm = pe.matmul(banks[4][0:T, 0:D], rows_T[f], wg[:, f, :], start=f == 0, stop=f == H2 - 1)
                        mm.then_inc(sup_ps, 1)
                        rank_advance(pe, r, 0)
                        rank_before(pe, r + 1, 1)
                        pe.wait_ge(kphi_made, t + 2)
                        for f in range(H2):
                            mm = pe.matmul(kv_sum[f], kphi[:, f * P:(f + 1) * P], vt[:, f, :], start=False, stop=False,
                                           skip_group_check=True)
                        mm.then_inc(kv_added, 1)
                        if not last and j == BODY - 1:
                            turn_x(t + 1, 0)
                        rank_advance(pe, r + 1, 1)

                pe.matmul(ranks, ones_f[0:1, 0:T], base[0:1, :, :].rearrange("p k b -> p (k b)"), start=True,
                          stop=False, skip_group_check=True)
                for f in range(H2):
                    mm = pe.matmul(kv_sum[f], zero_b[:, :], hot[0].rearrange("p k b -> p (k b)")[:, 0:P + 1],
                                   start=True, stop=False, skip_group_check=True)
                mm.then_inc(sums_open, 1)
                turn_x(0, 0)
                with pe.Fori(0, TURNS - 1) as i:
                    turn(i)
                turn(TURNS - 1, last=True)

            @block.scalar
            def _(act):
                def copy_x(t, j):
                    act.wait_ge(xT_ps, t + 1)
                    act.copy(xnT[j % 2], banks[3][:, 0:H2 * T]).then_inc(xnT_made, 1)

                def turn(i, last=False):
                    for j in range(BODY):
                        t = BODY * i + j
                        act.wait_ge(kb_made, t + 1)
                        act.wait_ge(kphi_made, t + 1)
                        act.activation(ke, kb, ACT.Exp)
                        act.activation(kr, kb, ACT.Relu).then_inc(ke_made, 1)
                        act.wait_ge(q_ps, t + 1)
                        act.wait_ge(qphi_made, t + 1)
                        for m in range(H2):
                            act.activation(qe[:, m * T:(m + 1) * T], banks[6][:, m * T:(m + 1) * T], ACT.Exp,
                                           bias=bqc[:, m:m + 1])
                        for m in range(H2):
                            mm = act.activation(qr[:, m * T:(m + 1) * T], banks[6][:, m * T:(m + 1) * T], ACT.Relu,
                                                bias=bqc[:, m:m + 1])
                        mm.then_inc(qe_made, 1)
                        if j < BODY - 1:
                            copy_x(t + 1, j + 1)
                        act.wait_ge(stored[(j + 2) % BODY], 32 * i + 32)
                        act.wait_ge(sup_ps, t + 1)
                        act.copy(sup[j % 2], banks[4][0:T, 0:D]).then_inc(sup_read, 1)
                        if j % 2 == 0:
                            ring_records(act, i, j // 2)
                        if not last and j == BODY - 1:
                            copy_x(t + 1, 0)

                copy_x(0, 0)
                with act.Fori(0, TURNS - 1) as i:
                    turn(i)
                turn(TURNS - 1, last=True)

            @block.vector
            def _(dve):
                def row_moments(a, i, j):
                    dve.wait_ge(x_in[j], 16 * i + 16)
                    a.then(dve.bn_stats(stats6[:, j, :], xt[j]))
                    dve.sem_inc(gate, 1)
                    a.issue(dve.bn_aggr(mean_var[:, j, :], stats6[:, j, :]))

                def normalise_rows(a, i):
                    a.settle()
                    a.then(dve.tensor_scalar(var4, mean_var[:, :, 1], LN_EPS, None, ALU.add))
                    a.then(dve.tensor_scalar(t4.bitcast(I32), var4.bitcast(I32), 1, None, ALU.logical_shift_right))
                    a.then(dve.tensor_scalar(rstd4.bitcast(I32), t4.bitcast(I32), -1.0, float(0x5F3759DF), ALU.mult,
                                             ALU.add))
                    for _ in range(3):
                        a.then(dve.tensor_tensor(t4, rstd4, rstd4, ALU.mult))
                        a.then(dve.tensor_tensor(t4, t4, var4, ALU.mult))
                        a.then(dve.tensor_scalar(t4, t4, -0.5, 1.5, ALU.mult, ALU.add))
                        a.then(dve.tensor_tensor(rstd4, rstd4, t4, ALU.mult))
                    for j in range(BODY):
                        dve.wait_ge(xn_stored[j], 16 * i + 16)
                        dve.tensor_scalar(xn[j], xt[j], mean_var[:, j, 0:1], rstd4[:, j:j + 1], ALU.subtract,
                                          ALU.mult).then_inc(xn_made, 1)

                def turn(i, last=False):
                    a = Steps(dve, a_step, A_FRONT + A_STEPS * i)
                    for j in range(BODY):
                        t, r = BODY * i + j, RANKS * i + 2 * j
                        rank_hot(dve, r, 0)
                        dve.wait_ge(kv_ps, t + 1)
                        dve.tensor_tensor(kb, banks[5][0:T, 0:D], rows["bkr"][:, :], ALU.add).then_inc(kb_made, 1)
                        dve.wait_ge(kv_added, t + 1)
                        dve.tensor_tensor(vt[:, :, 0:P], banks[5][0:T, D:2 * D].rearrange("p (f c) -> p f c", f=H2),
                                          rows["bvr"][:, :].rearrange("p (f c) -> p f c", f=H2), ALU.add).then_inc(kv_read, 1)
                        rank_product(dve, r, 2 * j % HALF)
                        if not last:
                            row_moments(a, i + 1, j)
                        rank_reduce(dve, r, 2 * j % HALF)
                        rank_hot(dve, r + 1, 1)
                        dve.wait_ge(ke_made, t + 1)
                        dve.wait_ge(kv_read, t + 2)
                        dve.scalar_tensor_tensor(kphi, ke, 1.0, kr, ALU.min, ALU.add).then_inc(kphi_made, 1)
                        dve.wait_ge(qe_made, t + 1)
                        dve.wait_ge(stored[(j + 2) % BODY], 32 * i + 32)
                        dve.scalar_tensor_tensor(qphi[j % 2], qe, 1.0, qr, ALU.min, ALU.add).then_inc(qphi_made, 1)
                        if not last and j == BODY - 1:
                            dve.wait_ge(xT_ps, t + 1)
                            normalise_rows(a, i + 1)
                        rank_product(dve, r + 1, 2 * j % HALF + 1)
                        rank_reduce(dve, r + 1, 2 * j % HALF + 1)
                        if j % 2:
                            addresses(dve, i, j // 2, a)
                    assert last or a.n == A_STEPS, a.n

                dve.memset(vt[:, :, P:P + 1], 1.0)
                dve.wait_ge(sums_open, 1)
                a = Steps(dve, a_step)
                for j in range(BODY):
                    row_moments(a, 0, j)
                normalise_rows(a, 0)
                assert a.n == A_FRONT, a.n
                with dve.Fori(0, TURNS - 1) as i:
                    turn(i)
                turn(TURNS - 1, last=True)
                dve.wait_ge(kv_added, NT + 1)
                for f in range(H2):
                    for h in range(HPH):
                        q = slice(h * DH, (h + 1) * DH)
                        dve.tensor_copy(kvb[q, f, q], kv_sum[f][q, q]).then_inc(kvb_made, 1)
                        dve.tensor_copy(kvb[q, f, P + h:P + h + 1], kv_sum[f][q, P:P + 1]).then_inc(kvb_made, 1)

        with nc.Block() as block:
            @block.sync
            def _(sp):
                def load(i, j):
                    t = BODY * i + j
                    sp.wait_ge(mix_used, t + 1)
                    sp.dma_start(qT[j], q_d[bass.ds(t, 1)].rearrange("t p c -> (t p) c")).then_inc(mix_in[j], 16)
                    sp.dma_start(xr[j], xn_d[bass.ds(t * T, T), :]).then_inc(mix_in[j], 16)
                    sp.dma_start(xo[j], x[bass.ds(t * T, T), :]).then_inc(mix_in[j], 16)

                with sp.Fori(0, TURNS) as i:
                    for j in range(BODY):
                        load(i, j)

            @block.gpsimd
            def _(pool):
                with pool.Fori(TURNS, 2 * TURNS) as i:
                    for b in range(2):
                        scatter(pool, i, b)
                for b in range(2):
                    pool.wait_ge(scattered[b], 16 * BATCH * 2 * TURNS + 16)

            attn = banks[1][0:T, 0:H2 * KVW]

            @block.tensor
            def _(pe):
                def attend(i, j):
                    pe.wait_ge(mix_in[j], 48 * i + 48)
                    for f in range(H2):
                        mm = pe.matmul(attn[:, f * KVW:(f + 1) * KVW], qT[j][:, f * T:(f + 1) * T], kvb[:, f, :],
                                       start=True, stop=True)
                    mm.then_inc(at_ps, 1)

                def turn_attention(t):
                    pe.wait_ge(at_made, t + 1)
                    for f in range(H2):
                        mm = pe.transpose(banks[2][:, f * T:(f + 1) * T], at[:, f * P:(f + 1) * P], ident[0:T, 0:T])
                    mm.then_inc(atT_ps, 1)

                def project(t):
                    pe.wait_ge(atT_made, t + 1)
                    for f in range(H2):
                        mm = pe.matmul(banks[3][0:T, 0:D], atT[:, f * T:(f + 1) * T], wo[:, f, :], start=f == 0,
                                       stop=f == H2 - 1)
                    mm.then_inc(wo_ps, 1)

                def turn_x1(t, j):
                    pe.wait_ge(x1_made, t + 1)
                    for f in range(H2):
                        mm = pe.transpose(banks[4][:, f * T:(f + 1) * T], x1[j % 2][:, f * P:(f + 1) * P],
                                          ident[0:T, 0:T])
                    mm.then_inc(x1T_ps, 1)

                def widen(t, chunks):
                    for m in chunks:
                        for f in range(H2):
                            mm = pe.matmul(banks[5 + m // 4][:, m % 4 * T:(m % 4 + 1) * T], w1[:, f, m * P:(m + 1) * P],
                                           x1T[:, f * T:(f + 1) * T], start=f == 0, stop=f == H2 - 1)
                        if m % 4 == 3:
                            mm.then_inc(h_ps, 1)

                def narrow(t):
                    pe.wait_ge(h_made, t + 1)
                    pe.wait_ge(ff_read, t + 1)
                    for m in range(FC):
                        mm = pe.matmul(banks[7][0:T, 0:D], hT[:, m, :], w2[:, m, :], start=m == 0, stop=m == FC - 1)
                    mm.then_inc(ff_ps, 1)

                def turn(i, last=False):
                    for j in range(BODY):
                        t, r = BODY * i + j, RANKS * (i + TURNS) + 2 * j
                        front = not (last and j == BODY - 1)
                        n = (i, j + 1) if j < BODY - 1 else (i + 1, 0)
                        rank_before(pe, r, 0)
                        if front:
                            attend(*n)
                        pe.wait_ge(x1T_made, t + 1)
                        widen(t, range(0, 4))
                        if front:
                            turn_attention(t + 1)
                        widen(t, range(4, 6))
                        if front:
                            project(t + 1)
                        rank_advance(pe, r, 0)
                        widen(t, range(6, 8))
                        rank_before(pe, r + 1, 1)
                        narrow(t)
                        rank_advance(pe, r + 1, 1)
                        if front:
                            turn_x1(t + 1, j + 1)

                pe.wait_ge(kvb_made, 4 * HPH)
                attend(0, 0)
                turn_attention(0)
                project(0)
                turn_x1(0, 0)
                with pe.Fori(0, TURNS - 1) as i:
                    turn(i)
                turn(TURNS - 1, last=True)

            @block.scalar
            def _(act):
                def copies(t):
                    act.wait_ge(atT_ps, t + 1)
                    act.copy(atT, banks[2][:, 0:H2 * T]).then_inc(atT_made, 1)

                def hidden(t, c):
                    act.wait_ge(h_ps, 2 * t + c + 1)
                    for m in range(c * FC // 2, (c + 1) * FC // 2):
                        mm = act.activation(hT[:, m, :], banks[5 + c][:, m % 4 * T:(m % 4 + 1) * T], ACT.Relu,
                                            bias=b1c[:, m:m + 1])
                    if c:
                        mm.then_inc(h_made, 1)

                def x1_copy(t):
                    act.wait_ge(x1T_ps, t + 1)
                    act.copy(x1T, banks[4][:, 0:H2 * T]).then_inc(x1T_made, 1)

                def turn(i, first=False, last=False):
                    for j in range(BODY):
                        t = BODY * i + j
                        front = not (last and j == BODY - 1)
                        if j % 2 == 0:
                            ring_records(act, i + TURNS, j // 2)
                        if not (first and j == 0):
                            deviation(t - 1, var2_made, std2_made, ln2)
                        hidden(t, 0)
                        if front:
                            copies(t + 1)
                        hidden(t, 1)
                        if front:
                            deviation(t + 1, var1_made, std1_made, ln)
                            x1_copy(t + 1)

                def deviation(t, variance, made, stats):
                    act.wait_ge(variance, t + 1)
                    act.activation(stats[:, 9:10], stats[:, 7:8], ACT.Sqrt, bias=eps[:, 0:1]).then_inc(made, 1)

                copies(0)
                deviation(0, var1_made, std1_made, ln)
                x1_copy(0)
                turn(0, first=True)
                with act.Fori(1, TURNS - 1) as i:
                    turn(i)
                turn(TURNS - 1, last=True)
                deviation(NT - 1, var2_made, std2_made, ln2)

            @block.vector
            def _(dve):
                def normalise(b, i, j):
                    t = BODY * i + j
                    dve.wait_ge(at_ps, t + 1)
                    halves = attn.rearrange("p (f c) -> p f c", f=H2)
                    b.then(dve.tensor_scalar(zr, halves[:, :, P:KVW], 1e-6, None, ALU.add))
                    b.then(dve.reciprocal(zr, zr))
                    for f in range(H2):
                        mm = dve.tensor_tensor(at[:, f * P:(f + 1) * P].rearrange("p (h e) -> p h e", h=HPH),
                                               halves[:, f, 0:P].rearrange("p (h e) -> p h e", h=HPH),
                                               zr[:, f, :].unsqueeze(2).to_broadcast([T, HPH, DH]), ALU.mult)
                    mm.then_inc(at_made, 1)

                def first_norm(b, i, j, between=None):
                    t = BODY * i + j
                    b.settle()
                    dve.wait_ge(wo_ps, t + 1)
                    b.then(dve.tensor_tensor(r1, banks[3][0:T, 0:D], xr[j], ALU.add))
                    moments(b, dve, r1, ln)
                    dve.sem_inc(var1_made, 1)
                    if between:
                        between()
                    dve.wait_ge(std1_made, t + 1)
                    b.then(dve.reciprocal(ln[:, 8:9], ln[:, 9:10]))
                    b.then(dve.tensor_scalar(r1, r1, ln[:, 6:7], ln[:, 8:9], ALU.subtract, ALU.mult))
                    b.then(dve.tensor_tensor(r1, r1, rows["g1r"][:, :], ALU.mult))
                    b.then(dve.tensor_tensor(x1[j % 2], r1, rows["be1r"][:, :], ALU.add))
                    dve.sem_inc(x1_made, 1)

                def second_moments(b, t, j):
                    dve.wait_ge(x1T_ps, t + 1)
                    b.issue(dve.tensor_tensor(x1[j % 2], x1[j % 2], rows["b2r"][:, :], ALU.add))
                    b.then(dve.tensor_tensor(xo[j], xo[j], rows["be2r"][:, :], ALU.add))
                    dve.wait_ge(ff_ps, t + 1)
                    dve.tensor_tensor(r2, banks[7][0:T, 0:D], x1[j % 2], ALU.add).then_inc(ff_read, 1)
                    dve.wait_ge(ff_read, t + 2)
                    moments(b, dve, r2, ln2)
                    dve.sem_inc(var2_made, 1)

                def second_norm(b, t, j):
                    dve.wait_ge(std2_made, t + 1)
                    b.then(dve.reciprocal(ln2[:, 8:9], ln2[:, 9:10]))
                    b.then(dve.tensor_scalar(r2, r2, ln2[:, 6:7], ln2[:, 8:9], ALU.subtract, ALU.mult))
                    b.then(dve.tensor_tensor(r2, r2, rows["g2r"][:, :], ALU.mult))
                    b.then(dve.tensor_tensor(acc_flat[:, bass.ds(t * D, D)], r2, xo[j], ALU.add))
                    dve.sem_inc(mix_used, 1)

                def turn(i, first=False, last=False):
                    b = Steps(dve, b_step, B_FRONT + B_STEPS * i - (0 if first else B_BACK))
                    for j in range(BODY):
                        t, r = BODY * i + j, RANKS * (i + TURNS) + 2 * j
                        front = not (last and j == BODY - 1)
                        back = not (first and j == 0)
                        n = (i, j + 1) if j < BODY - 1 else (i + 1, 0)
                        rank_hot(dve, r, 0)
                        if back:
                            second_moments(b, t - 1, (j - 1) % BODY)
                        if front:
                            normalise(b, *n)
                        rank_product(dve, r, 2 * j % HALF)
                        if front:
                            b.issue(dve.tensor_tensor(xr[n[1]], xr[n[1]], rows["bor"][:, :], ALU.add))
                        rank_reduce(dve, r, 2 * j % HALF)
                        if back:
                            second_norm(b, t - 1, (j - 1) % BODY)
                        rank_hot(dve, r + 1, 1)
                        if front:
                            first_norm(b, *n, between=lambda: rank_product(dve, r + 1, 2 * j % HALF + 1))
                        else:
                            rank_product(dve, r + 1, 2 * j % HALF + 1)
                        rank_reduce(dve, r + 1, 2 * j % HALF + 1)
                        if j % 2:
                            addresses(dve, i + TURNS, j // 2, b)
                    assert last or b.n == B_STEPS - B_BACK * first, b.n
                    return b

                b = Steps(dve, b_step)
                normalise(b, 0, 0)
                b.then(dve.tensor_tensor(xr[0], xr[0], rows["bor"][:, :], ALU.add))
                first_norm(b, 0, 0)
                assert b.n == B_FRONT, b.n
                turn(0, first=True)
                with dve.Fori(1, TURNS - 1) as i:
                    turn(i)
                b = turn(TURNS - 1, last=True)
                second_moments(b, NT - 1, (NT - 1) % BODY)
                second_norm(b, NT - 1, (NT - 1) % BODY)

        products = [banks[b][0:T, :] for b in range(AHEAD)]
        with nc.Block() as block:
            @block.sync
            def _(sp):
                sp.dma_start(binof, binof_d.rearrange("(a c) -> a c", a=1)).then_inc(bins_in, 16)
                table_groups = table_d.rearrange("(g p c) w -> g p (c w)", p=P, c=CH)

                def load(g, h):
                    sp.dma_start(recs[h].rearrange("p c w -> p (c w)"),
                                 table_groups[bass.ds(g, 1)].rearrange("g p c -> (g p) c")).then_inc(recs_in[h], 16)

                load(0, 0)
                load(1, 1)
                with sp.Fori(0, GROUPS // 2) as i:
                    for h in range(2):
                        sp.wait_ge(recs_used, 2 * i + h + 1)
                        load(2 * i + h + 2, h)
                for h in range(2):
                    sp.wait_ge(recs_in[h], 16 * (GROUPS // 2 + 1))

            @block.gpsimd
            def _(pool):
                with pool.Fori(0, GROUPS // 2) as i:
                    for h in range(2):
                        for q in range(4):
                            if q == 0:
                                pool.wait_ge(gidx_made, 2 * i + h + 1)
                            pool.wait_ge(pair_ps, PAIRS * (2 * i + h) + 2 * q + 2)
                            pool.sem_inc(pool_go, 1)
                            for c in range(4 * q, 4 * q + 4):
                                pool.indirect_dma_start(rowbuf[h][c], None, support_d,
                                                        bass.IndirectOffsetOnAxis(gidx[h][:, c:c + 1], 0)
                                                        ).then_inc(landed[4 * h + q], 16)

            @block.tensor
            def _(pe):
                with pe.Fori(0, GROUPS // 2) as i:
                    for h in range(2):
                        g = 2 * i + h
                        for p in range(PAIRS):
                            if p % 2 == 0:
                                pe.wait_ge(landed[4 * h + p // 2], 64 * i + 64)
                            pe.wait_ge(onehot_made, PAIRS * g + p + 1)
                            pe.wait_ge(acc_step, CH * g + 2 * p + 2)
                            for c in range(2):
                                mm = pe.matmul(products[p % AHEAD][:, c * D:(c + 1) * D], onehot[p % AHEAD][:, c, :],
                                               rowbuf[h][2 * p + c], start=True, stop=True)
                            mm.then_inc(pair_ps, 1)

            @block.vector
            def _(dve):
                def select(h, p, c):
                    mm = dve.tensor_scalar(onehot[p % AHEAD][:, c, :], iota_n[:, :], recs[h][:, 2 * p + c, 1:2],
                                           recs[h][:, 2 * p + c, 2:3], ALU.is_equal, ALU.mult)
                    if c:
                        mm.then_inc(onehot_made, 1)

                column_regs = [dve.alloc_register(f"column{c}") for c in range(CH)]
                dve.wait_ge(bins_in, 16)
                dve.wait_ge(recs_in[0], 16)
                dve.tensor_copy(gidx[0], recs[0][:, :, 0]).then_inc(gidx_made, 1)
                for p in range(2):
                    for c in range(2):
                        select(0, p, c)
                with dve.Fori(0, GROUPS // 2) as i:
                    for h in range(2):
                        g = 2 * i + h
                        dve.load(column_regs, binof[0:1, bass.ds(CH * g, CH)])
                        columns = [dve.snap(c, min_val=0, max_val=(NT - 1) * D) for c in column_regs]
                        dve.wait_ge(recs_in[1 - h], 16 * i + 16 + 16 * h)
                        dve.tensor_copy(gidx[1 - h], recs[1 - h][:, :, 0]).then_inc(gidx_made, 1)
                        for p in range(PAIRS):
                            if p == PAIRS - 2:
                                dve.wait_ge(onehot_made, PAIRS * (g + 1))
                                dve.sem_inc(recs_used, 1)
                            dve.wait_ge(pair_ps, PAIRS * (g + 2) + p + 1)
                            for c in range(2):
                                a = acc_flat[:, bass.ds(columns[2 * p + c], D)]
                                dve.wait_ge(acc_step, CH * g + 2 * p + c + 8)
                                dve.tensor_tensor(a, products[p % AHEAD][:, c * D:(c + 1) * D], a, ALU.add).then_inc(acc_step, 1)
                                if p < PAIRS - 2:
                                    select(h, p + 2, c)
                                else:
                                    select(1 - h, p + 2 - PAIRS, c)

        with nc.Block() as block:
            @block.sync
            def _(sp):
                with sp.Fori(0, NT // 2) as i:
                    for h in range(2):
                        sp.wait_ge(res_made, 2 * i + h + 1)
                        sp.dma_start(out[bass.ds((2 * i + h) * T, T), :], res[h]).then_inc(out_stored[h], 16)
                for h in range(2):
                    sp.wait_ge(out_stored[h], 16 * (NT // 2) + 16)

            @block.gpsimd
            def _(pool):
                with pool.Fori(0, NT) as t:
                    pool.wait_ge(var_made, t + 1)
                    pool.tensor_tensor(lne[:, 8:9], lne[:, 9:10], eps[:, 1:2], ALU.pow).then_inc(rstd_made, 1)

            @block.tensor
            def _(pe):
                def turn_y(t, h):
                    pe.wait_ge(yn_made, t + 1)
                    for f in range(H2):
                        mm = pe.transpose(banks[0][:, f * T:(f + 1) * T], yn[h][:, f * P:(f + 1) * P], ident[0:T, 0:T])
                    mm.then_inc(yT_ps, 1)

                def first(t):
                    pe.wait_ge(yT_made, t + 1)
                    pe.wait_ge(gate_read, t + 1)
                    for f in range(H2):
                        pe.matmul(banks[1][0:T, 0:NE], yT[:, f * T:(f + 1) * T], gw[:, f, :], start=f == 0,
                                  stop=f == H2 - 1)
                    for m in range(H2):
                        for f in range(H2):
                            pe.matmul(banks[2][:, m * T:(m + 1) * T], sw1[:, f, m * P:(m + 1) * P],
                                      yT[:, f * T:(f + 1) * T], start=f == 0, stop=f == H2 - 1)
                    for e in range(NE):
                        for f in range(H2):
                            mm = pe.matmul(banks[3][:, e * T:(e + 1) * T], ew1[:, f, e, :], yT[:, f * T:(f + 1) * T],
                                           start=f == 0, stop=f == H2 - 1)
                    mm.then_inc(l1_ps, 1)

                def second(t):
                    pe.wait_ge(l1_made, t + 1)
                    for m in range(H2):
                        pe.matmul(banks[2][:, H2 * T:(H2 + 1) * T], sw2[:, m, :], s1T[:, m, :], start=m == 0,
                                  stop=m == H2 - 1)
                    for e in range(NE):
                        mm = pe.matmul(banks[4][0:EH2, e * T:(e + 1) * T], ew2[:, e, :], e1T[:, e, :], start=True,
                                       stop=True)
                    mm.then_inc(l2_ps, 1)

                def third(t):
                    pe.wait_ge(l2_made, t + 1)
                    pe.wait_ge(l3_read, t + 1)
                    pe.matmul(banks[5][0:T, 0:D], s2T, sw3[:, :], start=True, stop=True)
                    for e in range(NE):
                        mm = pe.matmul(banks[6 + e // 2][0:T, e % 2 * D:(e % 2 + 1) * D], e2T[:, e, :], ew3[:, e, :],
                                       start=True, stop=True)
                    mm.then_inc(l3_ps, 1)

                turn_y(0, 0)
                first(0)
                second(0)
                turn_y(1, 1)
                with pe.Fori(0, NT // 2 - 1) as i:
                    for h in range(2):
                        t = 2 * i + h + 1
                        first(t)
                        third(t - 1)
                        second(t)
                        turn_y(t + 1, h)
                first(NT - 1)
                third(NT - 2)
                second(NT - 1)
                third(NT - 1)

            @block.scalar
            def _(act):
                def copy_y(t):
                    act.wait_ge(yT_ps, t + 1)
                    act.copy(yT, banks[0][:, 0:H2 * T]).then_inc(yT_made, 1)

                def hidden(t):
                    act.wait_ge(l1_ps, t + 1)
                    for m in range(H2):
                        act.activation(s1T[:, m, :], banks[2][:, m * T:(m + 1) * T], ACT.Relu, bias=sb1c[:, m:m + 1])
                    for e in range(NE):
                        mm = act.activation(e1T[:, e, :], banks[3][:, e * T:(e + 1) * T], ACT.Relu, bias=eb1c[:, e:e + 1])
                    mm.then_inc(l1_made, 1)
                    act.wait_ge(gexp_go, 2 * t + 1)
                    act.activation(soft, soft, ACT.Exp).then_inc(gexp_made, 1)
                    act.wait_ge(l2_ps, t + 1)
                    act.activation(s2T, banks[2][:, H2 * T:(H2 + 1) * T], ACT.Relu, bias=sb2c[:, 0:1])
                    for e in range(NE):
                        mm = act.activation(e2T[0:EH2, e, :], banks[4][0:EH2, e * T:(e + 1) * T], ACT.Relu,
                                            bias=eb2c[:, e:e + 1])
                    mm.then_inc(l2_made, 1)
                    act.wait_ge(gexp_go, 2 * t + 2)
                    act.activation(soft, soft, ACT.Exp).then_inc(gexp_made, 1)

                copy_y(0)
                hidden(0)
                with act.Fori(0, NT // 2 - 1) as i:
                    for h in range(2):
                        copy_y(2 * i + h + 1)
                        hidden(2 * i + h + 1)
                copy_y(NT - 1)
                hidden(NT - 1)

            @block.vector
            def _(dve):
                def norm(e, t, h):
                    row = acc_flat[:, bass.ds(t * D, D)]
                    moments(e, dve, row, lne)
                    dve.tensor_scalar(lne[:, 9:10], lne[:, 7:8], LN_EPS, None, ALU.add).then_inc(var_made, 1)
                    dve.wait_ge(rstd_made, t + 1)
                    dve.tensor_scalar(yn[h], row, lne[:, 6:7], lne[:, 8:9], ALU.subtract, ALU.mult).then_inc(yn_made, 1)
                    dve.wait_ge(yn_made, t + 1)

                def route(e, t, h):
                    dve.wait_ge(l1_ps, t + 1)
                    dve.tensor_tensor(logit, banks[1][0:T, 0:NE], gbr[:, :], ALU.add).then_inc(gate_read, 1)
                    dve.wait_ge(gate_read, t + 2)
                    e.then(dve.tensor_reduce(gstat[:, 0:1], logit, AX.X, ALU.max))
                    dve.tensor_scalar(soft, logit, gstat[:, 0:1], None, ALU.subtract).then_inc(gexp_go, 1)
                    dve.wait_ge(gexp_made, 2 * t + 1)
                    e.then(dve.tensor_reduce(gstat[:, 1:2], soft, AX.X, ALU.add))
                    e.then(dve.reciprocal(gstat[:, 2:3], gstat[:, 1:2]))
                    e.then(dve.tensor_scalar(logit, soft, gstat[:, 2:3], None, ALU.mult))
                    mine = logit.unsqueeze(2).to_broadcast([T, NE, NE])
                    others = logit.unsqueeze(1).to_broadcast([T, NE, NE])
                    e.then(dve.tensor_tensor(beats, others, mine, ALU.is_gt))
                    e.then(dve.tensor_tensor(ties, others, mine, ALU.is_equal))
                    e.then(dve.tensor_tensor(ties, ties, tiebreak[:, :, :], ALU.mult))
                    e.then(dve.tensor_tensor(beats, beats, ties, ALU.add))
                    e.then(dve.tensor_reduce(rank4, beats, AX.X, ALU.add))
                    e.then(dve.tensor_scalar(chosen, rank4, 1.5, None, ALU.is_lt))
                    e.then(dve.tensor_reduce(gstat[:, 0:1], logit, AX.X, ALU.max))
                    dve.tensor_scalar(soft, logit, gstat[:, 0:1], None, ALU.subtract).then_inc(gexp_go, 1)
                    dve.wait_ge(gexp_made, 2 * t + 2)
                    e.then(dve.tensor_tensor(soft, soft, chosen, ALU.mult))
                    e.then(dve.tensor_reduce(gstat[:, 1:2], soft, AX.X, ALU.add))
                    e.then(dve.reciprocal(gstat[:, 2:3], gstat[:, 1:2]))
                    e.then(dve.tensor_scalar(gwt[h], soft, gstat[:, 2:3], None, ALU.mult))

                def combine(e, t, h, use):
                    dve.wait_ge(l3_ps, t + 1)
                    dve.wait_ge(out_stored[h], use)
                    e.then(dve.tensor_tensor(res[h], banks[5][0:T, 0:D], acc_flat[:, bass.ds(t * D, D)], ALU.add))
                    e.then(dve.tensor_tensor(res[h], res[h], rows["sb3r"][:, :], ALU.add))
                    for n in range(NE):
                        e.then(dve.scalar_tensor_tensor(res[h], banks[6 + n // 2][0:T, n % 2 * D:(n % 2 + 1) * D],
                                                        gwt[h][:, n:n + 1], res[h], ALU.mult, ALU.add))
                    dve.sem_inc(l3_read, 1)
                    dve.sem_inc(res_made, 1)

                e = Steps(dve, e_step)
                e.then(dve.memset(e2T[EH2:EH2 + 1, :, :], 1.0))
                norm(e, 0, 0)
                norm(e, 1, 1)
                route(e, 0, 0)
                assert e.n == E_FRONT, e.n
                with dve.Fori(0, NT // 2 - 1) as i:
                    e = Steps(dve, e_step, E_FRONT + E_STEPS * i)
                    for h in range(2):
                        t = 2 * i + h + 1
                        norm(e, t + 1, h)
                        route(e, t, 1 - h)
                        combine(e, t - 1, h, 16 * i + 16)
                    assert e.n == E_STEPS, e.n
                e = Steps(dve, e_step, E_FRONT + E_STEPS * (NT // 2 - 1))
                route(e, NT - 1, 1)
                combine(e, NT - 2, 0, 16 * (NT // 2))
                combine(e, NT - 1, 1, 16 * (NT // 2))


_INS = ["x", "src", "dst", "edge_weight", "L0_gnn_weight", "L0_mix_Wq", "L0_mix_bq", "L0_mix_Wk", "L0_mix_bk",
        "L0_mix_Wv", "L0_mix_bv", "L0_mix_Wo", "L0_mix_bo", "L0_mix_W1", "L0_mix_b1", "L0_mix_W2", "L0_mix_b2",
        "L0_mix_ln1_g", "L0_mix_ln1_b", "L0_mix_ln2_g", "L0_mix_ln2_b", "L0_ffn_sW1", "L0_ffn_sb1", "L0_ffn_sW2",
        "L0_ffn_sb2", "L0_ffn_sW3", "L0_ffn_sb3", "L0_ffn_eW1", "L0_ffn_eb1", "L0_ffn_eW2", "L0_ffn_eb2",
        "L0_ffn_eW3", "L0_ffn_eb3", "L0_ffn_gW", "L0_ffn_gb"]
_OUTS = [((N, D), "float32")]


def kernel(**inputs):
    import numpy as _np
    import concourse.bacc as _bacc
    from concourse import mybir as _mybir
    from concourse.bass_utils import run_bass_kernel_spmd as _run

    nc = _bacc.Bacc("TRN2", target_bir_lowering=False, num_devices=1)
    arrays, args = {}, []
    for name in _INS:
        a = _np.ascontiguousarray(inputs[name])
        arrays[f"in_{name}_dram"] = a
        args.append(nc.dram_tensor(f"in_{name}_dram", a.shape, _mybir.dt.from_np(a.dtype), kind="ExternalInput").ap())
    for i, (shape, dtype) in enumerate(_OUTS):
        dt = _mybir.dt.from_np(_np.dtype(dtype))
        args.append(nc.dram_tensor(f"out_{i}_dram", shape, dt, kind="ExternalOutput").ap())
    build(nc, *args)
    r = _run(nc, [arrays], core_ids=[0])
    return r.results[0]["out_0_dram"]
```

```python
from contextlib import ExitStack

import concourse.bass as bass
from concourse import mybir

ALU = mybir.AluOpType
ACT = mybir.ActivationFunctionType
AX = mybir.AxisListType
F32, BF16, I32 = mybir.dt.float32, mybir.dt.bfloat16, mybir.dt.int32

N, D, E = 12500, 256, 200000
T = 125
NT = N // T
P = 128
H2 = D // P
HEADS, DH = 8, 32
HPH = P // DH
RW = 3
FF = 1024
FC = FF // P
NE, EH2 = 4, 64
COLS = E // T
STREAMS = 4
SC = COLS // STREAMS
DIGIT = 10
WIDE = 8
BODY = 4
TURNS = NT // BODY
RANKS = SC // (2 * TURNS)
HALF = RANKS // 2
BATCH = HALF * STREAMS
CH = 16
GROUPS = -(-((E + NT * (P - 1)) // P) // (2 * CH)) * 2
CHUNKS = GROUPS * CH
CPP = 16
CPART = CHUNKS // CPP
GROUP = CH * P
SLOTS = (GROUPS + 2) * GROUP
assert DIGIT * DIGIT == NT and SC % (2 * WIDE) == 0
assert RANKS * 2 * TURNS == SC and SC * STREAMS == COLS and COLS * T == E and CPP * CPART == CHUNKS and CPART <= T
ZEROS = GROUP * RW // 2
LN_EPS = 1e-5
A_STEPS, A_FRONT, B_STEPS, B_FRONT, B_BACK, G_FRONT, G_STEPS, G_TOTAL, R_STEPS = 31, 23, 80, 10, 8, 10, 46, 2301, 46
LAG = GROUPS - NT
NORM_LAG, COMBINE_LAG = LAG + 1, LAG + 2
assert LAG >= 2 and LAG % 2 == 0
KVW = P + HPH


class Steps:

    def __init__(self, engine, sem, base=0):
        self.engine, self.sem, self.base, self.n = engine, sem, base, 0

    def issue(self, instruction):
        self.n += 1
        instruction.then_inc(self.sem, 1)

    def settle(self):
        self.engine.wait_ge(self.sem, self.base + self.n)

    def then(self, instruction):
        self.issue(instruction)
        self.settle()


def build(nc, x, src, dst, edge_weight, Wg, Wq, bq, Wk, bk, Wv, bv, Wo, bo, W1, b1, W2, b2, g1, be1, g2, be2,
          sW1, sb1, sW2, sb2, sW3, sb3, eW1, eb1, eW2, eb2, eW3, eb3, gW, gb, out):
    ctx = ExitStack()
    with ctx:
        def sb(name, shape, dt=F32):
            return ctx.enter_context(nc.sbuf_tensor(name, shape, dt))

        def sem(name):
            return ctx.enter_context(nc.semaphore(name))

        def sems(name, n):
            return [sem(f"{name}{i}") for i in range(n)]

        banks = [ctx.enter_context(nc.psum_tensor(f"bank{i}", [P, 512], F32)) for i in range(8)]

        support_d = nc.dram_tensor("support_rows", [N, D], F32, kind="Internal").ap()
        xn_d = nc.dram_tensor("xn_rows", [N, D], F32, kind="Internal").ap()
        q_d = nc.dram_tensor("q_phi", [NT, P, H2 * T], F32, kind="Internal").ap()
        table_d = nc.dram_tensor("edge_table", [SLOTS, RW], F32, kind="Internal").ap()
        hist_d = nc.dram_tensor("group_counts", [STREAMS, DIGIT, DIGIT], F32, kind="Internal").ap()
        binof_d = nc.dram_tensor("chunk_offsets", [CHUNKS], I32, kind="Internal").ap()

        wg = sb("wg", [P, H2, D])
        wq, wk, wv, wo = (sb(n, [P, H2, D]) for n in ("wq", "wk", "wv", "wo"))
        w1 = sb("w1", [P, H2, FF])
        w2 = sb("w2", [P, FC, D])
        sw1 = sb("sw1", [P, H2, D])
        sw2 = sb("sw2", [P, H2, P])
        sw3 = sb("sw3", [P, D])
        ew1 = sb("ew1", [P, H2, NE, P])
        ew2 = sb("ew2", [P, NE, EH2])
        ew3 = sb("ew3", [EH2 + 1, NE, D])
        gw = sb("gw", [P, H2, NE])
        bqc, b1c = sb("bqc", [P, H2]), sb("b1c", [P, FC])
        sb1c, sb2c = sb("sb1c", [P, H2]), sb("sb2c", [P, 1])
        eb1c, eb2c = sb("eb1c", [P, NE]), sb("eb2c", [EH2, NE])
        rows = {n: sb(n, [T, D]) for n in ("bkr", "bvr", "bor", "g1r", "be1r", "b2r", "g2r", "be2r", "sb3r")}
        gbr = sb("gbr", [T, NE])
        ident = sb("ident", [P, P])
        iota_n = sb("iota_n", [P, T])
        ones_b = sb("ones_b", [T, P], BF16)
        before = sb("before", [T, T], BF16)
        upto = sb("upto", [T, T], BF16)
        iota_b = sb("iota_b", [T, NT], BF16)
        tiebreak = sb("tiebreak", [T, NE, NE])
        kvb = sb("kvb", [P, H2, KVW])
        late_i = sb("late", [T, 1], I32)
        base = sb("base", [T, STREAMS, NT])
        ones_f = sb("ones_f", [1, P])
        zero_b = sb("zero_b", [T, P], BF16)
        eps = sb("eps", [T, 2])
        acc = sb("acc", [T, NT, D])

        PAIRS = CH // 2
        AHEAD = 4
        SLOTS_PS = 8

        WORK = 54 * 1024 // 4
        work = sb("work", [P, WORK])
        acc_flat = acc[:, :, :].rearrange("p a b -> p (a b)")
        top = [0]

        def carve(shape, dt=F32, memory=work):
            words = 1
            for s in shape[1:]:
                words *= s
            words = words if dt != BF16 else -(-words // 2)
            a = memory[0:shape[0], top[0]:top[0] + words]
            top[0] += words
            assert top[0] <= memory.shape[1], top[0]
            if dt != F32:
                a = a.bitcast(dt)
            if len(shape) > 2:
                names = "abcd"[:len(shape) - 1]
                a = a.rearrange(f"p ({' '.join(names)}) -> p {' '.join(names)}",
                                **{k: s for k, s in zip(names, shape[1:])})
            return a

        src_i, dst_i = (carve([T, COLS], I32, acc_flat) for _ in range(2))
        wgt, grp, srcf = (carve([T, COLS], F32, acc_flat) for _ in range(3))
        iota_i = carve([T, P], I32, acc_flat)
        zeros = carve([GROUPS + 2, ZEROS], F32, acc_flat)
        hist = carve([T, STREAMS, NT], F32, acc_flat)
        counts = carve([STREAMS * DIGIT, STREAMS * DIGIT], F32, acc_flat)
        tens = carve([T, COLS], F32, acc_flat)
        digits = [carve([T, COLS], BF16, acc_flat) for _ in range(2)]
        digit_hot = [[carve([T, WIDE, STREAMS, DIGIT], BF16, acc_flat) for _ in range(2)] for _ in range(2)]
        total, chunks_f, nothing, first, cum, ended = (carve([T, NT], F32, acc_flat) for _ in range(6))
        chunks_i = carve([T, NT], I32, acc_flat)
        chunk_i, bin_i = (carve([CPART, CPP], I32, acc_flat) for _ in range(2))
        chunk_f, bin_f = (carve([CPART, CPP], F32, acc_flat) for _ in range(2))
        top[0] = 0
        rec = carve([T, COLS, RW])
        grp_b = carve([T, COLS], BF16)
        hot = [carve([T, STREAMS, NT], BF16) for _ in range(2)]
        prod = carve([T, STREAMS, NT])
        slot_f = carve([T, BATCH])
        slot_i, slot_t = carve([T, BATCH], I32), carve([T, BATCH], I32)
        addr = [carve([T, BATCH], I32) for _ in range(2)]
        ring = [carve([T, BATCH, RW]) for _ in range(2)]
        ln, ln2 = carve([T, 16]), carve([T, 16])
        spread_top = top[0]
        qT = [carve([P, H2 * T]) for _ in range(BODY)]
        xr = [carve([T, D]) for _ in range(BODY)]
        xo = [carve([T, D]) for _ in range(BODY)]
        zr = carve([T, H2, HPH])
        at = carve([T, D])
        atT, x1T = carve([P, H2 * T]), carve([P, H2 * T])
        r1 = carve([T, D])
        x1 = [carve([T, D]) for _ in range(2)]
        r2 = carve([T, D])
        hT = carve([P, FC, T])
        top[0] = spread_top
        qe, qr = (carve([P, H2 * T]) for _ in range(2))
        xnT = [carve([P, H2 * T]) for _ in range(2)]
        qphi = [carve([P, H2 * T]) for _ in range(2)]
        top[0] = 0
        xt, xn = ([carve([T, D], F32, acc_flat) for _ in range(BODY)] for _ in range(2))
        sup = [carve([T, D], F32, acc_flat) for _ in range(2)]
        stats6, mean_var = carve([T, BODY, 6], F32, acc_flat), carve([T, BODY, 2], F32, acc_flat)
        var4, rstd4, t4 = (carve([T, BODY], F32, acc_flat) for _ in range(3))
        kb, ke, kr, kphi = (carve([T, D], F32, acc_flat) for _ in range(4))
        vt = carve([T, H2, P + 1], F32, acc_flat)
        top[0] = 0
        rowbuf = [[carve([P, D]) for _ in range(CH)] for _ in range(2)]
        onehot = [carve([P, 2, T]) for _ in range(AHEAD)]
        recs = [carve([P, CH, RW]) for _ in range(2)]
        gidx = [carve([P, CH], I32) for _ in range(2)]
        binof = carve([1, CHUNKS], I32)
        yn = carve([T, D])
        s2T = carve([P, T])
        lne = [carve([T, 16]) for _ in range(2)]
        logit, soft, chosen, rank4 = (carve([T, NE]) for _ in range(4))
        beats, ties = carve([T, NE, NE]), carve([T, NE, NE])
        gstat = carve([T, 4])
        gwt = [carve([T, NE]) for _ in range(2)]
        top[0] = 0
        w1_flat = w1[:, :, :].rearrange("p a b -> p (a b)")
        res = [carve([T, D], F32, w1_flat) for _ in range(2)]
        yT = carve([P, H2 * T], F32, w1_flat)
        s1T, e1T = carve([P, H2, T], F32, w1_flat), carve([P, NE, T], F32, w1_flat)
        e2T = carve([EH2 + 1, NE, T], F32, w1_flat)

        gate = sem("gate")
        loads, made, pool_step, edges_in = sem("loads"), sem("made"), sem("pool_step"), sem("edges_in")
        dve_step, hist_hot, hist_mm = sem("dve_step"), sem("hist_hot"), sem("hist_mm")
        counted, hist_out, hist_in = sem("counted"), sem("hist_out"), sem("hist_in")
        base_made, bins_out, bins_in = sem("base_made"), sem("bins_out"), sem("bins_in")
        hot_made, rank_ps, rank_read, rank_next = sem("hot_made"), sem("rank_ps"), sem("rank_read"), sem("rank_next")
        rank_step, addr_made, ring_made, pool_go = sem("rank_step"), sem("addr_made"), sem("ring_made"), sem("pool_go")
        scattered = sems("scattered", 2)
        x_in = sems("x_in", BODY)
        a_step, xn_made, xT_ps, xnT_made = (sem(n) for n in ("a_step", "xn_made", "xT_ps", "xnT_made"))
        sup_ps, kv_ps, q_ps, sup_read, kv_read = (sem(n) for n in (
            "sup_ps", "kv_ps", "q_ps", "sup_read", "kv_read"))
        kb_made, ke_made, qe_made, kphi_made, qphi_made, kv_added = (sem(n) for n in (
            "kb_made", "ke_made", "qe_made", "kphi_made", "qphi_made", "kv_added"))
        xn_stored = sems("xn_stored", BODY)
        stored = sems("stored", BODY)
        mix_in = sems("mix_in", BODY)
        sums_open, kvb_made, mix_used, b_step = sem("sums_open"), sem("kvb_made"), sem("mix_used"), sem("b_step")
        at_ps, at_made, atT_ps, atT_made, wo_ps, r1_made, x1_made, x1T_ps, x1T_made, h_ps, h_made, ff_ps, ff_read = (
            sem(n) for n in ("at_ps", "at_made", "atT_ps", "atT_made", "wo_ps", "r1_made", "x1_made", "x1T_ps",
                             "x1T_made", "h_ps", "h_made", "ff_ps", "ff_read"))
        var1_made, std1_made, var2_made, std2_made = (sem(n) for n in ("var1_made", "std1_made", "var2_made", "std2_made"))
        recs_in, landed = sems("recs_in", 2), sems("landed", 8)
        recs_used, gidx_made, onehot_made, pair_ps, acc_step = (sem(n) for n in (
            "recs_used", "gidx_made", "onehot_made", "pair_ps", "acc_step"))
        e_step, yn_made, yT_ps, yT_made, l1_ps, l1_made, l2_ps, l2_made, l3_ps, l3_read, gate_read, res_made = (
            sem(n) for n in ("e_step", "yn_made", "yT_ps", "yT_made", "l1_ps", "l1_made", "l2_ps", "l2_made",
                             "l3_ps", "l3_read", "gate_read", "res_made"))
        var_made, rstd_made = sem("var_made"), sem("rstd_made")
        logits_made, gexp_go, gexp_made = sem("logits_made"), sem("gexp_go"), sem("gexp_made")
        out_stored = sems("out_stored", 2)

        def moments(steps, dve, source, stats):
            steps.then(dve.bn_stats(stats[:, 0:6], source))
            dve.sem_inc(gate, 1)
            steps.then(dve.bn_aggr(stats[:, 6:8], stats[:, 0:6]))

        columns = [(bqc[:, :], bq.rearrange("(h p) -> p h", p=P)), (b1c[:, :], b1.rearrange("(h p) -> p h", p=P)),
                   (sb1c[:, :], sb1.rearrange("(h p) -> p h", p=P)), (sb2c[:, :], sb2.rearrange("(h p) -> p h", p=P)),
                   (eb1c[:, :], eb1.rearrange("e p -> p e")), (eb2c[:, :], eb2.rearrange("e p -> p e"))]
        blocks = [(w[:, :, :], d.rearrange("(h p) n -> p h n", p=P)) for w, d in
                  ((wg, Wg), (wq, Wq), (wk, Wk), (wv, Wv), (wo, Wo), (w1, W1), (w2, W2), (sw1, sW1), (sw2, sW2), (gw, gW))]
        blocks += [(sw3[:, :], sW3), (ew2[:, :, :], eW2.rearrange("e p n -> p e n")),
                   (ew3[0:EH2, :, :], eW3.rearrange("e p n -> p e n")),
                   (ew3[EH2:EH2 + 1, :, :], eb3.rearrange("(a e) n -> a e n", a=1))]
        blocks += [(ew1[:, :, e, :], eW1[e].rearrange("(h p) n -> p h n", p=P)) for e in range(NE)]
        broadcasts = [(rows[n][:, :], d.partition_broadcast(T)) for n, d in
                      (("bkr", bk), ("bvr", bv), ("bor", bo), ("g1r", g1), ("be1r", be1), ("b2r", b2), ("g2r", g2),
                       ("be2r", be2), ("sb3r", sb3))] + [(gbr[:, :], gb.partition_broadcast(T))]
        n_loads = len(columns) + len(blocks) + len(broadcasts)

        with nc.Block() as block:
            @block.sync
            def _(sp):
                for a, d in ((src_i, src), (dst_i, dst), (wgt, edge_weight)):
                    sp.dma_start(a, d.rearrange("(p c) -> p c", p=T)).then_inc(edges_in, 16)
                for a, d in blocks + broadcasts:
                    sp.dma_start(a, d).then_inc(loads, 16)
                with nc.allow_non_contiguous_dma(reason="bias columns, once"):
                    for a, d in columns:
                        sp.dma_start(a, d).then_inc(loads, 16)
                for s, n in ((rank_next, 2), (rank_step, 1), (kphi_made, 1), (qphi_made, 1), (sup_read, 1), (kv_read, 1), (kv_added, 1),
                             (stored[2], 32), (stored[3], 32), (mix_used, BODY), (ff_read, 1),
                             (pair_ps, 2 * PAIRS), (yT_ps, 1), (acc_step, SLOTS_PS), (l3_read, 6), (l2_made, 1), (gate_read, 1),
                             (out_stored[0], 16), (out_stored[1], 16)):
                    sp.sem_inc(s, n)
                for j in range(BODY):
                    sp.sem_inc(xn_stored[j], 16)
                sp.wait_ge(counted, 1)
                for k in range(STREAMS):
                    block_k = slice(k * DIGIT, (k + 1) * DIGIT)
                    sp.dma_start(hist_d[k], counts[block_k, block_k]).then_inc(hist_out, 16)
                sp.wait_ge(hist_out, 16 * STREAMS)
                sp.dma_start(hist.rearrange("p k b -> p (k b)"),
                             hist_d.rearrange("k a b -> (k a b)").partition_broadcast(T)).then_inc(hist_in, 16)
                sp.wait_ge(loads, 16 * n_loads)
                sp.wait_ge(base_made, 1)
                sp.dma_start(binof_d.rearrange("(p c) -> p c", p=CPART), bin_i).then_inc(bins_out, 16)
                sp.wait_ge(bins_out, 16)

            @block.gpsimd
            def _(pool):
                pool.iota(iota_i, pattern=[[1, P]], base=0, channel_multiplier=0).then_inc(made, 1)
                pool.iota(chunk_i, pattern=[[1, CPP]], base=0, channel_multiplier=CPP).then_inc(made, 1)
                pool.iota(iota_n[:, :], pattern=[[1, T]], base=0, channel_multiplier=0,
                          allow_small_or_imprecise_dtypes=True).then_inc(pool_step, 1)
                pool.memset(zeros, 0.0).then_inc(made, 1)
                pool.memset(kvb[:, :, :], 0.0).then_inc(made, 1)
                pool.memset(ident[:, :], 0.0).then_inc(pool_step, 1)
                pool.memset(ones_b[:, :], 1.0).then_inc(pool_step, 1)
                pool.memset(ones_f[:, :], 1.0).then_inc(pool_step, 1)
                pool.memset(zero_b[:, :], 0.0).then_inc(pool_step, 1)
                pool.memset(tiebreak[:, :, :], 1.0).then_inc(pool_step, 1)
                pool.memset(hot[0], 0.0).then_inc(made, 1)
                pool.memset(eps[:, 0:1], LN_EPS).then_inc(pool_step, 1)
                pool.memset(eps[:, 1:2], -0.5).then_inc(pool_step, 1)
                pool.wait_ge(pool_step, 8)
                pool.affine_select(out=ident[:, :], in_=ident[:, :], compare_op=ALU.not_equal, fill=1.0, base=0,
                                   pattern=[[-1, P]], channel_multiplier=1).then_inc(pool_step, 1)
                pool.affine_select(out=before[:, :], in_=ones_b[:, 0:T], compare_op=ALU.is_gt, fill=0.0, base=0,
                                   pattern=[[1, T]], channel_multiplier=-1).then_inc(pool_step, 1)
                pool.affine_select(out=upto[:, :], in_=ones_b[:, 0:T], compare_op=ALU.is_ge, fill=0.0, base=0,
                                   pattern=[[-1, T]], channel_multiplier=1).then_inc(pool_step, 1)
                pool.affine_select(out=tiebreak[:, :, :], in_=tiebreak[:, :, :], compare_op=ALU.is_gt, fill=0.0,
                                   base=0, pattern=[[1, NE], [-1, NE]], channel_multiplier=0).then_inc(pool_step, 1)
                pool.wait_ge(made, 4)
                table_rows = table_d.rearrange("(p c) w -> p (c w)", p=GROUPS + 2)
                for k in range(2):
                    pool.dma_start(table_rows[:, k * ZEROS:(k + 1) * ZEROS], zeros).then_inc(scattered[k], 16)
                pool.wait_ge(pool_step, 12)
                for k in range(2):
                    pool.wait_ge(scattered[k], 16)

            MAGIC = 12582912.0

            @block.vector
            def _(dve):
                s = Steps(dve, dve_step)
                dve.wait_ge(edges_in, 48)
                dve.wait_ge(made, 2)
                s.then(dve.tensor_copy(srcf, src_i))
                s.then(dve.tensor_scalar(grp, srcf, -float(T // 2), 1.0 / T, ALU.add, ALU.mult))
                s.then(dve.tensor_scalar(grp, grp, MAGIC, None, ALU.add))
                s.then(dve.tensor_scalar(grp, grp, -MAGIC, None, ALU.add))
                s.then(dve.tensor_copy(grp_b, grp))
                s.then(dve.tensor_copy(iota_b[:, :], iota_i[:, 0:NT]))
                s.then(dve.tensor_scalar(tens, grp, -(DIGIT - 1) / 2, 1.0 / DIGIT, ALU.add, ALU.mult))
                s.then(dve.tensor_scalar(tens, tens, MAGIC, None, ALU.add))
                s.then(dve.tensor_scalar(tens, tens, -MAGIC, None, ALU.add))
                s.then(dve.tensor_copy(digits[0], tens))
                s.then(dve.scalar_tensor_tensor(digits[1], tens, -float(DIGIT), grp, ALU.mult, ALU.add))
                with dve.Fori(0, SC // WIDE // 2) as i:
                    for h in range(2):
                        dve.wait_ge(hist_mm, 2 * i + h + 1)
                        for d in range(2):
                            values = digits[d].rearrange("p (k r) -> p r k", k=STREAMS)
                            mm = dve.tensor_tensor(
                                    digit_hot[h][d], values[:, bass.ds((2 * i + h) * WIDE, WIDE), :].unsqueeze(3)
                                    .to_broadcast([T, WIDE, STREAMS, DIGIT]),
                                    iota_b[:, 0:DIGIT].unsqueeze(1).unsqueeze(1).to_broadcast([T, WIDE, STREAMS, DIGIT]),
                                    ALU.is_equal)
                        mm.then_inc(hist_hot, 1)
                dve.wait_ge(hist_mm, SC // WIDE + 2)
                dve.tensor_copy(counts, banks[7][0:STREAMS * DIGIT, 0:STREAMS * DIGIT]).then_inc(counted, 1)
                dve.wait_ge(hist_in, 16)
                s.then(dve.tensor_reduce(total, hist.rearrange("p k b -> p b k"), AX.X, ALU.add))
                s.then(dve.tensor_scalar(chunks_i, total, float(P - 1), None, ALU.add))
                s.then(dve.tensor_scalar(chunks_i, chunks_i, 7, None, ALU.logical_shift_right))
                s.then(dve.tensor_copy(chunks_f, chunks_i))
                s.then(dve.memset(nothing, 0.0))
                s.then(dve.tensor_tensor_scan(cum, chunks_f, nothing, 0.0, ALU.add, ALU.add))
                s.then(dve.tensor_tensor(first, cum, chunks_f, ALU.subtract))
                s.then(dve.tensor_scalar(base[:, 0, :], first, float(P), None, ALU.mult))
                for k in range(1, STREAMS):
                    s.then(dve.tensor_tensor(base[:, k, :], base[:, k - 1, :], hist[:, k - 1, :], ALU.add))
                dve.wait_ge(pool_step, 12)
                s.then(dve.tensor_scalar(nothing, iota_n[0:T, 0:NT], float(CH), float(CH * LAG), ALU.mult, ALU.add))
                s.then(dve.tensor_tensor(nothing, cum, nothing, ALU.is_gt))
                s.then(dve.tensor_reduce(total[:, 0:1], nothing, AX.X, ALU.max))
                s.then(dve.tensor_copy(late_i[:, :], total[:, 0:1]))
                s.then(dve.tensor_copy(chunk_f, chunk_i))
                for q in range(CPP):
                    s.then(dve.tensor_scalar(ended[0:CPART], cum[0:CPART], chunk_f[:, q:q + 1], None, ALU.is_le))
                    s.then(dve.tensor_reduce(bin_f[:, q:q + 1], ended[0:CPART], AX.X, ALU.add))
                s.then(dve.tensor_scalar(bin_f, bin_f, float(NT - 1), float(D), ALU.min, ALU.mult))
                dve.tensor_copy(bin_i, bin_f).then_inc(base_made, 1)
                s.then(dve.tensor_scalar(grp, grp, -float(T), None, ALU.mult))
                s.then(dve.tensor_tensor(rec[:, :, 1], srcf, grp, ALU.add))
                s.then(dve.tensor_copy(rec[:, :, 0], dst_i))
                s.then(dve.tensor_copy(rec[:, :, 2], wgt))

            @block.tensor
            def _(pe):
                side = STREAMS * DIGIT
                pe.sem_inc(hist_mm, 2)
                pe.wait_ge(pool_step, 12)
                pe.matmul(banks[7][0:side, 0:side], zero_b[:, 0:side], zero_b[:, 0:side], start=True, stop=False,
                          skip_group_check=True)
                with pe.Fori(0, SC // WIDE // 2) as i:
                    for h in range(2):
                        pe.wait_ge(hist_hot, 2 * i + h + 1)
                        for r in range(WIDE):
                            tens_hot, ones_hot = (digit_hot[h][d][:, r].rearrange("p k b -> p (k b)") for d in range(2))
                            mm = pe.matmul(banks[7][0:side, 0:side], tens_hot, ones_hot, start=False, stop=False,
                                           skip_group_check=True)
                        mm.then_inc(hist_mm, 1)

        ranks = banks[0][0:T, 0:STREAMS * NT]
        groups = grp_b.rearrange("p (k r) -> p k r", k=STREAMS)
        records = rec.rearrange("p (k r) w -> p k r w", k=STREAMS)

        def rank_hot(dve, r, h):
            dve.wait_ge(rank_next, r + 1)
            dve.tensor_tensor(hot[h], groups[:, :, bass.ds(r, 1)].to_broadcast([T, STREAMS, NT]),
                              iota_b[:, :].unsqueeze(1).to_broadcast([T, STREAMS, NT]), ALU.is_equal).then_inc(hot_made, 1)

        def rank_product(dve, r, u):
            dve.wait_ge(rank_ps, r + 1)
            dve.wait_ge(rank_step, r + 1)
            dve.tensor_tensor(prod, ranks.rearrange("p (k b) -> p k b", k=STREAMS), hot[u % 2],
                              ALU.mult).then_inc(rank_read, 1)

        def rank_reduce(dve, r, u):
            dve.wait_ge(rank_read, r + 1)
            dve.tensor_reduce(slot_f[:, u * STREAMS:(u + 1) * STREAMS], prod, AX.X, ALU.add).then_inc(rank_step, 1)

        def rank_before(pe, r, h):
            pe.wait_ge(hot_made, r + 1)
            pe.matmul(ranks, before[:, :], hot[h].rearrange("p k b -> p (k b)"), start=False, stop=False,
                      skip_group_check=True).then_inc(rank_ps, 1)

        def rank_advance(pe, r, h):
            pe.wait_ge(rank_read, r + 1)
            pe.matmul(ranks, upto[:, :], hot[h].rearrange("p k b -> p (k b)"), start=False, stop=False,
                      skip_group_check=True).then_inc(rank_next, 1)

        def addresses(dve, turn, b, s):
            dve.wait_ge(rank_step, RANKS * turn + HALF * (b + 1) + 1)
            s.then(dve.tensor_copy(slot_i, slot_f))
            s.then(dve.tensor_scalar(slot_t, slot_i, P - 1, 4, ALU.bitwise_and, ALU.logical_shift_left))
            s.then(dve.scalar_tensor_tensor(slot_t, slot_i, -GROUP, slot_t, ALU.bitwise_and, ALU.bitwise_or))
            s.then(dve.tensor_scalar(slot_i, slot_i, 7, CH - 1, ALU.logical_shift_right, ALU.bitwise_and))
            dve.wait_ge(scattered[b], 16 * BATCH * turn + 16)
            dve.tensor_tensor(addr[b], slot_i, slot_t, ALU.bitwise_or).then_inc(addr_made, 1)

        def ring_records(act, turn, b):
            act.wait_ge(scattered[b], 16 * BATCH * turn + 16)
            act.sem_inc(gate, 1)
            act.copy(ring[b].rearrange("p (u k) w -> p k u w", u=HALF),
                     records[:, :, bass.ds(RANKS * turn + HALF * b, HALF), :]).then_inc(ring_made, 1)

        def scatter(pool, turn, b):
            pool.wait_ge(addr_made, 2 * turn + b + 1)
            pool.wait_ge(ring_made, 2 * turn + b + 1)
            pool.sem_inc(pool_go, 1)
            for c in range(BATCH):
                pool.indirect_dma_start(table_d, bass.IndirectOffsetOnAxis(addr[b][:, c:c + 1], 0), ring[b][:, c, :],
                                        None).then_inc(scattered[b], 16)

        kv_sum = [banks[1][:, 0:P + 1], banks[2][:, 0:P + 1]]

        with nc.Block() as block:
            @block.sync
            def _(sp):
                def turn(i, last=False):
                    for j in range(BODY):
                        sp.wait_ge(xn_made, BODY * i + j + 1)
                        sp.dma_start(xn_d[bass.ds((BODY * i + j) * T, T), :], xn[j]).then_inc(xn_stored[j], 16)
                        if not last:
                            sp.dma_start(xt[j], x[bass.ds((BODY * i + BODY + j) * T, T), :]).then_inc(x_in[j], 16)
                    for j in range(BODY):
                        t = BODY * i + j
                        sp.wait_ge(sup_read, t + 2)
                        sp.dma_start(support_d[bass.ds(t * T, T), :], sup[j % 2]).then_inc(stored[j], 16)
                        sp.wait_ge(qphi_made, t + 2)
                        sp.dma_start(q_d[bass.ds(t, 1)].rearrange("t p c -> (t p) c"), qphi[j % 2]).then_inc(stored[j], 16)

                for j in range(BODY):
                    sp.dma_start(xt[j], x[j * T:(j + 1) * T, :]).then_inc(x_in[j], 16)
                with sp.Fori(0, TURNS - 1) as i:
                    turn(i)
                turn(TURNS - 1, last=True)
                for j in range(BODY):
                    sp.wait_ge(stored[j], 32 * (TURNS + (j >= 2)))
                    sp.wait_ge(xn_stored[j], 16 * TURNS + 16)

            @block.gpsimd
            def _(pool):
                with pool.Fori(0, TURNS) as i:
                    for b in range(2):
                        scatter(pool, i, b)

            @block.tensor
            def _(pe):
                def turn_x(t, j):
                    pe.wait_ge(xn_made, t + 1)
                    for f in range(H2):
                        mm = pe.transpose(banks[3][:, f * T:(f + 1) * T], xn[j][:, f * P:(f + 1) * P], ident[0:T, 0:T])
                    mm.then_inc(xT_ps, 1)

                def turn(i, last=False):
                    for j in range(BODY):
                        t, r = BODY * i + j, RANKS * i + 2 * j
                        rows_T = [xnT[j % 2][:, f * T:(f + 1) * T] for f in range(H2)]
                        rank_before(pe, r, 0)
                        pe.wait_ge(xnT_made, t + 1)
                        pe.wait_ge(kv_read, t + 1)
                        for n, w in enumerate((wk, wv)):
                            for f in range(H2):
                                mm = pe.matmul(banks[5][0:T, n * D:(n + 1) * D], rows_T[f], w[:, f, :], start=f == 0,
                                               stop=f == H2 - 1)
                        mm.then_inc(kv_ps, 1)
                        for m in range(H2):
                            for f in range(H2):
                                mm = pe.matmul(banks[6][:, m * T:(m + 1) * T], wq[:, f, m * P:(m + 1) * P], rows_T[f],
                                               start=f == 0, stop=f == H2 - 1)
                        mm.then_inc(q_ps, 1)
                        if j < BODY - 1:
                            turn_x(t + 1, j + 1)
                        pe.wait_ge(sup_read, t + 1)
                        for f in range(H2):
                            mm = pe.matmul(banks[4][0:T, 0:D], rows_T[f], wg[:, f, :], start=f == 0, stop=f == H2 - 1)
                        mm.then_inc(sup_ps, 1)
                        rank_advance(pe, r, 0)
                        rank_before(pe, r + 1, 1)
                        pe.wait_ge(kphi_made, t + 2)
                        for f in range(H2):
                            mm = pe.matmul(kv_sum[f], kphi[:, f * P:(f + 1) * P], vt[:, f, :], start=False, stop=False,
                                           skip_group_check=True)
                        mm.then_inc(kv_added, 1)
                        if not last and j == BODY - 1:
                            turn_x(t + 1, 0)
                        rank_advance(pe, r + 1, 1)

                pe.matmul(ranks, ones_f[0:1, 0:T], base[0:1, :, :].rearrange("p k b -> p (k b)"), start=True,
                          stop=False, skip_group_check=True)
                for f in range(H2):
                    mm = pe.matmul(kv_sum[f], zero_b[:, :], hot[0].rearrange("p k b -> p (k b)")[:, 0:P + 1],
                                   start=True, stop=False, skip_group_check=True)
                mm.then_inc(sums_open, 1)
                turn_x(0, 0)
                with pe.Fori(0, TURNS - 1) as i:
                    turn(i)
                turn(TURNS - 1, last=True)

            @block.scalar
            def _(act):
                def copy_x(t, j):
                    act.wait_ge(xT_ps, t + 1)
                    act.copy(xnT[j % 2], banks[3][:, 0:H2 * T]).then_inc(xnT_made, 1)

                def turn(i, last=False):
                    for j in range(BODY):
                        t = BODY * i + j
                        act.wait_ge(kb_made, t + 1)
                        act.wait_ge(kphi_made, t + 1)
                        act.activation(ke, kb, ACT.Exp)
                        act.activation(kr, kb, ACT.Relu).then_inc(ke_made, 1)
                        act.wait_ge(q_ps, t + 1)
                        act.wait_ge(qphi_made, t + 1)
                        for m in range(H2):
                            act.activation(qe[:, m * T:(m + 1) * T], banks[6][:, m * T:(m + 1) * T], ACT.Exp,
                                           bias=bqc[:, m:m + 1])
                        for m in range(H2):
                            mm = act.activation(qr[:, m * T:(m + 1) * T], banks[6][:, m * T:(m + 1) * T], ACT.Relu,
                                                bias=bqc[:, m:m + 1])
                        mm.then_inc(qe_made, 1)
                        if j < BODY - 1:
                            copy_x(t + 1, j + 1)
                        act.wait_ge(stored[(j + 2) % BODY], 32 * i + 32)
                        act.wait_ge(sup_ps, t + 1)
                        act.copy(sup[j % 2], banks[4][0:T, 0:D]).then_inc(sup_read, 1)
                        if j % 2 == 0:
                            ring_records(act, i, j // 2)
                        if not last and j == BODY - 1:
                            copy_x(t + 1, 0)

                copy_x(0, 0)
                with act.Fori(0, TURNS - 1) as i:
                    turn(i)
                turn(TURNS - 1, last=True)

            @block.vector
            def _(dve):
                def row_moments(a, i, j):
                    dve.wait_ge(x_in[j], 16 * i + 16)
                    a.then(dve.bn_stats(stats6[:, j, :], xt[j]))
                    dve.sem_inc(gate, 1)
                    a.issue(dve.bn_aggr(mean_var[:, j, :], stats6[:, j, :]))

                def normalise_rows(a, i):
                    a.settle()
                    a.then(dve.tensor_scalar(var4, mean_var[:, :, 1], LN_EPS, None, ALU.add))
                    a.then(dve.tensor_scalar(t4.bitcast(I32), var4.bitcast(I32), 1, None, ALU.logical_shift_right))
                    a.then(dve.tensor_scalar(rstd4.bitcast(I32), t4.bitcast(I32), -1.0, float(0x5F3759DF), ALU.mult,
                                             ALU.add))
                    for _ in range(3):
                        a.then(dve.tensor_tensor(t4, rstd4, rstd4, ALU.mult))
                        a.then(dve.tensor_tensor(t4, t4, var4, ALU.mult))
                        a.then(dve.tensor_scalar(t4, t4, -0.5, 1.5, ALU.mult, ALU.add))
                        a.then(dve.tensor_tensor(rstd4, rstd4, t4, ALU.mult))
                    for j in range(BODY):
                        dve.wait_ge(xn_stored[j], 16 * i + 16)
                        dve.tensor_scalar(xn[j], xt[j], mean_var[:, j, 0:1], rstd4[:, j:j + 1], ALU.subtract,
                                          ALU.mult).then_inc(xn_made, 1)

                def turn(i, last=False):
                    a = Steps(dve, a_step, A_FRONT + A_STEPS * i)
                    for j in range(BODY):
                        t, r = BODY * i + j, RANKS * i + 2 * j
                        dve.wait_ge(kv_ps, t + 1)
                        dve.tensor_tensor(kb, banks[5][0:T, 0:D], rows["bkr"][:, :], ALU.add).then_inc(kb_made, 1)
                        dve.wait_ge(kv_added, t + 1)
                        dve.tensor_tensor(vt[:, :, 0:P], banks[5][0:T, D:2 * D].rearrange("p (f c) -> p f c", f=H2),
                                          rows["bvr"][:, :].rearrange("p (f c) -> p f c", f=H2), ALU.add).then_inc(kv_read, 1)
                        rank_product(dve, r, 2 * j % HALF)
                        rank_hot(dve, r + 1, 1)
                        if not last:
                            row_moments(a, i + 1, j)
                        rank_reduce(dve, r, 2 * j % HALF)
                        dve.wait_ge(ke_made, t + 1)
                        dve.wait_ge(kv_read, t + 2)
                        dve.scalar_tensor_tensor(kphi, ke, 1.0, kr, ALU.min, ALU.add).then_inc(kphi_made, 1)
                        dve.wait_ge(qe_made, t + 1)
                        dve.wait_ge(stored[(j + 2) % BODY], 32 * i + 32)
                        dve.scalar_tensor_tensor(qphi[j % 2], qe, 1.0, qr, ALU.min, ALU.add).then_inc(qphi_made, 1)
                        if not last and j == BODY - 1:
                            dve.wait_ge(xT_ps, t + 1)
                            normalise_rows(a, i + 1)
                        rank_product(dve, r + 1, 2 * j % HALF + 1)
                        if not (last and j == BODY - 1):
                            rank_hot(dve, r + 2, 0)
                        rank_reduce(dve, r + 1, 2 * j % HALF + 1)
                        if j % 2:
                            addresses(dve, i, j // 2, a)
                    assert last or a.n == A_STEPS, a.n

                dve.memset(vt[:, :, P:P + 1], 1.0)
                dve.wait_ge(sums_open, 1)
                a = Steps(dve, a_step)
                rank_hot(dve, 0, 0)
                for j in range(BODY):
                    row_moments(a, 0, j)
                normalise_rows(a, 0)
                assert a.n == A_FRONT, a.n
                with dve.Fori(0, TURNS - 1) as i:
                    turn(i)
                turn(TURNS - 1, last=True)
                dve.wait_ge(kv_added, NT + 1)
                for f in range(H2):
                    for h in range(HPH):
                        q = slice(h * DH, (h + 1) * DH)
                        dve.tensor_copy(kvb[q, f, q], kv_sum[f][q, q]).then_inc(kvb_made, 1)
                        dve.tensor_copy(kvb[q, f, P + h:P + h + 1], kv_sum[f][q, P:P + 1]).then_inc(kvb_made, 1)

        with nc.Block() as block:
            @block.sync
            def _(sp):
                def load(i, j):
                    t = BODY * i + j
                    sp.wait_ge(mix_used, t + 1)
                    sp.dma_start(qT[j], q_d[bass.ds(t, 1)].rearrange("t p c -> (t p) c")).then_inc(mix_in[j], 16)
                    sp.dma_start(xr[j], xn_d[bass.ds(t * T, T), :]).then_inc(mix_in[j], 16)
                    sp.dma_start(xo[j], x[bass.ds(t * T, T), :]).then_inc(mix_in[j], 16)

                with sp.Fori(0, TURNS) as i:
                    for j in range(BODY):
                        load(i, j)

            @block.gpsimd
            def _(pool):
                with pool.Fori(TURNS, 2 * TURNS) as i:
                    for b in range(2):
                        scatter(pool, i, b)
                for b in range(2):
                    pool.wait_ge(scattered[b], 16 * BATCH * 2 * TURNS + 16)

            attn = banks[1][0:T, 0:H2 * KVW]

            @block.tensor
            def _(pe):
                def attend(i, j):
                    pe.wait_ge(mix_in[j], 48 * i + 48)
                    for f in range(H2):
                        mm = pe.matmul(attn[:, f * KVW:(f + 1) * KVW], qT[j][:, f * T:(f + 1) * T], kvb[:, f, :],
                                       start=True, stop=True)
                    mm.then_inc(at_ps, 1)

                def turn_attention(t):
                    pe.wait_ge(at_made, t + 1)
                    for f in range(H2):
                        mm = pe.transpose(banks[2][:, f * T:(f + 1) * T], at[:, f * P:(f + 1) * P], ident[0:T, 0:T])
                    mm.then_inc(atT_ps, 1)

                def project(t):
                    pe.wait_ge(atT_made, t + 1)
                    for f in range(H2):
                        mm = pe.matmul(banks[3][0:T, 0:D], atT[:, f * T:(f + 1) * T], wo[:, f, :], start=f == 0,
                                       stop=f == H2 - 1)
                    mm.then_inc(wo_ps, 1)

                def turn_x1(t, j):
                    pe.wait_ge(x1_made, t + 1)
                    for f in range(H2):
                        mm = pe.transpose(banks[4][:, f * T:(f + 1) * T], x1[j % 2][:, f * P:(f + 1) * P],
                                          ident[0:T, 0:T])
                    mm.then_inc(x1T_ps, 1)

                def widen(t, chunks):
                    for m in chunks:
                        for f in range(H2):
                            mm = pe.matmul(banks[5 + m // 4][:, m % 4 * T:(m % 4 + 1) * T], w1[:, f, m * P:(m + 1) * P],
                                           x1T[:, f * T:(f + 1) * T], start=f == 0, stop=f == H2 - 1)
                        if m % 4 == 3:
                            mm.then_inc(h_ps, 1)

                def narrow(t):
                    pe.wait_ge(h_made, t + 1)
                    pe.wait_ge(ff_read, t + 1)
                    for m in range(FC):
                        mm = pe.matmul(banks[7][0:T, 0:D], hT[:, m, :], w2[:, m, :], start=m == 0, stop=m == FC - 1)
                    mm.then_inc(ff_ps, 1)

                def turn(i, last=False):
                    for j in range(BODY):
                        t, r = BODY * i + j, RANKS * (i + TURNS) + 2 * j
                        front = not (last and j == BODY - 1)
                        rank_before(pe, r, 0)
                        pe.wait_ge(x1T_made, t + 1)
                        widen(t, range(0, 2))
                        if front:
                            turn_attention(t + 1)
                        widen(t, range(2, 6))
                        if front:
                            project(t + 1)
                        rank_advance(pe, r, 0)
                        widen(t, range(6, 8))
                        rank_before(pe, r + 1, 1)
                        if not (last and j >= BODY - 2):
                            attend(i + (j + 2) // BODY, (j + 2) % BODY)
                        narrow(t)
                        rank_advance(pe, r + 1, 1)
                        if front:
                            turn_x1(t + 1, j + 1)

                pe.wait_ge(kvb_made, 4 * HPH)
                attend(0, 0)
                turn_attention(0)
                attend(0, 1)
                project(0)
                turn_x1(0, 0)
                with pe.Fori(0, TURNS - 1) as i:
                    turn(i)
                turn(TURNS - 1, last=True)

            @block.scalar
            def _(act):
                def copies(t):
                    act.wait_ge(atT_ps, t + 1)
                    act.copy(atT, banks[2][:, 0:H2 * T]).then_inc(atT_made, 1)

                def hidden(t, c):
                    act.wait_ge(h_ps, 2 * t + c + 1)
                    for m in range(c * FC // 2, (c + 1) * FC // 2):
                        mm = act.activation(hT[:, m, :], banks[5 + c][:, m % 4 * T:(m % 4 + 1) * T], ACT.Relu,
                                            bias=b1c[:, m:m + 1])
                    if c:
                        mm.then_inc(h_made, 1)

                def x1_copy(t):
                    act.wait_ge(x1T_ps, t + 1)
                    act.copy(x1T, banks[4][:, 0:H2 * T]).then_inc(x1T_made, 1)

                def turn(i, first=False, last=False):
                    for j in range(BODY):
                        t = BODY * i + j
                        front = not (last and j == BODY - 1)
                        if j % 2 == 0:
                            ring_records(act, i + TURNS, j // 2)
                        if front:
                            copies(t + 1)
                        hidden(t, 0)
                        if not (first and j == 0):
                            deviation(t - 1, var2_made, std2_made, ln2)
                        hidden(t, 1)
                        if front:
                            deviation(t + 1, var1_made, std1_made, ln)
                            x1_copy(t + 1)

                def deviation(t, variance, made, stats):
                    act.wait_ge(variance, t + 1)
                    act.activation(stats[:, 9:10], stats[:, 7:8], ACT.Sqrt, bias=eps[:, 0:1]).then_inc(made, 1)

                copies(0)
                deviation(0, var1_made, std1_made, ln)
                x1_copy(0)
                turn(0, first=True)
                with act.Fori(1, TURNS - 1) as i:
                    turn(i)
                turn(TURNS - 1, last=True)
                deviation(NT - 1, var2_made, std2_made, ln2)

            @block.vector
            def _(dve):
                def normalise(b, i, j):
                    t = BODY * i + j
                    dve.wait_ge(at_ps, t + 1)
                    halves = attn.rearrange("p (f c) -> p f c", f=H2)
                    b.then(dve.tensor_scalar(zr, halves[:, :, P:KVW], 1e-6, None, ALU.add))
                    b.then(dve.reciprocal(zr, zr))
                    for f in range(H2):
                        mm = dve.tensor_tensor(at[:, f * P:(f + 1) * P].rearrange("p (h e) -> p h e", h=HPH),
                                               halves[:, f, 0:P].rearrange("p (h e) -> p h e", h=HPH),
                                               zr[:, f, :].unsqueeze(2).to_broadcast([T, HPH, DH]), ALU.mult)
                    mm.then_inc(at_made, 1)

                def first_norm(b, i, j, between=None):
                    t = BODY * i + j
                    b.settle()
                    dve.wait_ge(wo_ps, t + 1)
                    b.then(dve.tensor_tensor(r1, banks[3][0:T, 0:D], xr[j], ALU.add))
                    moments(b, dve, r1, ln)
                    dve.sem_inc(var1_made, 1)
                    if between:
                        between()
                    dve.wait_ge(std1_made, t + 1)
                    b.then(dve.reciprocal(ln[:, 8:9], ln[:, 9:10]))
                    b.then(dve.tensor_scalar(r1, r1, ln[:, 6:7], ln[:, 8:9], ALU.subtract, ALU.mult))
                    b.then(dve.tensor_tensor(r1, r1, rows["g1r"][:, :], ALU.mult))
                    b.then(dve.tensor_tensor(x1[j % 2], r1, rows["be1r"][:, :], ALU.add))
                    dve.sem_inc(x1_made, 1)

                def second_moments(b, t, j):
                    dve.wait_ge(x1T_ps, t + 1)
                    b.issue(dve.tensor_tensor(x1[j % 2], x1[j % 2], rows["b2r"][:, :], ALU.add))
                    b.then(dve.tensor_tensor(xo[j], xo[j], rows["be2r"][:, :], ALU.add))
                    dve.wait_ge(ff_ps, t + 1)
                    dve.tensor_tensor(r2, banks[7][0:T, 0:D], x1[j % 2], ALU.add).then_inc(ff_read, 1)
                    dve.wait_ge(ff_read, t + 2)
                    moments(b, dve, r2, ln2)
                    dve.sem_inc(var2_made, 1)

                def second_norm(b, t, j):
                    dve.wait_ge(std2_made, t + 1)
                    b.then(dve.reciprocal(ln2[:, 8:9], ln2[:, 9:10]))
                    b.then(dve.tensor_scalar(r2, r2, ln2[:, 6:7], ln2[:, 8:9], ALU.subtract, ALU.mult))
                    b.then(dve.tensor_tensor(r2, r2, rows["g2r"][:, :], ALU.mult))
                    b.then(dve.tensor_tensor(acc_flat[:, bass.ds(t * D, D)], r2, xo[j], ALU.add))
                    dve.sem_inc(mix_used, 1)

                def turn(i, first=False, last=False):
                    b = Steps(dve, b_step, B_FRONT + B_STEPS * i - (0 if first else B_BACK))
                    for j in range(BODY):
                        t, r = BODY * i + j, RANKS * (i + TURNS) + 2 * j
                        front = not (last and j == BODY - 1)
                        back = not (first and j == 0)
                        n = (i, j + 1) if j < BODY - 1 else (i + 1, 0)
                        if front:
                            normalise(b, *n)
                        if back:
                            second_moments(b, t - 1, (j - 1) % BODY)
                        rank_product(dve, r, 2 * j % HALF)
                        rank_hot(dve, r + 1, 1)
                        if front:
                            b.issue(dve.tensor_tensor(xr[n[1]], xr[n[1]], rows["bor"][:, :], ALU.add))
                        rank_reduce(dve, r, 2 * j % HALF)
                        if back:
                            second_norm(b, t - 1, (j - 1) % BODY)
                        if front:
                            first_norm(b, *n, between=lambda: rank_product(dve, r + 1, 2 * j % HALF + 1))
                        else:
                            rank_product(dve, r + 1, 2 * j % HALF + 1)
                        if front:
                            rank_hot(dve, r + 2, 0)
                        rank_reduce(dve, r + 1, 2 * j % HALF + 1)
                        if j % 2:
                            addresses(dve, i + TURNS, j // 2, b)
                    assert last or b.n == B_STEPS - B_BACK * first, b.n
                    return b

                b = Steps(dve, b_step)
                rank_hot(dve, RANKS * TURNS, 0)
                normalise(b, 0, 0)
                b.then(dve.tensor_tensor(xr[0], xr[0], rows["bor"][:, :], ALU.add))
                first_norm(b, 0, 0)
                assert b.n == B_FRONT, b.n
                turn(0, first=True)
                with dve.Fori(1, TURNS - 1) as i:
                    turn(i)
                b = turn(TURNS - 1, last=True)
                second_moments(b, NT - 1, (NT - 1) % BODY)
                second_norm(b, NT - 1, (NT - 1) % BODY)

        y_ps = banks[2][:, H2 * T:2 * H2 * T]
        s1_ps, s2_ps = banks[2][:, 0:H2 * T], banks[2][:, 0:T]
        logits_ps = banks[5][0:T, D:D + NE]

        def turn_y(pe, t):
            pe.wait_ge(yn_made, t + 1)
            pe.wait_ge(l2_made, t + 1)
            for f in range(H2):
                mm = pe.transpose(y_ps[:, f * T:(f + 1) * T], yn[:, f * P:(f + 1) * P], ident[0:T, 0:T])
            mm.then_inc(yT_ps, 1)

        def first_shared(pe, t):
            pe.wait_ge(yT_made, t + 1)
            for m in range(H2):
                for f in range(H2):
                    mm = pe.matmul(s1_ps[:, m * T:(m + 1) * T], sw1[:, f, m * P:(m + 1) * P],
                                   yT[:, f * T:(f + 1) * T], start=f == 0, stop=f == H2 - 1)
            mm.then_inc(l1_ps, 1)
            pe.wait_ge(gate_read, t + 1)
            pe.wait_ge(l3_read, 3 * t + 4)
            for f in range(H2):
                mm = pe.matmul(logits_ps, yT[:, f * T:(f + 1) * T], gw[:, f, :], start=f == 0, stop=f == H2 - 1)
            mm.then_inc(logits_made, 1)

        def first_experts(pe, t, experts):
            for e in experts:
                for f in range(H2):
                    mm = pe.matmul(banks[3][:, e * T:(e + 1) * T], ew1[:, f, e, :], yT[:, f * T:(f + 1) * T],
                                   start=f == 0, stop=f == H2 - 1)
            if e == NE - 1:
                mm.then_inc(l1_ps, 1)

        def second_layers(pe, t):
            pe.wait_ge(l1_made, t + 1)
            for m in range(H2):
                pe.matmul(s2_ps, sw2[:, m, :], s1T[:, m, :], start=m == 0, stop=m == H2 - 1)
            for e in range(NE):
                mm = pe.matmul(banks[3][0:EH2, e * T:(e + 1) * T], ew2[:, e, :], e1T[:, e, :], start=True, stop=True)
            mm.then_inc(l2_ps, 1)

        def third_layers(pe, t, half):
            if half == 0:
                pe.wait_ge(l2_made, t + 2)
                pe.wait_ge(gate_read, t + 2)
                pe.wait_ge(l3_read, 3 * t + 6)
                pe.matmul(banks[5][0:T, 0:D], s2T, sw3[:, :], start=True, stop=True)
            else:
                pe.wait_ge(l3_read, 3 * t + 8)
            for k in range(2):
                mm = pe.matmul(banks[7][0:T, k * D:(k + 1) * D], e2T[:, 2 * half + k, :], ew3[:, 2 * half + k, :],
                               start=True, stop=True)
            mm.then_inc(l3_ps, 1)

        def hidden_layers(act, t):
            act.wait_ge(yT_ps, t + 2)
            act.copy(yT, y_ps).then_inc(yT_made, 1)
            act.wait_ge(l1_ps, 2 * t + 1)
            for m in range(H2):
                act.activation(s1T[:, m, :], s1_ps[:, m * T:(m + 1) * T], ACT.Relu, bias=sb1c[:, m:m + 1])
            act.wait_ge(l1_ps, 2 * t + 2)
            for e in range(NE):
                mm = act.activation(e1T[:, e, :], banks[3][:, e * T:(e + 1) * T], ACT.Relu, bias=eb1c[:, e:e + 1])
            mm.then_inc(l1_made, 1)
            act.wait_ge(gexp_go, 2 * t + 1)
            act.activation(soft, soft, ACT.Exp).then_inc(gexp_made, 1)
            act.wait_ge(l2_ps, t + 1)
            act.wait_ge(l3_ps, 2 * t + 1)
            act.activation(s2T, s2_ps, ACT.Relu, bias=sb2c[:, 0:1])
            for e in range(NE):
                mm = act.activation(e2T[0:EH2, e, :], banks[3][0:EH2, e * T:(e + 1) * T], ACT.Relu, bias=eb2c[:, e:e + 1])
            mm.then_inc(l2_made, 1)
            act.wait_ge(gexp_go, 2 * t + 2)
            act.activation(soft, soft, ACT.Exp).then_inc(gexp_made, 1)

        def tile_moments(e, dve, t, h):
            moments(e, dve, acc_flat[:, bass.ds(t * D, D)], lne[h])
            tile_variance(dve, h)

        def tile_variance(dve, h):
            dve.tensor_scalar(lne[h][:, 9:10], lne[h][:, 7:8], LN_EPS, None, ALU.add).then_inc(var_made, 1)

        def tile_rstd(pool, t, h):
            pool.wait_ge(var_made, t + 1)
            pool.tensor_tensor(lne[h][:, 8:9], lne[h][:, 9:10], eps[:, 1:2], ALU.pow).then_inc(rstd_made, 1)

        def tile_norm(dve, n, t, h):
            dve.wait_ge(rstd_made, n + 1)
            dve.wait_ge(yT_ps, n + 1)
            dve.tensor_scalar(yn, acc_flat[:, bass.ds(t * D, D)], lne[h][:, 6:7], lne[h][:, 8:9], ALU.subtract,
                              ALU.mult).then_inc(yn_made, 1)

        def route_logits(e, dve, t):
            dve.wait_ge(logits_made, t + 1)
            e.settle()
            dve.tensor_tensor(logit, logits_ps, gbr[:, :], ALU.add).then_inc(gate_read, 1)

        def largest(e, dve):
            e.issue(dve.tensor_reduce(gstat[:, 0:1], logit, AX.X, ALU.max))

        def ask_exp(e, dve):
            e.settle()
            dve.tensor_scalar(soft, logit, gstat[:, 0:1], None, ALU.subtract).then_inc(gexp_go, 1)

        def total_exp(e, dve, count):
            dve.wait_ge(gexp_made, count)
            e.settle()
            e.issue(dve.tensor_reduce(gstat[:, 1:2], soft, AX.X, ALU.add))

        def invert_total(e, dve):
            e.settle()
            e.issue(dve.reciprocal(gstat[:, 2:3], gstat[:, 1:2]))

        def gates(e, dve):
            e.settle()
            e.issue(dve.tensor_scalar(logit, soft, gstat[:, 2:3], None, ALU.mult))

        mine = logit.unsqueeze(2).to_broadcast([T, NE, NE])
        others = logit.unsqueeze(1).to_broadcast([T, NE, NE])

        def rank_compare(e, dve):
            e.settle()
            e.issue(dve.tensor_tensor(beats, others, mine, ALU.is_gt))
            e.issue(dve.tensor_tensor(ties, others, mine, ALU.is_equal))

        def rank_ties(e, dve):
            e.settle()
            e.issue(dve.tensor_tensor(ties, ties, tiebreak[:, :, :], ALU.mult))

        def rank_join(e, dve):
            e.settle()
            e.issue(dve.tensor_tensor(beats, beats, ties, ALU.add))

        def rank_count(e, dve):
            e.settle()
            e.issue(dve.tensor_reduce(rank4, beats, AX.X, ALU.add))

        def choose(e, dve):
            e.settle()
            e.issue(dve.tensor_scalar(chosen, rank4, 1.5, None, ALU.is_lt))

        def keep_chosen(e, dve, t):
            dve.wait_ge(gexp_made, 2 * t + 2)
            e.settle()
            e.issue(dve.tensor_tensor(soft, soft, chosen, ALU.mult))

        def weights(e, dve, h):
            e.settle()
            e.issue(dve.tensor_scalar(gwt[h], soft, gstat[:, 2:3], None, ALU.mult))

        def route_first(e, dve, t):
            route_logits(e, dve, t)
            dve.wait_ge(gate_read, t + 2)
            largest(e, dve)
            ask_exp(e, dve)
            total_exp(e, dve, 2 * t + 1)
            invert_total(e, dve)
            gates(e, dve)
            e.settle()
            largest(e, dve)

        def route_second(e, dve, t, h):
            ask_exp(e, dve)
            rank_compare(e, dve)
            rank_ties(e, dve)
            rank_join(e, dve)
            rank_count(e, dve)
            choose(e, dve)
            keep_chosen(e, dve, t)
            total_exp(e, dve, 2 * t + 2)
            invert_total(e, dve)
            weights(e, dve, h)

        def combine_shared(e, dve, n, t, h, use):
            dve.wait_ge(l3_ps, 2 * n + 2)
            dve.wait_ge(out_stored[h], use)
            e.settle()
            e.issue(dve.tensor_tensor(res[h], banks[5][0:T, 0:D], acc_flat[:, bass.ds(t * D, D)], ALU.add))

        def combine_bias(e, dve, h):
            e.settle()
            dve.sem_inc(l3_read, 1)
            e.issue(dve.tensor_tensor(res[h], res[h], rows["sb3r"][:, :], ALU.add))

        def combine_expert(e, dve, n, h, k):
            if k == 2:
                dve.wait_ge(l3_ps, 2 * n + 3)
            e.settle()
            e.issue(dve.scalar_tensor_tensor(res[h], banks[7][0:T, k % 2 * D:(k % 2 + 1) * D], gwt[h][:, k:k + 1], res[h],
                                             ALU.mult, ALU.add))

        def combine_done(e, dve, half):
            e.settle()
            dve.sem_inc(l3_read, 1)
            if half:
                dve.sem_inc(res_made, 1)

        def combine(e, dve, n, t, h, use):
            combine_shared(e, dve, n, t, h, use)
            combine_bias(e, dve, h)
            for k in range(NE):
                combine_expert(e, dve, n, h, k)
                if k % 2:
                    combine_done(e, dve, k // 2)

        def store_result(sp, t, h, count):
            sp.wait_ge(res_made, count)
            sp.dma_start(out[bass.ds(t * T, T), :], res[h]).then_inc(out_stored[h], 16)

        product = [banks[b][0:T, k * D:(k + 1) * D] for b in (0, 1, 4, 6) for k in range(2)]
        with nc.Block() as block:
            @block.sync
            def _(sp):
                sp.dma_start(binof, binof_d.rearrange("(a c) -> a c", a=1)).then_inc(bins_in, 16)
                table_groups = table_d.rearrange("(g p c) w -> g p (c w)", p=P, c=CH)

                def load(g, h):
                    sp.dma_start(recs[h].rearrange("p c w -> p (c w)"),
                                 table_groups[bass.ds(g, 1)].rearrange("g p c -> (g p) c")).then_inc(recs_in[h], 16)

                def turn(i, results):
                    for h in range(2):
                        sp.wait_ge(recs_used, 2 * i + h + 1)
                        load(2 * i + h + 2, h)
                        if results:
                            t = 2 * i + h - COMBINE_LAG
                            store_result(sp, t, h, t + 1)

                load(0, 0)
                load(1, 1)
                with sp.Fori(0, COMBINE_LAG // 2) as i:
                    turn(i, False)
                with sp.Fori(COMBINE_LAG // 2, GROUPS // 2) as i:
                    turn(i, True)
                for t in range(GROUPS - COMBINE_LAG, NT):
                    store_result(sp, t, t % 2, t + 1)
                for h in range(2):
                    sp.wait_ge(recs_in[h], 16 * (GROUPS // 2 + 1))
                    sp.wait_ge(out_stored[h], 16 * (NT // 2) + 16)

            @block.gpsimd
            def _(pool):
                def group(i, h, layers):
                    g = 2 * i + h
                    for q in range(4):
                        if layers and q == 1:
                            tile_rstd(pool, g - NORM_LAG, 1 - h)
                        if q == 0:
                            pool.wait_ge(gidx_made, g + 1)
                        pool.wait_ge(pair_ps, PAIRS * g + 2 * q + 2)
                        pool.sem_inc(pool_go, 1)
                        for c in range(4 * q, 4 * q + 4):
                            pool.indirect_dma_start(rowbuf[h][c], None, support_d,
                                                    bass.IndirectOffsetOnAxis(gidx[h][:, c:c + 1], 0)
                                                    ).then_inc(landed[4 * h + q], 16)

                with pool.Fori(0, LAG // 2) as i:
                    for h in range(2):
                        group(i, h, False)
                group(LAG // 2, 0, False)
                group(LAG // 2, 1, True)
                with pool.Fori(LAG // 2 + 1, GROUPS // 2) as i:
                    for h in range(2):
                        group(i, h, True)
                for t in range(GROUPS - NORM_LAG, NT):
                    tile_rstd(pool, t, t % 2)

            @block.tensor
            def _(pe):
                def sum_chunks(g, i, h, chunks):
                    for c in chunks:
                        if c % 4 == 0:
                            pe.wait_ge(landed[4 * h + c // 4], 64 * i + 64)
                        if c % 2 == 0:
                            pe.wait_ge(onehot_made, PAIRS * g + c // 2 + 1)
                            pe.wait_ge(acc_step, CH * g + c + 2)
                        mm = pe.matmul(product[c % SLOTS_PS], onehot[c // 2 % AHEAD][:, c % 2, :], rowbuf[h][c], start=True,
                                       stop=True)
                        if c % 2:
                            mm.then_inc(pair_ps, 1)

                def group(i, h, layers, thirds):
                    g = 2 * i + h
                    t = g - NORM_LAG
                    sum_chunks(g, i, h, range(0, 2))
                    if thirds:
                        third_layers(pe, t - 1, 0)
                    sum_chunks(g, i, h, range(2, 4))
                    if layers:
                        turn_y(pe, t)
                    sum_chunks(g, i, h, range(4, 8))
                    if layers:
                        first_shared(pe, t)
                    sum_chunks(g, i, h, range(8, 10))
                    if layers:
                        first_experts(pe, t, (0, 1))
                    sum_chunks(g, i, h, range(10, 12))
                    if layers:
                        first_experts(pe, t, (2, 3))
                    sum_chunks(g, i, h, range(12, 14))
                    if thirds:
                        third_layers(pe, t - 1, 1)
                    sum_chunks(g, i, h, range(14, 16))
                    if layers:
                        second_layers(pe, t)

                with pe.Fori(0, LAG // 2) as i:
                    for h in range(2):
                        group(i, h, False, False)
                group(LAG // 2, 0, False, False)
                group(LAG // 2, 1, True, False)
                with pe.Fori(LAG // 2 + 1, GROUPS // 2) as i:
                    for h in range(2):
                        group(i, h, True, True)
                t = NT - 1
                for half in range(2):
                    third_layers(pe, t - 1, half)
                turn_y(pe, t)
                first_shared(pe, t)
                first_experts(pe, t, range(NE))
                second_layers(pe, t)
                for half in range(2):
                    third_layers(pe, t, half)

            @block.scalar
            def _(act):
                with act.Fori(0, NT) as t:
                    hidden_layers(act, t)

            @block.vector
            def _(dve):
                def select(h, p, c):
                    mm = dve.tensor_scalar(onehot[p % AHEAD][:, c, :], iota_n[:, :], recs[h][:, 2 * p + c, 1:2],
                                           recs[h][:, 2 * p + c, 2:3], ALU.is_equal, ALU.mult)
                    if c:
                        mm.then_inc(onehot_made, 1)

                def group(e, i, h, stats, layers, sums):
                    g = 2 * i + h
                    t = g - NORM_LAG
                    dve.wait_ge(recs_in[1 - h], 16 * i + 16 + 16 * h)
                    dve.tensor_copy(gidx[1 - h], recs[1 - h][:, :, 0]).then_inc(gidx_made, 1)
                    for c in range(CH):
                        p = c // 2
                        if c % 4 == 0:
                            dve.load(column_regs, binof[0:1, bass.ds(CH * g + c, 4)])
                            columns = [dve.snap(r, min_val=0, max_val=(NT - 1) * D) for r in column_regs]
                        if c == CH - 6:
                            dve.wait_ge(onehot_made, PAIRS * (g + 1))
                            dve.sem_inc(recs_used, 1)
                        if c % 2 == 0:
                            dve.wait_ge(pair_ps, PAIRS * (g + 2) + p + 1)
                        dve.wait_ge(acc_step, CH * g + c + SLOTS_PS)
                        a = acc_flat[:, bass.ds(columns[c % 4], D)]
                        dve.tensor_tensor(a, product[c % SLOTS_PS], a, ALU.add).then_inc(acc_step, 1)
                        if p < PAIRS - 3:
                            select(h, p + 3, c % 2)
                        else:
                            select(1 - h, p + 3 - PAIRS, c % 2)
                        if (layers and c == 0) or (stats and c == 2) or (sums and c == 3):
                            dve.wait_ge(acc_step, CH * g + c + 1 + SLOTS_PS)
                        if layers and c == 0:
                            tile_norm(dve, t, t, 1 - h)
                        if stats and c == 2:
                            e.issue(dve.bn_stats(lne[h][:, 0:6], acc_flat[:, bass.ds((t + 1) * D, D)]))
                        if stats and c == 3:
                            e.settle()
                            dve.sem_inc(gate, 1)
                            e.issue(dve.bn_aggr(lne[h][:, 6:8], lne[h][:, 0:6]))
                        if stats and c == 4:
                            e.settle()
                            tile_variance(dve, h)
                        if sums:
                            if c == 0:
                                ask_exp(e, dve)
                                rank_compare(e, dve)
                            if c == 1:
                                rank_ties(e, dve)
                            if c == 2:
                                rank_join(e, dve)
                            if c == 3:
                                rank_count(e, dve)
                                combine_shared(e, dve, t - 1, t - 1, h, 16 * i - 16 * (COMBINE_LAG // 2) + 16)
                            if c == 4:
                                combine_bias(e, dve, h)
                                choose(e, dve)
                            if c == 5:
                                keep_chosen(e, dve, t - 1)
                            if c == 6:
                                total_exp(e, dve, 2 * t)
                            if c == 7:
                                invert_total(e, dve)
                            if c == 8:
                                weights(e, dve, h)
                        if layers:
                            if c == 8:
                                route_logits(e, dve, t)
                            if c == 9:
                                dve.wait_ge(gate_read, t + 2)
                                largest(e, dve)
                            if c == 10:
                                ask_exp(e, dve)
                            if c == 12:
                                total_exp(e, dve, 2 * t + 1)
                            if c == 13:
                                invert_total(e, dve)
                            if c == 14:
                                gates(e, dve)
                            if c == 15:
                                e.settle()
                                largest(e, dve)
                        if sums:
                            if c in (9, 10):
                                combine_expert(e, dve, t - 1, h, c - 9)
                            if c == 11:
                                combine_done(e, dve, 0)
                            if c in (14, 15):
                                combine_expert(e, dve, t - 1, h, c - 12)
                            if c == 15:
                                combine_done(e, dve, 1)

                column_regs = [dve.alloc_register(f"column{c}") for c in range(4)]
                e = Steps(dve, e_step)
                e.then(dve.memset(e2T[EH2:EH2 + 1, :, :], 1.0))
                dve.sem_inc(l3_ps, 1)
                dve.wait_ge(bins_in, 16)
                dve.wait_ge(recs_in[0], 16)
                dve.tensor_copy(gidx[0], recs[0][:, :, 0]).then_inc(gidx_made, 1)
                for p in range(3):
                    for c in range(2):
                        select(0, p, c)
                with dve.Fori(0, LAG // 2) as i:
                    for h in range(2):
                        group(e, i, h, False, False, False)
                group(e, LAG // 2, 0, True, False, False)
                group(e, LAG // 2, 1, True, True, False)
                assert e.n == G_FRONT, e.n
                with dve.Fori(LAG // 2 + 1, GROUPS // 2) as i:
                    e = Steps(dve, e_step, G_FRONT + G_STEPS * (i - (LAG // 2 + 1)))
                    for h in range(2):
                        group(e, i, h, True, True, True)
                    assert e.n == G_STEPS, e.n
                e = Steps(dve, e_step, G_FRONT + G_STEPS * (GROUPS // 2 - LAG // 2 - 1))
                t = NT - 1
                route_second(e, dve, t - 1, (t - 1) % 2)
                combine(e, dve, t - 1, t - 1, (t - 1) % 2, 16 * (NT // 2))
                tile_norm(dve, t, t, t % 2)
                route_first(e, dve, t)
                route_second(e, dve, t, t % 2)
                combine(e, dve, t, t, t % 2, 16 * (NT // 2))
                gather_steps = G_FRONT + G_STEPS * (GROUPS // 2 - LAG // 2 - 1) + e.n
                assert gather_steps == G_TOTAL, gather_steps

        with nc.Block() as block:
            @block.sync
            def _(sp):
                with sp.If(sp.value_load(late_i[0:1, 0:1], min_val=0, max_val=1) > 0):
                    with sp.Fori(0, NT // 2) as i:
                        for h in range(2):
                            store_result(sp, 2 * i + h, h, NT + 2 * i + h + 1)
                    for h in range(2):
                        sp.wait_ge(out_stored[h], 16 * NT + 16)

            @block.gpsimd
            def _(pool):
                with pool.If(pool.value_load(late_i[0:1, 0:1], min_val=0, max_val=1) > 0):
                    with pool.Fori(0, NT // 2) as i:
                        for h in range(2):
                            tile_rstd(pool, NT + 2 * i + h, h)

            @block.tensor
            def _(pe):
                with pe.If(pe.value_load(late_i[0:1, 0:1], min_val=0, max_val=1) > 0):
                    with pe.Fori(NT, 2 * NT) as t:
                        turn_y(pe, t)
                        first_shared(pe, t)
                        first_experts(pe, t, range(NE))
                        second_layers(pe, t)
                        for half in range(2):
                            third_layers(pe, t, half)

            @block.scalar
            def _(act):
                with act.If(act.value_load(late_i[0:1, 0:1], min_val=0, max_val=1) > 0):
                    with act.Fori(NT, 2 * NT) as t:
                        hidden_layers(act, t)

            @block.vector
            def _(dve):
                with dve.If(dve.value_load(late_i[0:1, 0:1], min_val=0, max_val=1) > 0):
                    with dve.Fori(0, NT // 2) as i:
                        e = Steps(dve, e_step, G_TOTAL + R_STEPS * i)
                        for h in range(2):
                            t = 2 * i + h
                            n = NT + t
                            tile_moments(e, dve, t, h)
                            tile_norm(dve, n, t, h)
                            route_first(e, dve, n)
                            route_second(e, dve, n, h)
                            combine(e, dve, n, t, h, 16 * (NT // 2) + 16 * i + 16)
                        assert e.n == R_STEPS, e.n


_INS = ["x", "src", "dst", "edge_weight", "L0_gnn_weight", "L0_mix_Wq", "L0_mix_bq", "L0_mix_Wk", "L0_mix_bk",
        "L0_mix_Wv", "L0_mix_bv", "L0_mix_Wo", "L0_mix_bo", "L0_mix_W1", "L0_mix_b1", "L0_mix_W2", "L0_mix_b2",
        "L0_mix_ln1_g", "L0_mix_ln1_b", "L0_mix_ln2_g", "L0_mix_ln2_b", "L0_ffn_sW1", "L0_ffn_sb1", "L0_ffn_sW2",
        "L0_ffn_sb2", "L0_ffn_sW3", "L0_ffn_sb3", "L0_ffn_eW1", "L0_ffn_eb1", "L0_ffn_eW2", "L0_ffn_eb2",
        "L0_ffn_eW3", "L0_ffn_eb3", "L0_ffn_gW", "L0_ffn_gb"]
_OUTS = [((N, D), "float32")]


def kernel(**inputs):
    import numpy as _np
    import concourse.bacc as _bacc
    from concourse import mybir as _mybir
    from concourse.bass_utils import run_bass_kernel_spmd as _run

    nc = _bacc.Bacc("TRN2", target_bir_lowering=False, num_devices=1)
    arrays, args = {}, []
    for name in _INS:
        a = _np.ascontiguousarray(inputs[name])
        arrays[f"in_{name}_dram"] = a
        args.append(nc.dram_tensor(f"in_{name}_dram", a.shape, _mybir.dt.from_np(a.dtype), kind="ExternalInput").ap())
    for i, (shape, dtype) in enumerate(_OUTS):
        dt = _mybir.dt.from_np(_np.dtype(dtype))
        args.append(nc.dram_tensor(f"out_{i}_dram", shape, dt, kind="ExternalOutput").ap())
    build(nc, *args)
    r = _run(nc, [arrays], core_ids=[0])
    return r.results[0]["out_0_dram"]
```
